# Optimizing a Trainium2 kernel written in Bass

```python
import numpy as np
import jax
import jax.numpy as jnp

def _softmax(x, axis=-1):
    return jax.nn.softmax(x, axis=axis)

def _gelu(x):
    return jax.nn.gelu(x, approximate=True)

def _silu(x):
    return jax.nn.silu(x)

def _sigmoid(x):
    return jax.nn.sigmoid(x)

def _layernorm(x, axis=-1, eps=1e-05):
    m = jnp.mean(x, axis=axis, keepdims=True)
    v = jnp.var(x, axis=axis, keepdims=True)
    return (x - m) / jnp.sqrt(v + eps)

def _scatter_add(tgt, idx, src, axis=0):
    return tgt.at[idx].add(src)

def _segment_sum(src, seg, n):
    return jax.ops.segment_sum(src, seg, n)
kernel_name = 'mk_metaformer_d2_conv_nhwc128_r2_1d9582'

def setup_inputs(seed: int=0):
    np.random.seed(seed)
    _w = jnp.asarray

    def _rec_inputs():
        import jax
        import jax.numpy as jnp
        _gk = jax.random.key(seed)
        x = 7.22e-05 + 1 * jax.random.normal(jax.random.fold_in(_gk, 1), (1, 128, 128, 64), jnp.float32)
        return x
    x = _rec_inputs()

    def _L0_conv_setup():
        import jax, jax.numpy as jnp
        import numpy as np
        D = 64
        C = 32
        H = 4
        L = 128
        N = 1
        EPS = 1e-05

        def _layernorm(x, gamma, beta):
            mu = jnp.mean(x, axis=-1, keepdims=True)
            var = jnp.mean(jnp.square(x - mu), axis=-1, keepdims=True)
            return (x - mu) * jax.lax.rsqrt(var + EPS) * gamma + beta
        key = jax.random.key(seed)
        ks = jax.random.split(key, 10)
        pair_rep = jax.random.normal(ks[0], (N, L, L, D), dtype=jnp.float32)
        mask = (jax.random.uniform(ks[1], (N, L, L)) < 0.9).astype(jnp.float32)
        s = 1.0 / np.sqrt(D)
        Wq = jax.random.normal(ks[2], (D, H * C), dtype=jnp.float32) * s
        Wk = jax.random.normal(ks[3], (D, H * C), dtype=jnp.float32) * s
        Wv = jax.random.normal(ks[4], (D, H * C), dtype=jnp.float32) * s
        Wb = jax.random.normal(ks[5], (D, H), dtype=jnp.float32) * s
        Wu = jax.random.normal(ks[6], (D, H * C), dtype=jnp.float32) * s
        bu = jnp.zeros((H * C,), dtype=jnp.float32)
        Wo = jax.random.normal(ks[7], (H * C, D), dtype=jnp.float32) / np.sqrt(H * C)
        bo = jnp.zeros((D,), dtype=jnp.float32)
        gamma = jnp.ones((D,), dtype=jnp.float32)
        beta = jnp.zeros((D,), dtype=jnp.float32)
        return dict(pair_rep=pair_rep, mask=mask, gamma=gamma, beta=beta, Wq=Wq, Wk=Wk, Wv=Wv, Wb=Wb, Wu=Wu, bu=bu, Wo=Wo, bo=bo)
    _L0_conv_all = _L0_conv_setup()
    _L0_conv_in = {k: v for k, v in _L0_conv_all.items() if k in ('mask', 'gamma', 'beta', 'Wq', 'Wk', 'Wv', 'Wb', 'Wu', 'bu', 'Wo', 'bo')}
    del _L0_conv_all

    def _L0_ffn_setup():
        import jax, jax.numpy as jnp
        import numpy as np
        BN_EPS = 1e-05
        key = jax.random.key(seed)
        k1, k2, k3 = jax.random.split(key, 3)
        B, T, I, H = (32, 1024, 64, 64)
        x = jax.random.normal(k1, (B, T, I), dtype=jnp.float32)
        W = jax.random.normal(k2, (H, I), dtype=jnp.float32) * (1.0 / np.sqrt(I))
        V = jnp.linalg.qr(jax.random.normal(k3, (H, H), dtype=jnp.float32))[0]
        gamma = jnp.ones((H,), dtype=jnp.float32)
        beta = jnp.zeros((H,), dtype=jnp.float32)
        return {'x': x, 'W': W, 'V': V, 'gamma': gamma, 'beta': beta}
    _L0_ffn_all = _L0_ffn_setup()
    _L0_ffn_in = {k: v for k, v in _L0_ffn_all.items() if k in ('W', 'V', 'gamma', 'beta')}
    del _L0_ffn_all

    def _L1_conv_setup():
        import jax, jax.numpy as jnp
        from jax import lax
        import numpy as np
        D_MODEL = 64
        D_STATE = 16
        D_CONV = 4
        EXPAND = 2
        D_INNER = EXPAND * D_MODEL
        DT_RANK = (D_MODEL + 15) // 16
        B, H, W = (2, 56, 56)

        def _mamba(x, in_w, conv_w, conv_b, x_w, dt_w, dt_b, A_log, D, out_w):
            Bn, L, _ = x.shape
            xz = x @ in_w.T
            xc, z = jnp.split(xz, 2, axis=-1)
            xt = jnp.transpose(xc, (0, 2, 1))
            xt = lax.conv_general_dilated(xt, conv_w[:, None, :], window_strides=(1,), padding=[(D_CONV - 1, 0)], feature_group_count=D_INNER)
            xt = xt + conv_b[None, :, None]
            xc = jax.nn.silu(jnp.transpose(xt, (0, 2, 1)))
            dbl = xc @ x_w.T
            dt, Bm, Cm = jnp.split(dbl, [DT_RANK, DT_RANK + D_STATE], axis=-1)
            dt = jax.nn.softplus(dt @ dt_w.T + dt_b)
            A = -jnp.exp(A_log)
            dA = jnp.exp(dt[..., None] * A)
            dBx = dt[..., None] * Bm[:, :, None, :] * xc[..., None]

            def step(h, inp):
                dA_t, dBx_t, C_t = inp
                h = dA_t * h + dBx_t
                y = jnp.einsum('bds,bs->bd', h, C_t)
                return (h, y)
            h0 = jnp.zeros((Bn, D_INNER, D_STATE), x.dtype)
            _, ys = lax.scan(step, h0, (jnp.swapaxes(dA, 0, 1), jnp.swapaxes(dBx, 0, 1), jnp.swapaxes(Cm, 0, 1)))
            y = jnp.swapaxes(ys, 0, 1) + xc * D
            y = y * jax.nn.silu(z)
            return y @ out_w.T
        key = jax.random.key(seed)
        ks = jax.random.split(key, 8)
        s = 0.02
        return {'x': jax.random.normal(ks[0], (B, H, W, D_MODEL), jnp.float32), 'in_w': jax.random.normal(ks[1], (2 * D_INNER, D_MODEL), jnp.float32) * s, 'conv_w': jax.random.normal(ks[2], (D_INNER, D_CONV), jnp.float32) * s, 'conv_b': jnp.zeros((D_INNER,), jnp.float32), 'x_w': jax.random.normal(ks[3], (DT_RANK + 2 * D_STATE, D_INNER), jnp.float32) * s, 'dt_w': jax.random.normal(ks[4], (D_INNER, DT_RANK), jnp.float32) * s, 'dt_b': jax.random.normal(ks[5], (D_INNER,), jnp.float32) * 0.1, 'A_log': jnp.tile(jnp.log(jnp.arange(1, D_STATE + 1, dtype=jnp.float32)), (D_INNER, 1)), 'D': jnp.ones((D_INNER,), jnp.float32), 'out_w': jax.random.normal(ks[6], (D_MODEL, D_INNER), jnp.float32) * s}
    _L1_conv_all = _L1_conv_setup()
    _L1_conv_in = {k: v for k, v in _L1_conv_all.items() if k in ('in_w', 'conv_w', 'conv_b', 'x_w', 'dt_w', 'dt_b', 'A_log', 'D', 'out_w')}
    del _L1_conv_all

    def _L1_ffn_setup():
        import jax, jax.numpy as jnp
        import numpy as np
        B, N, D, C, E, K = (8, 4096, 64, 64, 8, 2)
        key = jax.random.key(seed)
        k0, k1, k2 = jax.random.split(key, 3)
        x = jax.random.normal(k0, (B, N, D), dtype=jnp.float32)
        router_w = jax.random.normal(k1, (D, E), dtype=jnp.float32) * 0.05
        router_b = jnp.zeros((E,), dtype=jnp.float32)
        expert_w = jax.random.normal(k2, (E, D, C), dtype=jnp.float32) * (1.0 / np.sqrt(D))
        expert_b = jnp.zeros((E, C), dtype=jnp.float32)
        return {'x': x, 'router_w': router_w, 'router_b': router_b, 'expert_w': expert_w, 'expert_b': expert_b}
    _L1_ffn_all = _L1_ffn_setup()
    _L1_ffn_in = {k: v for k, v in _L1_ffn_all.items() if k in ('router_w', 'router_b', 'expert_w', 'expert_b')}
    del _L1_ffn_all
    return {'x': x, 'L0_conv_mask': _L0_conv_in['mask'], 'L0_conv_gamma': _L0_conv_in['gamma'], 'L0_conv_beta': _L0_conv_in['beta'], 'L0_conv_Wq': _L0_conv_in['Wq'], 'L0_conv_Wk': _L0_conv_in['Wk'], 'L0_conv_Wv': _L0_conv_in['Wv'], 'L0_conv_Wb': _L0_conv_in['Wb'], 'L0_conv_Wu': _L0_conv_in['Wu'], 'L0_conv_bu': _L0_conv_in['bu'], 'L0_conv_Wo': _L0_conv_in['Wo'], 'L0_conv_bo': _L0_conv_in['bo'], 'L0_ffn_W': _L0_ffn_in['W'], 'L0_ffn_V': _L0_ffn_in['V'], 'L0_ffn_gamma': _L0_ffn_in['gamma'], 'L0_ffn_beta': _L0_ffn_in['beta'], 'L1_conv_in_w': _L1_conv_in['in_w'], 'L1_conv_conv_w': _L1_conv_in['conv_w'], 'L1_conv_conv_b': _L1_conv_in['conv_b'], 'L1_conv_x_w': _L1_conv_in['x_w'], 'L1_conv_dt_w': _L1_conv_in['dt_w'], 'L1_conv_dt_b': _L1_conv_in['dt_b'], 'L1_conv_A_log': _L1_conv_in['A_log'], 'L1_conv_D': _L1_conv_in['D'], 'L1_conv_out_w': _L1_conv_in['out_w'], 'L1_ffn_router_w': _L1_ffn_in['router_w'], 'L1_ffn_router_b': _L1_ffn_in['router_b'], 'L1_ffn_expert_w': _L1_ffn_in['expert_w'], 'L1_ffn_expert_b': _L1_ffn_in['expert_b']}

def reference(x, L0_conv_mask, L0_conv_gamma, L0_conv_beta, L0_conv_Wq, L0_conv_Wk, L0_conv_Wv, L0_conv_Wb, L0_conv_Wu, L0_conv_bu, L0_conv_Wo, L0_conv_bo, L0_ffn_W, L0_ffn_V, L0_ffn_gamma, L0_ffn_beta, L1_conv_in_w, L1_conv_conv_w, L1_conv_conv_b, L1_conv_x_w, L1_conv_dt_w, L1_conv_dt_b, L1_conv_A_log, L1_conv_D, L1_conv_out_w, L1_ffn_router_w, L1_ffn_router_b, L1_ffn_expert_w, L1_ffn_expert_b):
    import jax
    import jax.numpy as jnp

    def _L0_conv_ref(pair_rep, mask, gamma, beta, Wq, Wk, Wv, Wb, Wu, bu, Wo, bo):
        import jax, jax.numpy as jnp
        import numpy as np
        D = 64
        C = 32
        H = 4
        L = 128
        N = 1
        EPS = 1e-05

        def _layernorm(x, gamma, beta):
            mu = jnp.mean(x, axis=-1, keepdims=True)
            var = jnp.mean(jnp.square(x - mu), axis=-1, keepdims=True)
            return (x - mu) * jax.lax.rsqrt(var + EPS) * gamma + beta
        x = _layernorm(pair_rep, gamma, beta)
        n, s, _, _ = x.shape
        q = x @ Wq * C ** (-0.5)
        q = q.reshape(n, s, s, H, C)
        k = (x @ Wk).reshape(n, s, s, H, C)
        v = (x @ Wv).reshape(n, s, s, H, C)
        dpa = jnp.einsum('nsqhc,nsvhc->nsqvh', k, q)
        pair_bias = x @ Wb
        bias = 1000000000.0 * (mask - 1.0)
        dpa = dpa + bias[:, None, :, :, None]
        attention = jax.nn.softmax(dpa + pair_bias[:, None], axis=3)
        out = jnp.einsum('nsqvh,nsvhc->nsqhc', attention, v)
        fu = jax.nn.sigmoid(x @ Wu + bu).reshape(n, s, s, H, C)
        out = out * fu
        out = out.reshape(n, s, s, H * C) @ Wo + bo
        out = out * mask[..., None]
        return out

    def _L0_ffn_ref(x, W, V, gamma, beta):
        import jax, jax.numpy as jnp
        import numpy as np
        BN_EPS = 1e-05
        B, T, H = (x.shape[0], x.shape[1], W.shape[0])
        Wx = jnp.einsum('bti,hi->bth', x, W)
        flat = Wx.reshape(B * T, H)
        mean = jnp.mean(flat, axis=0)
        var = jnp.var(flat, axis=0)
        Wx = ((flat - mean) * jax.lax.rsqrt(var + BN_EPS) * gamma + beta).reshape(B, T, H)
        Vt = V.T

        def step(yt, wx_t):
            yt = jax.nn.sigmoid(wx_t + yt @ Vt)
            return (yt, yt)
        y0 = jnp.zeros((B, H), dtype=Wx.dtype)
        _, ys = jax.lax.scan(step, y0, jnp.swapaxes(Wx, 0, 1))
        return jnp.swapaxes(ys, 0, 1)

    def _L1_conv_ref(x, in_w, conv_w, conv_b, x_w, dt_w, dt_b, A_log, D, out_w):
        import jax, jax.numpy as jnp
        from jax import lax
        import numpy as np
        D_MODEL = 64
        D_STATE = 16
        D_CONV = 4
        EXPAND = 2
        D_INNER = EXPAND * D_MODEL
        DT_RANK = (D_MODEL + 15) // 16
        B, H, W = (2, 56, 56)

        def _mamba(x, in_w, conv_w, conv_b, x_w, dt_w, dt_b, A_log, D, out_w):
            Bn, L, _ = x.shape
            xz = x @ in_w.T
            xc, z = jnp.split(xz, 2, axis=-1)
            xt = jnp.transpose(xc, (0, 2, 1))
            xt = lax.conv_general_dilated(xt, conv_w[:, None, :], window_strides=(1,), padding=[(D_CONV - 1, 0)], feature_group_count=D_INNER)
            xt = xt + conv_b[None, :, None]
            xc = jax.nn.silu(jnp.transpose(xt, (0, 2, 1)))
            dbl = xc @ x_w.T
            dt, Bm, Cm = jnp.split(dbl, [DT_RANK, DT_RANK + D_STATE], axis=-1)
            dt = jax.nn.softplus(dt @ dt_w.T + dt_b)
            A = -jnp.exp(A_log)
            dA = jnp.exp(dt[..., None] * A)
            dBx = dt[..., None] * Bm[:, :, None, :] * xc[..., None]

            def step(h, inp):
                dA_t, dBx_t, C_t = inp
                h = dA_t * h + dBx_t
                y = jnp.einsum('bds,bs->bd', h, C_t)
                return (h, y)
            h0 = jnp.zeros((Bn, D_INNER, D_STATE), x.dtype)
            _, ys = lax.scan(step, h0, (jnp.swapaxes(dA, 0, 1), jnp.swapaxes(dBx, 0, 1), jnp.swapaxes(Cm, 0, 1)))
            y = jnp.swapaxes(ys, 0, 1) + xc * D
            y = y * jax.nn.silu(z)
            return y @ out_w.T
        Bn, Hn, Wn, C = x.shape
        x_flat = x.reshape(Bn, Hn * Wn, C)
        params = (in_w, conv_w, conv_b, x_w, dt_w, dt_b, A_log, D, out_w)
        y_fwd = _mamba(x_flat, *params)
        y_bwd = jnp.flip(_mamba(jnp.flip(x_flat, axis=1), *params), axis=1)
        return (y_fwd + y_bwd).reshape(Bn, Hn, Wn, C)

    def _L1_ffn_ref(x, router_w, router_b, expert_w, expert_b):
        import jax, jax.numpy as jnp
        import numpy as np
        B, N, D, C, E, K = (8, 4096, 64, 64, 8, 2)
        router_probs = jax.nn.softmax(x @ router_w + router_b, axis=-1)
        top_p, top_i = jax.lax.top_k(router_probs, K)
        top_p = top_p / jnp.sum(top_p, axis=-1, keepdims=True)
        expert_out = jnp.einsum('bnd,edc->bnec', x, expert_w) + expert_b
        gathered = jnp.take_along_axis(expert_out, top_i[..., None], axis=2)
        return jnp.einsum('bnk,bnkc->bnc', top_p, gathered)

    def _gn(v, G=32, eps=1e-05):
        B_, H_, W_, C_ = v.shape
        g = v.reshape(B_, H_, W_, G, C_ // G)
        m = jnp.mean(g, axis=(1, 2, 4), keepdims=True)
        s = jnp.var(g, axis=(1, 2, 4), keepdims=True)
        return ((g - m) / jnp.sqrt(s + eps)).reshape(v.shape)

    def _ln_c(v, eps=1e-06):
        m = jnp.mean(v, axis=-1, keepdims=True)
        s = jnp.var(v, axis=-1, keepdims=True)
        return (v - m) / jnp.sqrt(s + eps)

    def _ln_t(v, eps=1e-05):
        m = jnp.mean(v, axis=-1, keepdims=True)
        s = jnp.var(v, axis=-1, keepdims=True)
        return (v - m) / jnp.sqrt(s + eps)

    def _to_tokens(v):
        B_, H_, W_, C_ = v.shape
        return v.reshape(B_, H_ * W_, C_)

    def _from_tokens(t, like):
        return t.reshape(like.shape)
    x = x + _L0_conv_ref(_ln_c(x), L0_conv_mask, L0_conv_gamma, L0_conv_beta, L0_conv_Wq, L0_conv_Wk, L0_conv_Wv, L0_conv_Wb, L0_conv_Wu, L0_conv_bu, L0_conv_Wo, L0_conv_bo)
    t = _to_tokens(x)
    t = t + _L0_ffn_ref(_ln_t(t), L0_ffn_W, L0_ffn_V, L0_ffn_gamma, L0_ffn_beta)
    x = _from_tokens(t, x)
    x = x + _L1_conv_ref(_ln_c(x), L1_conv_in_w, L1_conv_conv_w, L1_conv_conv_b, L1_conv_x_w, L1_conv_dt_w, L1_conv_dt_b, L1_conv_A_log, L1_conv_D, L1_conv_out_w)
    t = _to_tokens(x)
    t = t + _L1_ffn_ref(_ln_t(t), L1_ffn_router_w, L1_ffn_router_b, L1_ffn_expert_w, L1_ffn_expert_b)
    x = _from_tokens(t, x)
    return x

_drawn_inputs = setup_inputs


def setup_inputs(seed=0):
    import zlib

    import numpy as np

    out = dict(_drawn_inputs(seed))
    spreads = {'L0_conv_gamma': (1.0, 0.2),
     'L0_conv_beta': (0.0, 0.1),
     'L0_conv_bu': (0.0, 0.1),
     'L0_conv_bo': (0.0, 0.1),
     'L0_ffn_gamma': (1.0, 0.2),
     'L0_ffn_beta': (0.0, 0.1),
     'L1_conv_conv_b': (0.0, 0.417),
     'L1_conv_D': (1.0, 0.6),
     'L1_ffn_router_b': (0.0, 0.1),
     'L1_ffn_expert_b': (0.0, 0.1)}
    factors = {'L1_conv_in_w': 3.464,
     'L1_conv_conv_w': 8.0,
     'L1_conv_x_w': 8.0,
     'L1_conv_dt_w': 21.626,
     'L1_conv_dt_b': 8.0,
     'L1_conv_A_log': 8.0,
     'L1_conv_out_w': 3.516}
    for name, (base, spread) in spreads.items():
        noise = np.random.default_rng([zlib.crc32(name.encode()), seed]).standard_normal(out[name].shape)
        drawn = base * np.exp(spread * noise) if base else spread * noise
        out[name] = jnp.asarray(drawn.astype(out[name].dtype))
    for name, factor in factors.items():
        out[name] = (out[name] * factor).astype(out[name].dtype)
    return out
```

```python
import numpy as np
from contextlib import ExitStack
import concourse.bass as bass
from concourse import mybir

F32 = mybir.dt.float32
BF16 = mybir.dt.bfloat16
I32 = mybir.dt.int32
ACT = mybir.ActivationFunctionType
ALU = mybir.AluOpType
AX = mybir.AxisListType

S = 128
Q = 128
D = 64
T = S * Q
GR = 4
GT = GR * Q
NG = S // GR
HEADS, HC = 4, 32
NEG = 1.0e9


def need(eng, sem, count):
    if not (isinstance(count, int) and count <= 0):
        eng.wait_ge(sem, count)


class Chain:

    def __init__(self, eng, sem):
        self.eng, self.sem, self.base, self.n = eng, sem, 0, 0

    def at(self, base):
        self.base, self.n = base, 0

    def __call__(self, ins):
        self.n += 1
        ins.then_inc(self.sem, 1)
        self.eng.wait_ge(self.sem, self.base + self.n)


def row_of(ap):
    return ap.rearrange("(a n) -> a n", a=1)


def col_of(ap):
    return ap.rearrange("(p a) -> p a", a=1)


class Core:

    def __init__(self, nc, ctx):
        self.nc, self.used = nc, []

        def sb(name, shape, dt=F32):
            return ctx.enter_context(nc.sbuf_tensor(name, shape, dt))
        self.x = sb("x_tok", [Q, S, D])
        self.mean = sb("row_mean", [Q, S])
        self.rstd = sb("row_rstd", [Q, S])
        self.ident = sb("ident", [128, 128])
        self.one = sb("one_col", [128, 1])

    def sem(self, name):
        self.used.append(self.nc.alloc_semaphore(name=name))
        return self.used[-1]

    def clear_semaphores(self):
        self.nc.clear_and_free_semaphores(self.used)
        self.nc.all_engine_barrier()
        self.used = []


def load_stage(nc, c, x_in):
    with ExitStack() as ctx:
        loaded = c.sem("ld_x")
        blank = c.sem("ld_blank")
        made = c.sem("ld_ident")
        block = ctx.enter_context(nc.Block())
        xv = x_in.rearrange("b s q d -> q (b s) d")

        @block.sync
        def _(sp):
            for k in range(4):
                sp.dma_start(c.x[:, k * 32:(k + 1) * 32, :], xv[:, k * 32:(k + 1) * 32, :]).then_inc(loaded, 16)
            sp.wait_ge(loaded, 64)

        @block.gpsimd
        def _(pool):
            nc.gpsimd.memset(c.ident[:, :], 0.0).then_inc(blank, 1)
            nc.gpsimd.memset(c.one[:, :], 1.0).then_inc(made, 1)
            pool.wait_ge(blank, 1)
            nc.gpsimd.affine_select(out=c.ident[:, :], in_=c.ident[:, :], compare_op=ALU.not_equal, fill=1.0,
                                    base=0, pattern=[[-1, 128]], channel_multiplier=1).then_inc(made, 1)
            pool.wait_ge(made, 2)


def store_stage(nc, c, out):
    with ExitStack() as ctx:
        stored = c.sem("st_x")
        block = ctx.enter_context(nc.Block())
        ov = out.rearrange("b s q d -> q (b s) d")

        @block.sync
        def _(sp):
            for k in range(4):
                sp.dma_start(ov[:, k * 32:(k + 1) * 32, :], c.x[:, k * 32:(k + 1) * 32, :]).then_inc(stored, 16)
            sp.wait_ge(stored, 64)


def stats_stage(nc, c, name, var_scale, var_add):
    with ExitStack() as ctx:
        st = ctx.enter_context(nc.sbuf_tensor(name + "_st", [Q, S, 6], F32))
        dd = ctx.enter_context(nc.sbuf_tensor(name + "_dd", [Q, S], F32))
        vv = ctx.enter_context(nc.sbuf_tensor(name + "_vv", [Q, S], F32))
        sem = lambda n: c.sem(name + n)
        rows_done, steps, var_ready, std_ready = sem("_rows"), sem("_steps"), sem("_var"), sem("_std")
        block = ctx.enter_context(nc.Block())
        UN = 16

        @block.vector
        def _(dve):
            with dve.Fori(0, S // UN) as i:
                r = i * UN
                for j in range(UN):
                    nc.vector.bn_stats(st[:, bass.ds(r + j, 1), :].rearrange("p a n -> p (a n)"),
                                       c.x[:, bass.ds(r + j, 1), :].rearrange("p a n -> p (a n)")).then_inc(rows_done, 1)
            dve.wait_ge(rows_done, S)
            me, m2e, mo, m2o = st[:, :, 1], st[:, :, 2], st[:, :, 4], st[:, :, 5]
            chain = Chain(dve, steps)
            nc.vector.tensor_tensor(vv[:, :], m2e, m2o, ALU.add).then_inc(rows_done, 1)
            nc.vector.tensor_tensor(c.mean[:, :], me, mo, ALU.add).then_inc(rows_done, 1)
            chain(nc.vector.tensor_tensor(dd[:, :], me, mo, ALU.subtract))
            chain(nc.vector.tensor_tensor(dd[:, :], dd[:, :], dd[:, :], ALU.mult))
            dve.wait_ge(rows_done, S + 2)
            chain(nc.vector.scalar_tensor_tensor(out=vv[:, :], in0=dd[:, :], scalar=D / 4.0, in1=vv[:, :],
                                                 op0=ALU.mult, op1=ALU.add))
            nc.vector.tensor_scalar(vv[:, :], vv[:, :], var_scale / D, var_add, ALU.mult, ALU.add).then_inc(var_ready, 1)
            chain(nc.vector.tensor_scalar(c.mean[:, :], c.mean[:, :], 0.5, None, ALU.mult))
            dve.wait_ge(std_ready, 1)
            chain(nc.vector.reciprocal(c.rstd[:, :], dd[:, :]))

        @block.scalar
        def _(act):
            act.wait_ge(var_ready, 1)
            nc.scalar.activation(dd[:, :], vv[:, :], ACT.Sqrt).then_inc(std_ready, 1)
            act.wait_ge(std_ready, 1)


def transpose_stage(nc, c, name, paired, evacuate, dve_extra=None):
    groups = NG // 2 if paired else NG
    with ExitStack() as ctx:
        ring = ctx.enter_context(nc.sbuf_tensor(name + "_ring", [Q, 2, GR, 2, D], F32))
        ps = ctx.enter_context(nc.psum_tensor(name + "_ps", [128, 2, GT], F32))
        sem = lambda n: c.sem(name + n)
        normed, turned, taken = sem("_normed"), sem("_turned"), sem("_taken")
        block = ctx.enter_context(nc.Block())
        per = 2 * GR if paired else GR

        @block.vector
        def _(dve):
            def group(g, k):
                need(dve, turned, g - 1)
                for j in range(GR):
                    for half in ((0, 1) if paired else (0,)):
                        row = GR * g + j + half * (S // 2)
                        src = c.x[:, bass.ds(row, 1), :]
                        if paired:
                            dst = ring[:, k, j, half:half + 1, :]
                        else:
                            dst, src = ring[:, k, j, :, :], src.to_broadcast([Q, 2, D])
                        nc.vector.tensor_scalar(dst, src, c.mean[:, bass.ds(row, 1)], c.rstd[:, bass.ds(row, 1)],
                                                ALU.subtract, ALU.mult).then_inc(normed, 1)
            group(0, 0)
            group(1, 1)
            with dve.Fori(1, groups // 2) as i:
                g = 2 * i
                group(g, 0)
                group(g + 1, 1)

        @block.tensor
        def _(pe):
            def group(g, k):
                need(pe, taken, g - 1)
                pe.wait_ge(normed, per * (g + 1))
                for j in range(GR):
                    ins = nc.tensor.transpose(ps[:, k, j * Q:(j + 1) * Q],
                                              ring[:, k, j, :, :].rearrange("p a d -> p (a d)"), c.ident[:, :])
                ins.then_inc(turned, 1)
            group(0, 0)
            group(1, 1)
            with pe.Fori(1, groups // 2) as i:
                g = 2 * i
                group(g, 0)
                group(g + 1, 1)

        @block.scalar
        def _(act):
            with act.Fori(0, groups // 2) as i:
                g = 2 * i
                for k in range(2):
                    act.wait_ge(turned, g + k + 1)
                    evacuate(g + k, ps[:, k, :]).then_inc(taken, 1)


def attention_stage(nc, c, A, pair_scratch):
    with ExitStack() as ctx:
        def sb(name, shape, dt=F32):
            return ctx.enter_context(nc.sbuf_tensor(name, shape, dt))
        xT = sb("at_xT", [D + 1, T])
        wq, wk = sb("at_wq", [D, 128]), sb("at_wk", [D, 128])
        wvu = sb("at_wvu", [D + 1, 256])
        wb = sb("at_wb", [D, 128])
        wo = sb("at_wo", [128, D])
        bo = sb("at_bo", [1, D])
        ones = sb("at_ones", [1, 128])
        gamma, beta = sb("at_gamma", [D, 1]), sb("at_beta", [D, 1])
        mask, maskT = sb("at_mask", [128, 128]), sb("at_maskT", [128, 128])
        bias = sb("at_bias", [128, HEADS, 128])

        stats_stage(nc, c, "at_s", 1.0 + 1e-5, 1e-5 * 1e-6)
        with ExitStack() as wctx:
            wsem = c.sem("at_w")
            set_ = c.sem("at_set")
            block = wctx.enter_context(nc.Block())

            @block.sync
            def _(sp):
                n = 0
                for dst, src in ((wq[:, :], A["Wq"]), (wk[:, :], A["Wk"]), (wvu[0:D, 0:128], A["Wv"]),
                                 (wvu[0:D, 128:256], A["Wu"]), (wvu[D:D + 1, 128:256], row_of(A["bu"])),
                                 (wb[:, 0:HEADS], A["Wb"]), (wo[:, :], A["Wo"]), (bo[:, :], row_of(A["bo"])),
                                 (gamma[:, :], col_of(A["gamma"])), (beta[:, :], col_of(A["beta"])),
                                 (mask[:, :], A["mask"].rearrange("n s q -> (n s) q"))):
                    sp.dma_start(dst, src).then_inc(wsem, 16)
                    n += 16
                sp.wait_ge(wsem, n)

            @block.gpsimd
            def _(pool):
                nc.gpsimd.memset(xT[D:D + 1, :], 1.0).then_inc(set_, 1)
                nc.gpsimd.memset(wvu[D:D + 1, 0:128], 0.0).then_inc(set_, 1)
                nc.gpsimd.memset(ones[:, :], 1.0).then_inc(set_, 1)
                nc.gpsimd.memset(wb[:, HEADS:128], 0.0).then_inc(set_, 1)
                pool.wait_ge(set_, 4)

        def evacuate(g, ps):
            return nc.scalar.activation(xT[0:D, bass.ds(g * GT, GT)], ps[0:D, :], ACT.Identity,
                                        bias=beta[:, :], scale=gamma[:, :])
        transpose_stage(nc, c, "at_t", False, evacuate)

        with ExitStack() as bctx:
            pb = bctx.enter_context(nc.sbuf_tensor("at_pb", [HEADS, 2, GT], F32))
            psb = bctx.enter_context(nc.psum_tensor("at_psb", [128, 2, GT], F32))
            pst = bctx.enter_context(nc.psum_tensor("at_pst", [128, 128], F32))
            sem = lambda n: c.sem("ab_" + n)
            projected, copied, loaded, masked, turned, done = (
                sem(n) for n in ("proj", "copied", "loaded", "masked", "turned", "done"))
            stored = [sem("stored0"), sem("stored1")]
            block = bctx.enter_context(nc.Block())

            @block.tensor
            def _(pe):
                nc.tensor.transpose(pst[:, :], mask[:, :], c.ident[:, :]).then_inc(turned, 1)

                def group(g, k):
                    need(pe, copied, g - 1)
                    nc.tensor.matmul(psb[:, k, :], lhsT=wb[:, :], rhs=xT[0:D, bass.ds(g * GT, GT)],
                                     start=True, stop=True).then_inc(projected, 1)
                group(0, 0)
                group(1, 1)
                with pe.Fori(1, NG // 2) as i:
                    g = 2 * i
                    group(g, 0)
                    group(g + 1, 1)

            @block.scalar
            def _(act):
                def group(g, k, stores=0):
                    act.wait_ge(projected, g + 1)
                    need(act, stored[k], 16 * stores)
                    nc.scalar.copy(pb[:, k, :], psb[0:HEADS, k, :]).then_inc(copied, 1)
                group(0, 0)
                group(1, 1)
                with act.Fori(1, NG // 2) as i:
                    group(2 * i, 0, i)
                    group(2 * i + 1, 1, i)

            @block.sync
            def _(sp):
                with sp.Fori(0, NG // 2) as i:
                    g = 2 * i
                    for k in range(2):
                        sp.wait_ge(copied, g + k + 1)
                        sp.dma_start(pair_scratch[:, bass.ds((g + k) * GT, GT)], pb[:, k, :]).then_inc(stored[k], 16)
                for k in range(2):
                    sp.wait_ge(stored[k], 16 * NG // 2)
                sp.dma_start(bias[:, :, :], pair_scratch.rearrange("h (q v) -> q h v", q=128)).then_inc(loaded, 16)
                sp.wait_ge(loaded, 16)

            @block.vector
            def _(dve):
                dve.wait_ge(turned, 1)
                nc.vector.tensor_copy(maskT[:, :], pst[:, :]).then_inc(done, 1)
                nc.vector.tensor_scalar(mask[:, :], mask[:, :], 1.0, NEG, ALU.subtract, ALU.mult).then_inc(masked, 1)
                nc.vector.tensor_scalar(wo[:, :], wo[:, :], 0.5, None, ALU.mult).then_inc(done, 1)
                dve.wait_ge(masked, 1)
                dve.wait_ge(loaded, 16)
                for h in range(HEADS):
                    nc.vector.tensor_tensor(bias[:, h, :], bias[:, h, :], mask[:, :], ALU.add).then_inc(done, 1)
                dve.wait_ge(done, 2 + HEADS)

        attention_rows(nc, c, xT, wq, wk, wvu, wo, bo, ones, maskT, bias)


def attention_rows(nc, c, xT, wq, wk, wvu, wo, bo, ones, maskT, bias):
    with ExitStack() as ctx:
        def sb(name, shape, dt=F32):
            return ctx.enter_context(nc.sbuf_tensor(name, shape, dt))
        xg = sb("ar_xg", [D + 1, 2, GT])
        kT = sb("ar_kT", [128, 2, GT])
        qd = sb("ar_qd", [128, 2, GR, HEADS, 128])
        va = sb("ar_va", [128, 2, HEADS, HC + 1])
        gate = sb("ar_gate", [128, 2, 128])
        sc = sb("ar_sc", [128, 2, HEADS, 128])
        mx = sb("ar_mx", [128, 2, HEADS])
        ex = sb("ar_ex", [128, 2, HEADS, 128])
        exT = sb("ar_exT", [128, 2, HEADS * 128])
        rs = sb("ar_rs", [128, 2, HEADS])
        og = sb("ar_og", [128, 2, 128])
        og2 = sb("ar_og2", [128, 2, 128])
        ogT = sb("ar_ogT", [128, 2, 128])
        ps_s = ctx.enter_context(nc.psum_tensor("ar_pss", [128, 2, HEADS, 128], F32))
        ps_p = ctx.enter_context(nc.psum_tensor("ar_psp", [128, GT], F32))
        ps_v = ctx.enter_context(nc.psum_tensor("ar_psv", [128, 512], F32))
        ps_t = ctx.enter_context(nc.psum_tensor("ar_pst", [128, 512], F32))
        ps_o = ctx.enter_context(nc.psum_tensor("ar_pso", [128, 512], F32))
        ps_ot = ctx.enter_context(nc.psum_tensor("ar_psot", [128, 512], F32))
        ps_y = ctx.enter_context(nc.psum_tensor("ar_psy", [128, 512], F32))
        o_v = ps_o[:, 0:HEADS * (HC + 1)].rearrange("p (h c) -> p h c", h=HEADS)
        o_t = ps_ot[:, 0:128]
        o_y = ps_y[:, 0:D]
        sem = lambda n: c.sem("ar_" + n)
        g_proj, g_taken = sem("g_proj"), sem("g_taken")
        g_loaded = [sem("g_loaded0"), sem("g_loaded1")]
        (scored, vu_made, v_taken, g_made, added, maxed, shifted, exped, e_turned, e_taken, o_made,
         summed, gated, scaled, o_turned, o_taken, y_made, x_done, ones_set) = (
            sem(n) for n in ("scored", "vu", "v", "g", "added", "maxed", "shifted", "exped", "e_turned", "e_taken",
                             "o", "summed", "gated", "scaled", "o_turned", "o_taken", "y", "x", "ones"))
        block = ctx.enter_context(nc.Block())
        SCALE = float(HC) ** -0.5

        @block.sync
        def _(sp):
            def load(g, k):
                need(sp, vu_made, GR * (g - 1))
                sp.dma_start(xg[:, k, :], xT[:, bass.ds(g * GT, GT)]).then_inc(g_loaded[k], 16)
            load(0, 0)
            load(1, 1)
            with sp.Fori(1, NG // 2) as i:
                g = 2 * i
                load(g, 0)
                load(g + 1, 1)

        @block.tensor
        def _(pe):
            def project(g, k, which, pair):
                pe.wait_ge(g_loaded[k], 16 * (pair + 1))
                need(pe, g_taken, 2 * g + which)
                nc.tensor.matmul(ps_p[:, :], lhsT=(wq, wk)[which][:, :], rhs=xg[0:D, k, :],
                                 start=True, stop=True).then_inc(g_proj, 1)

            def front(r, j, g, k):
                pe.wait_ge(g_taken, 2 * (g + 1))
                need(pe, added, r - 1)
                nc.tensor.matmul(ps_s[:, j % 2, :, :], lhsT=kT[:, k, j * 128:(j + 1) * 128],
                                 rhs=qd[:, k, j, :, :], start=True, stop=True).then_inc(scored, 1)
                need(pe, v_taken, r)
                need(pe, g_made, r)
                nc.tensor.matmul(ps_v[:, 0:256], lhsT=xg[:, k, j * 128:(j + 1) * 128], rhs=wvu[:, :],
                                 start=True, stop=True).then_inc(vu_made, 1)

            def middle(r, j):
                b = j % 2
                pe.wait_ge(exped, r + 1)
                need(pe, e_taken, r)
                for h in range(HEADS):
                    ins = nc.tensor.transpose(ps_t[:, h * 128:(h + 1) * 128], ex[:, b, h, :], c.ident[:, :])
                ins.then_inc(e_turned, 1)

            def middle2(r, j):
                b = j % 2
                pe.wait_ge(e_taken, r + 1)
                pe.wait_ge(v_taken, r + 1)
                need(pe, gated, r)
                need(pe, summed, r)
                for h in range(HEADS):
                    ins = nc.tensor.matmul(o_v[:, h, :], lhsT=exT[:, b, h * 128:(h + 1) * 128], rhs=va[:, b, h, :],
                                           start=True, stop=True)
                ins.then_inc(o_made, 1)

            def back(r, j):
                b = j % 2
                pe.wait_ge(scaled, r + 1)
                need(pe, o_taken, r)
                nc.tensor.transpose(o_t, og2[:, b, :], c.ident[:, :]).then_inc(o_turned, 1)

            def back2(r, j):
                b = j % 2
                pe.wait_ge(o_taken, r + 1)
                need(pe, x_done, r)
                nc.tensor.matmul(o_y, lhsT=ogT[:, b, :], rhs=wo[:, :], start=True, stop=False)
                nc.tensor.matmul(o_y, lhsT=ones[:, :], rhs=bo[:, :], start=False, stop=True).then_inc(y_made, 1)

            def rows(g, k, pair=None, first=False, more=True):
                for j in range(GR):
                    r = g * GR + j
                    front(r, j, g, k)
                    if more and j in (1, 2):
                        project(g + 1, 1 - k, j - 1, pair)
                    if not (first and j < 1):
                        middle(r - 1, (j - 1) % GR)
                    if not (first and j < 2):
                        back(r - 2, (j - 2) % GR)
                    if not (first and j < 1):
                        middle2(r - 1, (j - 1) % GR)
                    if not (first and j < 2):
                        back2(r - 2, (j - 2) % GR)
            pe.wait_ge(ones_set, 2)
            project(0, 0, 0, 0)
            project(0, 0, 1, 0)
            rows(0, 0, 0, first=True)
            with pe.Fori(0, (NG - 1) // 2) as i:
                g = 2 * i + 1
                rows(g, 1, i + 1)
                rows(g + 1, 0, i + 1)
            rows(NG - 1, 1, more=False)
            middle(S - 1, GR - 1)
            back(S - 2, GR - 2)
            middle2(S - 1, GR - 1)
            back2(S - 2, GR - 2)
            back(S - 1, GR - 1)
            back2(S - 1, GR - 1)

        @block.vector
        def _(dve):
            nc.vector.memset(va[:, :, :, HC:HC + 1], 1.0).then_inc(ones_set, 1)
            nc.vector.memset(qd[:, :, :, :, :], 0.0).then_inc(ones_set, 1)

            def front(r, j, g):
                b = j % 2
                dve.wait_ge(scored, r + 1)
                need(dve, exped, r - 1)
                nc.vector.tensor_tensor(sc[:, b, :, :], ps_s[:, b, :, :], bias[:, :, :], ALU.add).then_inc(added, 1)

            def front2(r, j, g):
                b = j % 2
                dve.wait_ge(added, r + 1)
                nc.vector.reduce_max(mx[:, b, :], sc[:, b, :, :], AX.X).then_inc(maxed, 1)

            def recip(r, j):
                b = j % 2
                dve.wait_ge(o_made, r + 1)
                need(dve, scaled, r - 1)
                nc.vector.reciprocal(rs[:, b, :], o_v[:, :, HC]).then_inc(summed, 1)

            def gates(r, j):
                b = j % 2
                dve.wait_ge(g_made, r + 1)
                need(dve, scaled, r - 1)
                nc.vector.scalar_tensor_tensor(
                    out=og[:, b, :].rearrange("p (h c) -> p h c", h=HEADS),
                    in0=gate[:, b, :].rearrange("p (h c) -> p h c", h=HEADS), scalar=1.0, in1=o_v[:, :, 0:HC],
                    op0=ALU.add, op1=ALU.mult).then_inc(gated, 1)

            def scales(r, j):
                b = j % 2
                dve.wait_ge(gated, r + 1)
                dve.wait_ge(summed, r + 1)
                need(dve, o_turned, r - 1)
                nc.vector.tensor_tensor(og2[:, b, :].rearrange("p (h c) -> p h c", h=HEADS),
                                        og[:, b, :].rearrange("p (h c) -> p h c", h=HEADS),
                                        rs[:, b, :].to_broadcast([128, HEADS, HC]) if 0 else
                                        rs[:, b, :].rearrange("p (h a) -> p h a", a=1).to_broadcast([128, HEADS, HC]),
                                        ALU.mult).then_inc(scaled, 1)

            def final(r, j):
                dve.wait_ge(y_made, r + 1)
                xr = c.x[:, bass.ds(r, 1), :].rearrange("p a d -> p (a d)")
                nc.vector.scalar_tensor_tensor(out=xr, in0=o_y, scalar=maskT[:, bass.ds(r, 1)], in1=xr,
                                               op0=ALU.mult, op1=ALU.add).then_inc(x_done, 1)

            def rows(g, first=False):
                for j in range(GR):
                    r = g * GR + j
                    front(r, j, g)
                    if not (first and j < 1):
                        recip(r - 1, (j - 1) % GR)
                    front2(r, j, g)
                    if not (first and j < 1):
                        gates(r - 1, (j - 1) % GR)
                    if not (first and j < 2):
                        final(r - 2, (j - 2) % GR)
                    if not (first and j < 1):
                        scales(r - 1, (j - 1) % GR)
            rows(0, True)
            with dve.Fori(1, NG) as g:
                rows(g)
            recip(S - 1, GR - 1)
            gates(S - 1, GR - 1)
            final(S - 2, GR - 2)
            scales(S - 1, GR - 1)
            final(S - 1, GR - 1)
            dve.wait_ge(x_done, S)

        @block.gpsimd
        def _(pool):
            with pool.Fori(0, S // 2) as i:
                r = 2 * i
                for b in range(2):
                    pool.wait_ge(maxed, r + b + 1)
                    nc.gpsimd.tensor_tensor(sc[:, b, :, :], sc[:, b, :, :],
                                            mx[:, b, :].rearrange("p (h a) -> p h a", a=1).to_broadcast([128, HEADS, 128]),
                                            ALU.subtract).then_inc(shifted, 1)

        @block.scalar
        def _(act):
            def take(g, k, which):
                act.wait_ge(g_proj, 2 * g + which + 1)
                need(act, scored, GR * (g - 1))
                if which == 0:
                    for h in range(HEADS):
                        p = slice(HC * h, HC * (h + 1))
                        ins = nc.scalar.activation(qd[p, k, :, h, :], ps_p[p, :].rearrange("p (j v) -> p j v", j=GR),
                                                   ACT.Copy, scale=SCALE)
                else:
                    ins = nc.scalar.copy(kT[:, k, :], ps_p[:, :])
                ins.then_inc(g_taken, 1)

            def values(r, j):
                b = j % 2
                act.wait_ge(vu_made, r + 1)
                need(act, o_made, r - 1)
                nc.scalar.copy(va[:, b, :, 0:HC], ps_v[:, 0:128].rearrange("p (h c) -> p h c", h=HEADS)).then_inc(v_taken, 1)
                need(act, gated, r - 1)
                nc.scalar.activation(gate[:, b, :], ps_v[:, 128:256], ACT.Tanh, scale=0.5).then_inc(g_made, 1)

            def e_take(r, j):
                b = j % 2
                act.wait_ge(e_turned, r + 1)
                need(act, o_made, r - 1)
                nc.scalar.copy(exT[:, b, :], ps_t[:, :]).then_inc(e_taken, 1)

            def o_take(r, j):
                b = j % 2
                act.wait_ge(o_turned, r + 1)
                need(act, y_made, r - 1)
                nc.scalar.copy(ogT[:, b, :], o_t).then_inc(o_taken, 1)

            def exps(r, j):
                b = j % 2
                act.wait_ge(shifted, r + 1)
                need(act, e_turned, r - 1)
                nc.scalar.activation(ex[:, b, :, :], sc[:, b, :, :], ACT.Exp).then_inc(exped, 1)

            def rows(g, k, first=False, more=True):
                for j in range(GR):
                    r = g * GR + j
                    values(r, j)
                    if more and j in (1, 2):
                        take(g + 1, 1 - k, j - 1)
                    if not (first and j < 1):
                        e_take(r - 1, (j - 1) % GR)
                    if not (first and j < 2):
                        o_take(r - 2, (j - 2) % GR)
                    exps(r, j)
            act.wait_ge(ones_set, 2)
            take(0, 0, 0)
            take(0, 0, 1)
            rows(0, 0, first=True)
            with act.Fori(0, (NG - 1) // 2) as i:
                g = 2 * i + 1
                rows(g, 1)
                rows(g + 1, 0)
            rows(NG - 1, 1, more=False)
            e_take(S - 1, GR - 1)
            o_take(S - 2, GR - 2)
            o_take(S - 1, GR - 1)


def recurrence_stage(nc, c, W, V, gamma, beta):
    CH, L, HEAD = 256, 64, 16
    HALF = CH // 2
    TOL = 2.0 ** -21
    assert CH * L == T
    with ExitStack() as ctx:
        def sb(name, shape, dt=F32):
            return ctx.enter_context(nc.sbuf_tensor(name, shape, dt))
        n = sb("rn_n", [128, L, HALF])
        y = sb("rn_y", [128, L, HALF])
        stats_stage(nc, c, "rn_s", 1.0, 1e-5)

        def evacuate(g, ps):
            cs = Q // L * GR
            return nc.scalar.copy(n[:, :, bass.ds(g * cs, cs)].rearrange("p j c -> p c j"),
                                  ps.rearrange("p (c j) -> p c j", j=L))
        transpose_stage(nc, c, "rn_t", True, evacuate)

        wd = sb("rn_wd", [128, 128])
        wT = sb("rn_wT", [128, 128])
        vd, vT = sb("rn_vd", [128, 128]), sb("rn_vT", [128, 128])
        join = sb("rn_join", [128, 128])
        shift = sb("rn_shift", [128, 128])
        gm, bt = sb("rn_gamma", [128, 1]), sb("rn_beta", [128, 1])
        a, cc = sb("rn_a", [128, 1]), sb("rn_c", [128, 1])
        y0 = sb("rn_y0", [128, HALF])
        yh = sb("rn_yh", [128, HEAD, HALF])
        flag = sb("rn_flag", [1, 1], I32)

        with ExitStack() as bctx:
            st = bctx.enter_context(nc.sbuf_tensor("rn_st", [128, 16, 6], F32))
            mv = bctx.enter_context(nc.sbuf_tensor("rn_mv", [128, 2], F32))
            mc = bctx.enter_context(nc.sbuf_tensor("rn_mc", [128, 4], F32))
            ps = bctx.enter_context(nc.psum_tensor("rn_psw", [128, 2, 512], F32))
            pj = bctx.enter_context(nc.psum_tensor("rn_psj", [128, 512], F32))
            pt = bctx.enter_context(nc.psum_tensor("rn_pst", [128, 512], F32))
            sem = lambda s: c.sem("rb_" + s)
            cleared, loaded, turned, copied, made, read, joined, steps, var_ready, std_ready = (
                sem(s) for s in ("cleared", "loaded", "turned", "copied", "made", "read", "joined", "steps",
                                 "var", "std"))
            block = bctx.enter_context(nc.Block())

            @block.gpsimd
            def _(pool):
                for m in (wd, vd, join, shift):
                    nc.gpsimd.memset(m[:, :], 0.0).then_inc(cleared, 1)
                pool.wait_ge(cleared, 4)
                for k, base in enumerate((0, -D, D)):
                    nc.gpsimd.affine_select(out=join[:, :], in_=join[:, :], compare_op=ALU.not_equal, fill=0.5,
                                            base=base, pattern=[[-1, 128]], channel_multiplier=1).then_inc(cleared, 1)
                    pool.wait_ge(cleared, 5 + k)
                nc.gpsimd.affine_select(out=shift[:, :], in_=shift[:, :], compare_op=ALU.not_equal, fill=1.0,
                                        base=D, pattern=[[-1, 128]], channel_multiplier=1).then_inc(cleared, 1)
                pool.wait_ge(cleared, 8)

            @block.sync
            def _(sp):
                sp.wait_ge(cleared, 4)
                k = 0
                for half in (slice(0, D), slice(D, 2 * D)):
                    for dst, src in ((wd[half, half], W), (vd[half, half], V), (gm[half, :], col_of(gamma)),
                                     (bt[half, :], col_of(beta))):
                        sp.dma_start(dst, src).then_inc(loaded, 16)
                        k += 16
                sp.wait_ge(loaded, k)

            @block.tensor
            def _(pe):
                pe.wait_ge(loaded, 128)
                nc.tensor.transpose(pt[:, 0:128], wd[:, :], c.ident[:, :])
                nc.tensor.transpose(pt[:, 128:256], vd[:, :], c.ident[:, :]).then_inc(turned, 1)
                pe.wait_ge(copied, 2)
                nf = n[:, :, :].rearrange("p j c -> p (j c)")
                for k in range(16):
                    need(pe, read, k - 1)
                    nc.tensor.matmul(ps[:, k % 2, :], lhsT=wT[:, :], rhs=nf[:, k * 512:(k + 1) * 512],
                                     start=True, stop=True).then_inc(made, 1)
                pe.wait_ge(steps, 1)
                pe.wait_ge(cleared, 8)
                nc.tensor.matmul(pj[:, 0:1], lhsT=join[:, :], rhs=mv[:, 0:1], start=True, stop=True).then_inc(joined, 1)
                pe.wait_ge(steps, 5)
                nc.tensor.matmul(pj[:, 1:2], lhsT=join[:, :], rhs=mc[:, 2:3], start=True, stop=True).then_inc(joined, 1)
                pe.wait_ge(steps, 7)
                nc.tensor.transpose(pt[:, 0:128], wd[:, :], c.ident[:, :]).then_inc(turned, 1)

            @block.vector
            def _(dve):
                chain = Chain(dve, steps)
                dve.wait_ge(turned, 1)
                nc.vector.tensor_copy(wT[:, :], pt[:, 0:128]).then_inc(copied, 1)
                nc.vector.tensor_copy(vT[:, :], pt[:, 128:256]).then_inc(copied, 1)
                for k in range(16):
                    dve.wait_ge(made, k + 1)
                    nc.vector.bn_stats(st[:, k, :], ps[:, k % 2, :]).then_inc(read, 1)
                dve.wait_ge(read, 16)
                chain(nc.vector.bn_aggr(mv[:, :], st[:, :, :].rearrange("p k s -> p (k s)")))
                dve.wait_ge(joined, 1)
                chain(nc.vector.tensor_copy(mc[:, 0:1], pj[:, 0:1]))
                chain(nc.vector.tensor_tensor(mc[:, 1:2], mv[:, 0:1], mc[:, 0:1], ALU.subtract))
                chain(nc.vector.tensor_tensor(mc[:, 1:2], mc[:, 1:2], mc[:, 1:2], ALU.mult))
                chain(nc.vector.tensor_tensor(mc[:, 2:3], mc[:, 1:2], mv[:, 1:2], ALU.add))
                dve.wait_ge(joined, 2)
                nc.vector.tensor_scalar(mc[:, 3:4], pj[:, 1:2], 1e-5, None, ALU.add).then_inc(var_ready, 1)
                dve.wait_ge(std_ready, 1)
                chain(nc.vector.reciprocal(a[:, :], mc[:, 2:3]))
                dve.wait_ge(loaded, 128)
                chain(nc.vector.tensor_scalar(wd[:, :], wd[:, :], a[:, :], gm[:, :], ALU.mult, ALU.mult))
                chain(nc.vector.tensor_scalar(cc[:, :], mc[:, 0:1], a[:, :], gm[:, :], ALU.mult, ALU.mult))
                chain(nc.vector.tensor_tensor(cc[:, :], bt[:, :], cc[:, :], ALU.subtract))
                dve.wait_ge(turned, 2)
                chain(nc.vector.tensor_copy(wT[:, :], pt[:, 0:128]))

            @block.scalar
            def _(act):
                act.wait_ge(var_ready, 1)
                nc.scalar.activation(mc[:, 2:3], mc[:, 3:4], ACT.Sqrt).then_inc(std_ready, 1)
                act.wait_ge(std_ready, 1)

        with ExitStack() as sctx:
            pu = sctx.enter_context(nc.psum_tensor("rn_psu", [128, 4, 512], F32))
            pe_end = sctx.enter_context(nc.psum_tensor("rn_pse", [128, 512], F32))
            pf = sctx.enter_context(nc.psum_tensor("rn_psf", [128, 512], F32))
            diff = sctx.enter_context(nc.sbuf_tensor("rn_diff", [128, HALF], F32))
            worst = sctx.enter_context(nc.sbuf_tensor("rn_worst", [128, 1], F32))
            worst1 = sctx.enter_context(nc.sbuf_tensor("rn_worst1", [1, 1], F32))
            sem = lambda s: c.sem("rs_" + s)
            summed, stepped, shifted, started, compared, worst_turned, flagged = (
                sem(s) for s in ("summed", "stepped", "shifted", "started", "compared", "turned", "flagged"))
            more_summed, more_stepped, more_shifted, more_started = (
                sem(s) for s in ("more_summed", "more_stepped", "more_shifted", "more_started"))
            block = sctx.enter_context(nc.Block())
            UN = 4

            def drive(pe, slot, j, first=False):
                return nc.tensor.matmul(pu[:, slot, 0:HALF], lhsT=wT[:, :], rhs=at(n, j), start=True, stop=first)

            def at(tile, j):
                return tile[:, j, :] if isinstance(j, int) else tile[:, bass.ds(j, 1), :].rearrange("p a c -> p (a c)")

            @block.tensor
            def _(pe):
                def step(t, slot, before, summed, stepped):
                    if t is not None:
                        pe.wait_ge(stepped, t)
                    nc.tensor.matmul(pu[:, slot, 0:HALF], lhsT=vT[:, :], rhs=before, start=False,
                                     stop=True).then_inc(summed, 1)

                drive(pe, 0, 0, first=True).then_inc(summed, 1)
                drive(pe, 1, 1)
                step(1, 1, at(y, 0), summed, stepped)
                for j in (2, 3):
                    drive(pe, j, j)
                    step(j, j, at(y, j - 1), summed, stepped)
                with pe.Fori(1, L // UN) as i:
                    for k in range(UN):
                        j = i * UN + k
                        drive(pe, k, j)
                        step(j, k, at(y, j - 1), summed, stepped)
                pe.wait_ge(stepped, L)
                nc.tensor.matmul(pe_end[:, 0:1], lhsT=shift[:, :], rhs=y[:, L - 1, HALF - 1:HALF],
                                 start=True, stop=True).then_inc(shifted, 1)
                for j in range(HEAD):
                    drive(pe, j % UN, j)
                    if j == 0:
                        pe.wait_ge(started, 2)
                    step(L + j, j % UN, at(yh, j - 1) if j else y0[:, :], summed, stepped)
                pe.wait_ge(compared, 2)
                nc.tensor.transpose(pf[0:1, 0:128], worst[:, :], c.ident[:, :]).then_inc(worst_turned, 1)
                pe.wait_ge(flagged, 1)
                unmet = nc.tensor.value_load(flag[0:1, 0:1], min_val=0, max_val=1)
                with pe.If(unmet > 0):
                    with pe.Fori(0, CH) as sweep:
                        nc.tensor.matmul(pe_end[:, 0:1], lhsT=shift[:, :], rhs=y[:, L - 1, HALF - 1:HALF],
                                         start=True, stop=True).then_inc(more_shifted, 1)
                        drive(pe, 0, 0)
                        pe.wait_ge(more_started, 2 * sweep + 2)
                        step(None, 0, y0[:, :], more_summed, more_stepped)
                        for j in range(1, UN):
                            drive(pe, j, j)
                            step(sweep * L + j, j, at(y, j - 1), more_summed, more_stepped)
                        with pe.Fori(1, L // UN) as i:
                            for k in range(UN):
                                j = i * UN + k
                                drive(pe, k, j)
                                step(sweep * L + j, k, at(y, j - 1), more_summed, more_stepped)
                        pe.wait_ge(more_stepped, sweep * L + L)

            @block.scalar
            def _(act):
                def step(t, slot, out, summed, stepped):
                    act.wait_ge(summed, t + 1)
                    nc.scalar.activation(out, pu[:, slot, 0:HALF], ACT.Sigmoid, bias=cc[:, :]).then_inc(stepped, 1)
                with act.Fori(0, L // UN) as i:
                    for k in range(UN):
                        step(i * UN + k, k, at(y, i * UN + k), summed, stepped)
                for j in range(HEAD):
                    step(L + j, j % UN, at(yh, j), summed, stepped)
                act.wait_ge(flagged, 1)
                unmet = nc.scalar.value_load(flag[0:1, 0:1], min_val=0, max_val=1)
                with act.If(unmet > 0):
                    with act.Fori(0, CH) as sweep:
                        act.wait_ge(more_started, 2 * sweep + 2)
                        with act.Fori(0, L // UN) as i:
                            for k in range(UN):
                                step(sweep * L + i * UN + k, k, at(y, i * UN + k), more_summed, more_stepped)

            @block.vector
            def _(dve):
                def starts(shifted, count, started):
                    dve.wait_ge(shifted, count)
                    nc.vector.tensor_copy(y0[:, 1:HALF], y[:, L - 1, 0:HALF - 1]).then_inc(started, 1)
                    nc.vector.tensor_copy(y0[:, 0:1], pe_end[:, 0:1]).then_inc(started, 1)
                starts(shifted, 1, started)
                dve.wait_ge(stepped, L + HEAD)
                nc.vector.tensor_tensor(diff[:, :], yh[:, HEAD - 1, :], y[:, HEAD - 1, :],
                                        ALU.subtract).then_inc(compared, 1)
                dve.wait_ge(compared, 1)
                nc.vector.tensor_reduce(out=worst[:, :], in_=diff[:, :], axis=AX.X, op=ALU.max,
                                        apply_absolute_value=True).then_inc(compared, 1)
                nc.vector.tensor_copy(y[:, 0:HEAD, :], yh[:, :, :]).then_inc(compared, 1)
                dve.wait_ge(worst_turned, 1)
                nc.vector.reduce_max(worst1[:, :], pf[0:1, 0:128], AX.X).then_inc(compared, 1)
                dve.wait_ge(compared, 4)
                nc.vector.tensor_scalar(flag[:, :], worst1[:, :], TOL, None, ALU.is_gt).then_inc(flagged, 1)
                dve.wait_ge(flagged, 1)
                unmet = nc.vector.value_load(flag[0:1, 0:1], min_val=0, max_val=1)
                with dve.If(unmet > 0):
                    with dve.Fori(0, CH) as sweep:
                        starts(more_shifted, sweep + 1, more_started)

        with ExitStack() as octx:
            ring = octx.enter_context(nc.sbuf_tensor("rn_ring", [128, 2, GR, Q], F32))
            ps = octx.enter_context(nc.psum_tensor("rn_pso", [128, 2, GR, 2, D], F32))
            sem = lambda s: c.sem("ro_" + s)
            copied, turned, added = sem("copied"), sem("turned"), sem("added")
            block = octx.enter_context(nc.Block())
            groups = NG // 2
            cs = Q // L * GR

            @block.scalar
            def _(act):
                def group(g, k):
                    need(act, turned, g - 1)
                    nc.scalar.copy(ring[:, k, :, :].rearrange("p b (c j) -> p (b c) j", j=L),
                                   y[:, :, bass.ds(g * cs, cs)].rearrange("p j c -> p c j")).then_inc(copied, 1)
                group(0, 0)
                group(1, 1)
                with act.Fori(1, groups // 2) as i:
                    group(2 * i, 0)
                    group(2 * i + 1, 1)

            @block.tensor
            def _(pe):
                def group(g, k):
                    pe.wait_ge(copied, g + 1)
                    need(pe, added, 2 * (g - 1))
                    for j in range(GR):
                        ins = nc.tensor.transpose(ps[:, k, j, :, :].rearrange("p a d -> p (a d)"),
                                                  ring[:, k, j, :], c.ident[:, :])
                    ins.then_inc(turned, 1)
                group(0, 0)
                group(1, 1)
                with pe.Fori(1, groups // 2) as i:
                    group(2 * i, 0)
                    group(2 * i + 1, 1)

            @block.vector
            def _(dve):
                with dve.Fori(0, groups // 2) as i:
                    for k in range(2):
                        g = 2 * i + k
                        dve.wait_ge(turned, g + 1)
                        for half in range(2):
                            rows = c.x[:, bass.ds(g * GR + half * (S // 2), GR), :]
                            nc.vector.tensor_tensor(rows, rows, ps[:, k, :, half, :], ALU.add).then_inc(added, 1)
                dve.wait_ge(added, 2 * groups)


INNER, STATES, RANK, TAPS = 128, 16, 4, 4
TC = 1024
NC = T // TC
PAD = 4
BCW = 2 * STATES


def state_space_stage(nc, c, W, y_scratch):
    with ExitStack() as ctx:
        def sb(name, shape, dt=F32):
            return ctx.enter_context(nc.sbuf_tensor(name, shape, dt))
        ns = sb("ss_n", [128, T + 2 * PAD])
        k = dict(
            taps=sb("ss_taps", [128, 2, 2, INNER]),
            z=sb("ss_wz", [D, INNER]), bc=sb("ss_wbc", [INNER, 4 * BCW]), dt=sb("ss_wdt", [INNER, INNER]),
            out=sb("ss_wout", [INNER, D]), cb=sb("ss_cb", [INNER, 1]), db=sb("ss_db", [INNER, 1]),
            dd=sb("ss_D", [INNER, 1]), A=sb("ss_A", [INNER, STATES]),
            sel=sb("ss_sel", [128, BCW, 128], BF16))
        stats_stage(nc, c, "ss_s", 1.0, 1e-6)

        with ExitStack() as wctx:
            def wsb(name, shape, dt=F32):
                return wctx.enter_context(nc.sbuf_tensor(name, shape, dt))
            inx, inz = wsb("sw_inx", [INNER, D]), wsb("sw_inz", [INNER, D])
            cw, xw, dtw = wsb("sw_cw", [INNER, TAPS]), wsb("sw_xw", [RANK + BCW, INNER]), wsb("sw_dtw", [RANK, INNER])
            al, ow = wsb("sw_al", [INNER, STATES]), wsb("sw_ow", [D, INNER])
            tp = wsb("sw_tp", [INNER, 2, 2, 2, D])
            ps = wctx.enter_context(nc.psum_tensor("sw_ps", [128, 4, 512], F32))
            sem = lambda s: c.sem("sw_" + s)
            loaded, cleared, scaled, turned, copied, exped = (sem(s) for s in ("loaded", "cleared", "scaled",
                                                                              "turned", "copied", "exped"))
            block = wctx.enter_context(nc.Block())

            @block.sync
            def _(sp):
                n = 0
                with nc.allow_non_contiguous_dma(reason="512 weights"):
                    for dst, src in ((inx[:, :], W["in_w"][0:INNER, :]), (inz[:, :], W["in_w"][INNER:2 * INNER, :]),
                                     (cw[:, :], W["conv_w"]), (k["cb"][:, :], col_of(W["conv_b"])),
                                     (xw[:, :], W["x_w"]), (dtw[:, :], W["dt_w"].rearrange("d r -> r d")),
                                     (k["db"][:, :], col_of(W["dt_b"])), (al[:, :], W["A_log"]),
                                     (k["dd"][:, :], col_of(W["D"])), (ow[:, :], W["out_w"])):
                        sp.dma_start(dst, src).then_inc(loaded, 16)
                        n += 16
                assert n == 160
                sp.wait_ge(loaded, n)

            @block.gpsimd
            def _(pool):
                nc.gpsimd.memset(k["sel"][:, :, :], 0.0).then_inc(cleared, 1)
                nc.gpsimd.memset(ns[:, 0:PAD + 1], 0.0).then_inc(cleared, 1)
                nc.gpsimd.memset(ns[:, T + PAD:T + 2 * PAD], 0.0).then_inc(cleared, 1)
                pool.wait_ge(cleared, 3)
                for part, at in enumerate((0, 64, 96)):
                    nc.gpsimd.affine_select(out=k["sel"][:, :, :], in_=k["sel"][:, :, :], compare_op=ALU.not_equal,
                                            fill=1.0, base=-at, pattern=[[-1, BCW], [0, 128]],
                                            channel_multiplier=1).then_inc(cleared, 1)
                    pool.wait_ge(cleared, 4 + part)

            @block.scalar
            def _(act):
                act.wait_ge(loaded, 160)
                nc.scalar.activation(al[:, :], al[:, :], ACT.Exp).then_inc(exped, 1)

            @block.vector
            def _(dve):
                dve.wait_ge(loaded, 160)
                order = (((3, 2), (1, 0)), ((2, 3), (0, 1)))
                for way in range(2):
                    for pair in range(2):
                        for half in range(2):
                            tap = order[way][pair][half]
                            nc.vector.tensor_scalar(tp[:, way, pair, half, :], inx[:, :], cw[:, tap:tap + 1], None,
                                                    ALU.mult).then_inc(scaled, 1)
                dve.wait_ge(exped, 1)
                nc.vector.tensor_scalar(k["A"][:, :], al[:, :], -1.0, None, ALU.mult).then_inc(copied, 1)
                dve.wait_ge(turned, 1)
                for way in range(2):
                    for pair in range(2):
                        nc.vector.tensor_copy(k["taps"][:, way, pair, :],
                                              ps[:, 0, (2 * way + pair) * 128:(2 * way + pair + 1) * 128]).then_inc(copied, 1)
                nc.vector.tensor_copy(k["z"][:, :], ps[0:D, 1, 0:128]).then_inc(copied, 1)
                nc.vector.tensor_copy(k["out"][:, :], ps[:, 1, 128:128 + D]).then_inc(copied, 1)
                for part in range(4):
                    nc.vector.tensor_copy(k["bc"][:, part * BCW:(part + 1) * BCW],
                                          ps[:, 1, 256 + RANK:256 + RANK + BCW]).then_inc(copied, 1)
                nc.vector.tensor_copy(k["dt"][:, :], ps[:, 2, 0:128]).then_inc(copied, 1)
                dve.wait_ge(copied, 12)

            @block.tensor
            def _(pe):
                pe.wait_ge(scaled, 8)
                for way in range(2):
                    for pair in range(2):
                        nc.tensor.transpose(ps[:, 0, (2 * way + pair) * 128:(2 * way + pair + 1) * 128],
                                            tp[:, way, pair, :, :].rearrange("p a d -> p (a d)"), c.ident[:, :])
                nc.tensor.transpose(ps[0:D, 1, 0:128], inz[:, :], c.ident[:, :])
                nc.tensor.transpose(ps[:, 1, 128:128 + D], ow[:, :], c.ident[0:D, 0:D])
                nc.tensor.transpose(ps[:, 1, 256:256 + RANK + BCW], xw[:, :], c.ident[0:RANK + BCW, 0:RANK + BCW])
                nc.tensor.matmul(ps[:, 2, 0:128], lhsT=xw[0:RANK, :], rhs=dtw[:, :], start=True,
                                 stop=True).then_inc(turned, 1)

        def evacuate(g, ps):
            nc.scalar.copy(ns[0:D, bass.ds(g * GT + PAD, GT)], ps[0:D, :])
            return nc.scalar.copy(ns[D:2 * D, bass.ds(g * GT + PAD + 1, GT)], ps[D:2 * D, :])
        transpose_stage(nc, c, "ss_t", False, evacuate)

        for way in range(2):
            scan_direction(nc, c, ns, k, way, y_scratch)


def scan_direction(nc, c, ns, k, way, y_scratch):
    back = way == 1
    N = "sb_" if back else "sf_"
    U = STATES
    with ExitStack() as ctx:
        def sb(name, shape, dt=F32):
            return ctx.enter_context(nc.sbuf_tensor(N + name, shape, dt))

        def sem(name):
            return c.sem(N + name)
        xc, dt, dtx = sb("xc", [128, 2, TC]), sb("dt", [128, 2, TC]), sb("dtx", [128, 2, TC])
        bcs = sb("bcs", [128, 2, TC], BF16)
        dA, bb, dbx = sb("dA", [128, 2, TC]), sb("bb", [128, 2, TC]), sb("dbx", [128, 2, TC])
        h, hc = sb("h", [128, 2, TC]), sb("hc", [128, 2, TC])
        ta, tb, tc, rest = (sb(s, [128, TC]) for s in ("ta", "tb", "tc", "rest"))
        state = sb("state", [128, STATES])
        yo = sb("yo", [128, TC])
        if back:
            zs, yf = sb("zs", [128, TC]), sb("yf", [128, TC])
        bank = lambda name: ctx.enter_context(nc.psum_tensor(N + name, [128, TC], F32))
        p_b, p_c, p_y, p_p = bank("pb"), bank("pc"), bank("py"), bank("pp")
        b_made, b_taken, c_made, exped, injected, scanned, kept, read, summed = (
            sem(s) for s in ("b_made", "b_taken", "c_made", "exped", "injected", "scanned", "kept", "read", "summed"))
        (conv, conv_taken, z_made, z_copied, z_taken, dt_made, relu_made, dt_taken, e_made, log_made, w_made, corr,
         corr2, dt_done, dtx_done, bc_made, bc_hi, bc_rest, bc_mid, bc_low, y_taken, y_joined, y_gated, projected,
         x_done, y_stored, y_loaded, zeroed) = (
            sem(s) for s in ("conv", "conv_t", "z", "z_c", "z_t", "dt", "relu", "dt_t", "e", "log", "w", "corr", "corr2",
                             "dt_d", "dtx", "bc", "bc_hi", "bc_rest", "bc_mid", "bc_low", "y_t", "y_j", "y_g",
                             "proj", "x_d", "y_st", "y_ld", "zero"))
        block = ctx.enter_context(nc.Block())
        halves = [slice(0, 512), slice(512, 1024)]

        def base(n):
            return n * -TC + (NC - 1) * TC if back else n * TC

        def run(eng, unit, prepare=(), tail=(), own=()):
            def chunk(n, par, first=False, last=False):
                for s in range(U):
                    unit(n, par, s, first, last)
                    for at, step in prepare:
                        if at == s and not last:
                            step(n + 1, 1 - par)
                    for at, step in tail:
                        if at == s and not first:
                            step(n - 1, 1 - par, last)
                    for at, step in own:
                        if at == s:
                            step(n, last)
            for _, step in prepare:
                step(0, 0)
            chunk(0, 0, first=True)
            chunk(1, 1)
            with eng.Fori(1, NC // 2 - 1) as i:
                chunk(2 * i, 0)
                chunk(2 * i + 1, 1)
            chunk(NC - 2, 0)
            chunk(NC - 1, 1, last=True)

        @block.tensor
        def _(pe):
            def gate_in(m, last):
                need(pe, x_done, m)
                pe.wait_ge(bc_rest, NC if last else m + 2)
                for hf in halves:
                    ins = nc.tensor.matmul(p_p[:, hf], lhsT=k["z"][:, :],
                                           rhs=ns[0:D, bass.ds(base(m) + PAD + hf.start, 512)], start=True, stop=True)
                ins.then_inc(z_made, 1)

            def convolve(m, par):
                need(pe, bc_rest, m)
                if back:
                    need(pe, z_copied, m - 1)
                for hf in halves:
                    for pair, off in enumerate((1, 3) if back else (0, -2)):
                        ins = nc.tensor.matmul(p_p[:, hf], lhsT=k["taps"][:, way, pair, :],
                                               rhs=ns[:, bass.ds(base(m) + PAD + off + hf.start, 512)],
                                               start=(pair == 0), stop=(pair == 1))
                ins.then_inc(conv, 1)

            def step_size(m, par):
                pe.wait_ge(conv_taken, m + 1)
                for hf in halves:
                    ins = nc.tensor.matmul(p_p[:, hf], lhsT=k["dt"][:, :], rhs=xc[:, par, hf], start=True, stop=True)
                ins.then_inc(dt_made, 1)

            def in_out(m, par):
                pe.wait_ge(dt_taken, m + 1)
                for hf in halves:
                    ins = nc.tensor.matmul(p_p[:, hf], lhsT=k["bc"][:, :], rhs=xc[:, par, hf], start=True, stop=True)
                ins.then_inc(bc_made, 1)

            def spread(dst, row, par):
                for hf in halves:
                    ins = nc.tensor.matmul(dst[:, hf], lhsT=k["sel"][:, row, :], rhs=bcs[:, par, hf],
                                           start=True, stop=True)
                return ins

            def spread_b(u, s, n, par):
                if s == 0:
                    pe.wait_ge(bc_low, n + 1)
                need(pe, b_taken, u)
                spread(p_b, s, par).then_inc(b_made, 1)

            def total(u, s, n, b):
                pe.wait_ge(read, u + 1)
                if s == 0:
                    need(pe, y_taken, n)
                for hf in halves:
                    ins = nc.tensor.matmul(p_y[:, hf], lhsT=c.ident[:, :], rhs=hc[:, b, hf],
                                           start=(s == 0), stop=(s == U - 1))
                ins.then_inc(summed, 1)

            def project(m, par, last):
                pe.wait_ge(y_gated, m + 1)
                pe.wait_ge(bc_rest, NC if last else m + 3)
                need(pe, x_done, m)
                for j in range(TC // Q):
                    ins = nc.tensor.matmul(p_p[:, j * D:(j + 1) * D], lhsT=yo[:, j * Q:(j + 1) * Q],
                                           rhs=k["out"][:, :], start=True, stop=True)
                ins.then_inc(projected, 1)

            def unit(n, par, s, first, last):
                u = n * U + s
                if first and s == 0:
                    spread_b(u, s, n, par)
                    spread_b(u + 1, s + 1, n, par)
                if s < U - 2:
                    spread_b(u + 2, s + 2, n, par)
                elif not last:
                    spread_b(u + 2, s + 2 - U, n + 1, 1 - par)
                need(pe, read, u)
                spread(p_c, STATES + s, par).then_inc(c_made, 1)
                if not (first and s == 0):
                    total(u - 1, (s - 1) % U, n if s else n - 1, (s - 1) % 2)

            if back:
                run(pe, unit, [(0, convolve), (3, step_size), (6, in_out)], [(10, project)], [(12, gate_in)])
            else:
                run(pe, unit, [(0, convolve), (3, step_size), (6, in_out)])
            total(NC * U - 1, U - 1, NC - 1, (U - 1) % 2)
            if back:
                project(NC - 1, 1, True)

        @block.scalar
        def _(act):
            def take_z(m, last):
                act.wait_ge(z_made, m + 1)
                need(act, y_gated, m)
                nc.scalar.copy(zs[:, :], p_p[:, :]).then_inc(z_copied, 1)

            def silu_x(m, par):
                act.wait_ge(conv, m + 1)
                need(act, y_taken, m - 1)
                need(act, dtx_done, m - 1)
                nc.scalar.activation(xc[:, par, :], p_p[:, :], ACT.Silu, bias=k["cb"][:, :]).then_inc(conv_taken, 1)

            def silu_z(m, par, last):
                act.wait_ge(z_copied, m + 1)
                nc.scalar.activation(zs[:, :], zs[:, :], ACT.Silu).then_inc(z_taken, 1)

            def exp_log_tables(*_):
                nc.scalar.preload_act_table_set("natural_log_exp_and_others")

            def softplus_parts(m, par):
                act.wait_ge(dt_made, m + 1)
                need(act, corr, m)
                need(act, w_made, m)
                need(act, log_made, m)
                need(act, exped, U * (m - 1))
                nc.scalar.activation(dt[:, par, :], p_p[:, :], ACT.Relu, bias=k["db"][:, :]).then_inc(relu_made, 1)
                nc.scalar.activation(ta[:, :], p_p[:, :], ACT.Abs, bias=k["db"][:, :]).then_inc(dt_taken, 1)

            def softplus_log(m, par):
                act.wait_ge(dt_taken, m + 1)
                nc.scalar.activation(ta[:, :], ta[:, :], ACT.Exp, scale=-1.0).then_inc(e_made, 1)
                act.wait_ge(e_made, m + 1)
                need(act, corr2, m)
                nc.scalar.activation(tb[:, :], ta[:, :], ACT.Ln, bias=c.one[:, :]).then_inc(log_made, 1)

            def bc_high(m, par):
                act.wait_ge(bc_made, m + 1)
                need(act, c_made, U * (m - 1))
                nc.scalar.copy(bcs[:, par, :], p_p[:, :]).then_inc(bc_hi, 1)

            def bc_middle(m, par):
                act.wait_ge(bc_rest, m + 1)
                nc.scalar.copy(bcs[64:128, par, :], rest[64:128, :]).then_inc(bc_mid, 1)

            def unit(n, par, s, first, last):
                u, b = n * U + s, s % 2
                if s == 0:
                    act.wait_ge(dt_done, n + 1)
                need(act, scanned, u - 1)
                nc.scalar.activation(dA[:, b, :], dt[:, par, :], ACT.Exp, scale=k["A"][:, s:s + 1]).then_inc(exped, 1)
                if not (first and s < 2):
                    q = (s - 2) % U
                    e = 0 if back else TC - 1
                    nc.scalar.copy(state[:, q:q + 1], h[:, b, e:e + 1]).then_inc(kept, 1)
                act.wait_ge(b_made, u + 1)
                need(act, injected, u - 1)
                nc.scalar.copy(bb[:, b, :], p_b[:, :]).then_inc(b_taken, 1)

            act.wait_ge(zeroed, 1)
            prepare = [(3, silu_x), (5, softplus_parts), (6, softplus_log), (9, bc_high), (12, bc_middle)]
            exp_log_tables()
            if back:
                run(act, unit, prepare[:1] + [(4, exp_log_tables)] + prepare[1:],
                    [(3, silu_z)], [(15, take_z)])
                silu_z(NC - 1, 1, True)
            else:
                run(act, unit, prepare[:1] + [(3, exp_log_tables)] + prepare[1:])

        @block.gpsimd
        def _(pool):
            def correct(m, par):
                pool.wait_ge(w_made, m + 1)
                nc.gpsimd.tensor_tensor(tc[:, :], ta[:, :], tc[:, :], ALU.subtract).then_inc(corr, 1)

            def correct2(m, par):
                pool.wait_ge(corr, m + 1)
                pool.wait_ge(log_made, m + 1)
                nc.gpsimd.tensor_tensor(tc[:, :], tc[:, :], tb[:, :], ALU.add).then_inc(corr2, 1)

            def dt_x(m, par):
                pool.wait_ge(dt_done, m + 1)
                need(pool, injected, U * (m - 1))
                nc.gpsimd.tensor_tensor(dtx[:, par, :], dt[:, par, :], xc[:, par, :], ALU.mult).then_inc(dtx_done, 1)

            def join(m, par, last):
                pool.wait_ge(y_taken, m + 1)
                pool.wait_ge(y_loaded, 16 * (m + 1))
                nc.gpsimd.tensor_tensor(yo[:, :], yo[:, :], yf[:, :], ALU.add).then_inc(y_joined, 1)

            def unit(n, par, s, first, last):
                u, b = n * U + s, s % 2
                if s == 0:
                    pool.wait_ge(dtx_done, n + 1)
                pool.wait_ge(b_taken, u + 1)
                need(pool, scanned, u - 1)
                nc.gpsimd.tensor_tensor(dbx[:, b, :], dtx[:, par, :], bb[:, b, :], ALU.mult).then_inc(injected, 1)

            nc.gpsimd.memset(state[:, :], 0.0).then_inc(zeroed, 1)
            run(pool, unit, [(8, correct), (10, correct2), (13, dt_x)], [(2, join)] if back else [])
            if back:
                join(NC - 1, 1, True)

        @block.vector
        def _(dve):
            def one_plus(m, par):
                dve.wait_ge(e_made, m + 1)
                need(dve, dt_done, m)
                nc.vector.tensor_scalar(tc[:, :], ta[:, :], 1.0, 1.0, ALU.add, ALU.subtract).then_inc(w_made, 1)

            def step_sum(m, par):
                dve.wait_ge(corr2, m + 1)
                dve.wait_ge(relu_made, m + 1)
                nc.vector.tensor_tensor(dt[:, par, :], dt[:, par, :], tc[:, :], ALU.add).then_inc(dt_done, 1)

            def bc_remainder(m, par):
                dve.wait_ge(bc_hi, m + 1)
                need(dve, bc_low, m)
                need(dve, bc_mid, m)
                nc.vector.tensor_tensor(rest[:, :], p_p[:, :], bcs[:, par, :], ALU.subtract).then_inc(bc_rest, 1)

            def bc_lowest(m, par):
                dve.wait_ge(bc_mid, m + 1)
                dve.wait_ge(bc_rest, m + 1)
                nc.vector.tensor_tensor(bcs[96:128, par, :], rest[96:128, :], bcs[96:128, par, :],
                                        ALU.subtract).then_inc(bc_low, 1)

            def take_y(m, par, last):
                dve.wait_ge(summed, U * (m + 1))
                if back:
                    need(dve, projected, m)
                else:
                    need(dve, y_stored, 16 * m)
                nc.vector.scalar_tensor_tensor(out=yo[:, :], in0=xc[:, par, :], scalar=k["dd"][:, :], in1=p_y[:, :],
                                               op0=ALU.mult, op1=ALU.add).then_inc(y_taken, 1)

            def gate(m, par, last):
                dve.wait_ge(y_joined, m + 1)
                dve.wait_ge(z_taken, m + 1)
                nc.vector.tensor_tensor(yo[:, :], yo[:, :], zs[:, :], ALU.mult).then_inc(y_gated, 1)

            def add_x(m, par, last):
                dve.wait_ge(projected, m + 1)
                rows = TC // Q
                xr = c.x[:, bass.ds(m * -rows + (NC - 1) * rows, rows), :]
                nc.vector.tensor_tensor(xr, xr, p_p[:, 0:rows * D].rearrange("p (r d) -> p r d", d=D),
                                        ALU.add).then_inc(x_done, 1)

            def read_c(u, s):
                b = s % 2
                dve.wait_ge(scanned, u + 1)
                dve.wait_ge(c_made, u + 1)
                need(dve, summed, u - 1)
                nc.vector.tensor_tensor(hc[:, b, :], h[:, b, :], p_c[:, :], ALU.mult).then_inc(read, 1)

            def unit(n, par, s, first, last):
                u, b = n * U + s, s % 2
                dve.wait_ge(exped, u + 1)
                dve.wait_ge(injected, u + 1)
                need(dve, kept, u - 1)
                need(dve, read, u - 1)
                flow = (lambda t: t[:, b, ::-1]) if back else (lambda t: t[:, b, :])
                nc.vector.tensor_tensor_scan(out=flow(h), data0=flow(dA), data1=flow(dbx), initial=state[:, s:s + 1],
                                             op0=ALU.mult, op1=ALU.add).then_inc(scanned, 1)
                if not (first and s == 0):
                    read_c(u - 1, (s - 1) % U)

            dve.wait_ge(zeroed, 1)
            run(dve, unit, [(6, one_plus), (9, bc_remainder), (10, step_sum), (12, bc_lowest)],
                [(1, take_y), (4, gate), (11, add_x)] if back else [(1, take_y)])
            read_c(NC * U - 1, U - 1)
            take_y(NC - 1, 1, True)
            if back:
                gate(NC - 1, 1, True)
                add_x(NC - 1, 1, True)

        @block.sync
        def _(sp):
            if back:
                def load(n):
                    sp.dma_start(yf[:, :], y_scratch[:, bass.ds(base(n), TC)]).then_inc(y_loaded, 16)
                load(0)
                with sp.Fori(1, NC) as n:
                    sp.wait_ge(y_joined, n)
                    load(n)
            else:
                with sp.Fori(0, NC) as n:
                    sp.wait_ge(y_taken, n + 1)
                    sp.dma_start(y_scratch[:, bass.ds(base(n), TC)], yo[:, :]).then_inc(y_stored, 16)
                sp.wait_ge(y_stored, 16 * NC)


EXPERTS = 8


def experts_stage(nc, c, W, out):
    with ExitStack() as ctx:
        def sb(name, shape, dt=F32):
            return ctx.enter_context(nc.sbuf_tensor(name, shape, dt))
        xT = sb("ex_xT", [D + 1, T])
        wr = sb("ex_wr", [D + 1, EXPERTS])
        we = sb("ex_we", [D + 1, EXPERTS, D])
        wt = sb("ex_wt", [Q, S, EXPERTS])
        xg = sb("ex_xg", [D + 1, 2, GT])
        stats_stage(nc, c, "ex_s", 1.0, 1e-5)

        with ExitStack() as wctx:
            loaded = c.sem("ew_loaded")
            set_ = c.sem("ew_set")
            block = wctx.enter_context(nc.Block())

            @block.sync
            def _(sp):
                sp.dma_start(wr[0:D, :], W["router_w"]).then_inc(loaded, 16)
                sp.dma_start(wr[D:D + 1, :], row_of(W["router_b"])).then_inc(loaded, 16)
                sp.dma_start(we[0:D, :, :], W["expert_w"].rearrange("e d c -> d e c")).then_inc(loaded, 16)
                sp.dma_start(we[D:D + 1, :, :], W["expert_b"].rearrange("(a e) c -> a e c", a=1)).then_inc(loaded, 16)
                sp.wait_ge(loaded, 64)

            @block.gpsimd
            def _(pool):
                nc.gpsimd.memset(xT[D:D + 1, :], 1.0).then_inc(set_, 1)
                pool.wait_ge(set_, 1)

        def evacuate(g, ps):
            return nc.scalar.copy(xT[0:D, bass.ds(g * GT, GT)], ps[0:D, :])
        transpose_stage(nc, c, "ex_t", False, evacuate)

        def loads(sp, used, sems):
            def load(g, k):
                need(sp, used, GR * (g - 1))
                sp.dma_start(xg[:, k, :], xT[:, bass.ds(g * GT, GT)]).then_inc(sems[k], 16)
            load(0, 0)
            load(1, 1)
            with sp.Fori(1, NG // 2) as i:
                load(2 * i, 0)
                load(2 * i + 1, 1)

        with ExitStack() as rctx:
            def rsb(name, shape):
                return rctx.enter_context(nc.sbuf_tensor(name, shape, F32))
            p, e, eq = rsb("er_p", [Q, S, EXPERTS]), rsb("er_e", [Q, S, EXPERTS]), rsb("er_eq", [Q, S, EXPERTS])
            top = rsb("er_top", [Q, 2, S])
            key, tot = rsb("er_key", [Q, S]), rsb("er_tot", [Q, S])
            rank = rsb("er_rank", [Q, EXPERTS])
            ps = rctx.enter_context(nc.psum_tensor("er_ps", [Q, S, EXPERTS], F32))
            sem = lambda n: c.sem("er_" + n)
            routed, ranked, steps, shifted, exped = (sem(n) for n in ("routed", "ranked", "steps", "shifted", "exped"))
            loaded = [sem("loaded0"), sem("loaded1")]
            block = rctx.enter_context(nc.Block())
            wide = lambda t: t.rearrange("p (s a) -> p s a", a=1).to_broadcast([Q, S, EXPERTS])

            @block.sync
            def _(sp):
                loads(sp, routed, loaded)

            @block.tensor
            def _(pe):
                with pe.Fori(0, NG // 2) as i:
                    for k in range(2):
                        pe.wait_ge(loaded[k], 16 * (i + 1))
                        for j in range(GR):
                            nc.tensor.matmul(ps[:, bass.ds((2 * i + k) * GR + j, 1), :].rearrange("p a e -> p (a e)"),
                                             lhsT=xg[:, k, j * Q:(j + 1) * Q], rhs=wr[:, :],
                                             start=True, stop=True).then_inc(routed, 1)

            @block.gpsimd
            def _(pool):
                for j in range(EXPERTS):
                    nc.gpsimd.memset(rank[:, j:j + 1], float(EXPERTS - j)).then_inc(ranked, 1)

            @block.scalar
            def _(act):
                act.wait_ge(shifted, 1)
                nc.scalar.activation(e[:, :, :], p[:, :, :], ACT.Exp).then_inc(exped, 1)

            @block.vector
            def _(dve):
                chain = Chain(dve, steps)
                dve.wait_ge(routed, S)
                chain(nc.vector.reduce_max(key[:, :], ps[:, :, :], AX.X))
                nc.vector.tensor_tensor(p[:, :, :], ps[:, :, :], wide(key[:, :]), ALU.subtract).then_inc(shifted, 1)
                dve.wait_ge(exped, 1)
                chain(nc.vector.reduce_sum(tot[:, :], e[:, :, :], AX.X))
                chain(nc.vector.reciprocal(tot[:, :], tot[:, :]))
                chain(nc.vector.tensor_tensor(p[:, :, :], e[:, :, :], wide(tot[:, :]), ALU.mult))
                dve.wait_ge(ranked, EXPERTS)
                ranks = rank[:, :].rearrange("p (a e) -> p a e", a=1).to_broadcast([Q, S, EXPERTS])
                for choice, pick in ((0, e), (1, wt)):
                    chain(nc.vector.reduce_max(top[:, choice, :], p[:, :, :], AX.X))
                    chain(nc.vector.tensor_tensor(eq[:, :, :], p[:, :, :], wide(top[:, choice, :]), ALU.is_equal))
                    chain(nc.vector.tensor_tensor(eq[:, :, :], eq[:, :, :], ranks, ALU.mult))
                    chain(nc.vector.reduce_max(key[:, :], eq[:, :, :], AX.X))
                    chain(nc.vector.tensor_tensor(pick[:, :, :], eq[:, :, :], wide(key[:, :]), ALU.is_equal))
                    if choice == 0:
                        chain(nc.vector.scalar_tensor_tensor(out=p[:, :, :], in0=e[:, :, :], scalar=-2.0,
                                                             in1=p[:, :, :], op0=ALU.mult, op1=ALU.add))
                chain(nc.vector.tensor_tensor(tot[:, :], top[:, 0, :], top[:, 1, :], ALU.add))
                chain(nc.vector.reciprocal(tot[:, :], tot[:, :]))
                for choice, pick in ((0, e), (1, wt)):
                    chain(nc.vector.tensor_tensor(top[:, choice, :], top[:, choice, :], tot[:, :], ALU.mult))
                    chain(nc.vector.tensor_tensor(pick[:, :, :], pick[:, :, :], wide(top[:, choice, :]), ALU.mult))
                chain(nc.vector.tensor_tensor(wt[:, :, :], wt[:, :, :], e[:, :, :], ALU.add))

        with ExitStack() as ectx:
            hw = ectx.enter_context(nc.sbuf_tensor("ee_hw", [Q, 2, EXPERTS + 1, D], F32))
            ps = ectx.enter_context(nc.psum_tensor("ee_ps", [Q, GR, EXPERTS, D], F32))
            sem = lambda n: c.sem("ee_" + n)
            made, weighed, carried, summed, stored = (sem(n) for n in ("made", "weighed", "carried", "summed", "stored"))
            loaded = [sem("loaded0"), sem("loaded1")]
            block = ectx.enter_context(nc.Block())
            ov = out.rearrange("b s q d -> q (b s) d")

            @block.sync
            def _(sp):
                loads(sp, made, loaded)

            @block.tensor
            def _(pe):
                def group(g, k, i):
                    pe.wait_ge(loaded[k], 16 * (i + 1))
                    for j in range(GR):
                        need(pe, weighed, g * GR + j - GR + 1)
                        nc.tensor.matmul(ps[:, j, :, :], lhsT=xg[:, k, j * Q:(j + 1) * Q], rhs=we[:, :, :],
                                         start=True, stop=True).then_inc(made, 1)
                group(0, 0, 0)
                group(1, 1, 0)
                with pe.Fori(1, NG // 2) as i:
                    group(2 * i, 0, i)
                    group(2 * i + 1, 1, i)

            @block.scalar
            def _(act):
                def row(r, b):
                    need(act, summed, r - 1)
                    nc.scalar.copy(hw[:, b, EXPERTS:EXPERTS + 1, :], c.x[:, bass.ds(r, 1), :]).then_inc(carried, 1)
                row(0, 0)
                row(1, 1)
                with act.Fori(1, S // 2) as i:
                    row(2 * i, 0)
                    row(2 * i + 1, 1)

            @block.vector
            def _(dve):
                def weigh(r, j):
                    dve.wait_ge(made, r + 1)
                    need(dve, summed, r - 1)
                    nc.vector.tensor_tensor(
                        hw[:, j % 2, 0:EXPERTS, :], ps[:, j, :, :],
                        wt[:, bass.ds(r, 1), :].rearrange("p a (e b) -> p (a e) b", b=1).to_broadcast([Q, EXPERTS, D]),
                        ALU.mult).then_inc(weighed, 1)

                def add(r, j):
                    dve.wait_ge(weighed, r + 1)
                    dve.wait_ge(carried, r + 1)
                    nc.vector.tensor_reduce(out=c.x[:, bass.ds(r, 1), :].rearrange("p a d -> p (a d)"),
                                            in_=hw[:, j % 2, :, :].rearrange("p e d -> p d e"), axis=AX.X,
                                            op=ALU.add).then_inc(summed, 1)
                weigh(0, 0)
                for j in range(1, GR):
                    weigh(j, j)
                    add(j - 1, j - 1)
                with dve.Fori(1, NG) as g:
                    for j in range(GR):
                        weigh(g * GR + j, j)
                        add(g * GR + j - 1, (j - 1) % GR)
                add(S - 1, GR - 1)

            @block.gpsimd
            def _(pool):
                with pool.Fori(0, NG) as g:
                    pool.wait_ge(summed, GR * (g + 1))
                    nc.gpsimd.dma_start(ov[:, bass.ds(g * GR, GR), :], c.x[:, bass.ds(g * GR, GR), :]).then_inc(stored, 16)
                pool.wait_ge(stored, 16 * NG)


def build(nc, I, out, stages=(0, 1, 2, 3)):
    pair = nc.dram_tensor("pair_scratch", (HEADS, T), F32, kind="Internal").ap()
    with ExitStack() as ctx:
        c = Core(nc, ctx)
        load_stage(nc, c, I["x"])
        if 0 in stages:
            A = {n: I["L0_conv_" + n] for n in ("mask", "gamma", "beta", "Wq", "Wk", "Wv", "Wb", "Wu", "bu", "Wo", "bo")}
            attention_stage(nc, c, A, pair)
            c.clear_semaphores()
        if 1 in stages:
            recurrence_stage(nc, c, *(I["L0_ffn_" + n] for n in ("W", "V", "gamma", "beta")))
            c.clear_semaphores()
        if 2 in stages:
            y = nc.dram_tensor("y_scratch", (INNER, T), F32, kind="Internal").ap()
            W = {n: I["L1_conv_" + n] for n in ("in_w", "conv_w", "conv_b", "x_w", "dt_w", "dt_b", "A_log", "D", "out_w")}
            state_space_stage(nc, c, W, y)
            c.clear_semaphores()
        if 3 in stages:
            experts_stage(nc, c, {n: I["L1_ffn_" + n] for n in ("router_w", "router_b", "expert_w", "expert_b")}, out)
        else:
            store_stage(nc, c, out)


_INS = ['x', 'L0_conv_mask', 'L0_conv_gamma', 'L0_conv_beta', 'L0_conv_Wq', 'L0_conv_Wk', 'L0_conv_Wv', 'L0_conv_Wb',
        'L0_conv_Wu', 'L0_conv_bu', 'L0_conv_Wo', 'L0_conv_bo', 'L0_ffn_W', 'L0_ffn_V', 'L0_ffn_gamma',
        'L0_ffn_beta', 'L1_conv_in_w', 'L1_conv_conv_w', 'L1_conv_conv_b', 'L1_conv_x_w', 'L1_conv_dt_w',
        'L1_conv_dt_b', 'L1_conv_A_log', 'L1_conv_D', 'L1_conv_out_w', 'L1_ffn_router_w', 'L1_ffn_router_b',
        'L1_ffn_expert_w', 'L1_ffn_expert_b']
_OUT = ((1, 128, 128, 64), 'float32')


def kernel(**inputs):
    import numpy as _np
    import concourse.bacc as _bacc
    from concourse import mybir as _mybir
    from concourse.bass_utils import run_bass_kernel_spmd as _run

    nc = _bacc.Bacc("TRN2", target_bir_lowering=False, num_devices=1)
    arrays, aps = {}, {}
    for name in _INS:
        a = _np.ascontiguousarray(inputs[name])
        arrays[f"in_{name}_dram"] = a
        aps[name] = nc.dram_tensor(f"in_{name}_dram", a.shape, _mybir.dt.from_np(a.dtype), kind="ExternalInput").ap()
    shape, dtype = _OUT
    out = nc.dram_tensor("out_0_dram", shape, _mybir.dt.from_np(_np.dtype(dtype)), kind="ExternalOutput").ap()
    build(nc, aps, out)
    r = _run(nc, [arrays], core_ids=[0])
    return r.results[0]["out_0_dram"]
```

```python
import numpy as np
from contextlib import ExitStack
import concourse.bass as bass
from concourse import mybir

F32 = mybir.dt.float32
BF16 = mybir.dt.bfloat16
I32 = mybir.dt.int32
ACT = mybir.ActivationFunctionType
ALU = mybir.AluOpType
AX = mybir.AxisListType

S = 128
Q = 128
D = 64
T = S * Q
GR = 4
GT = GR * Q
NG = S // GR
HEADS, HC = 4, 32
LAG = 6
NEG = 1.0e9


def need(eng, sem, count):
    if not (isinstance(count, int) and count <= 0):
        eng.wait_ge(sem, count)


class Chain:

    def __init__(self, eng, sem):
        self.eng, self.sem, self.base, self.n = eng, sem, 0, 0

    def at(self, base):
        self.base, self.n = base, 0

    def __call__(self, ins):
        self.n += 1
        ins.then_inc(self.sem, 1)
        self.eng.wait_ge(self.sem, self.base + self.n)


def row_of(ap):
    return ap.rearrange("(a n) -> a n", a=1)


def col_of(ap):
    return ap.rearrange("(p a) -> p a", a=1)


class Core:

    def __init__(self, nc, ctx):
        self.nc, self.used = nc, []

        def sb(name, shape, dt=F32):
            return ctx.enter_context(nc.sbuf_tensor(name, shape, dt))
        self.x = sb("x_tok", [Q, S, D])
        self.mean = sb("row_mean", [Q, S])
        self.rstd = sb("row_rstd", [Q, S])
        self.ident = sb("ident", [128, 128])
        self.one = sb("one_col", [128, 1])

    def sem(self, name):
        self.used.append(self.nc.alloc_semaphore(name=name))
        return self.used[-1]

    def clear_semaphores(self):
        self.nc.clear_and_free_semaphores(self.used)
        self.nc.all_engine_barrier()
        self.used = []


def load_stage(nc, c, x_in):
    with ExitStack() as ctx:
        loaded = c.sem("ld_x")
        blank = c.sem("ld_blank")
        made = c.sem("ld_ident")
        block = ctx.enter_context(nc.Block())
        xv = x_in.rearrange("b s q d -> q (b s) d")

        @block.sync
        def _(sp):
            for k in range(4):
                sp.dma_start(c.x[:, k * 32:(k + 1) * 32, :], xv[:, k * 32:(k + 1) * 32, :]).then_inc(loaded, 16)
            sp.wait_ge(loaded, 64)

        @block.gpsimd
        def _(pool):
            nc.gpsimd.memset(c.ident[:, :], 0.0).then_inc(blank, 1)
            nc.gpsimd.memset(c.one[:, :], 1.0).then_inc(made, 1)
            pool.wait_ge(blank, 1)
            nc.gpsimd.affine_select(out=c.ident[:, :], in_=c.ident[:, :], compare_op=ALU.not_equal, fill=1.0,
                                    base=0, pattern=[[-1, 128]], channel_multiplier=1).then_inc(made, 1)
            pool.wait_ge(made, 2)


def store_stage(nc, c, out):
    with ExitStack() as ctx:
        stored = c.sem("st_x")
        block = ctx.enter_context(nc.Block())
        ov = out.rearrange("b s q d -> q (b s) d")

        @block.sync
        def _(sp):
            for k in range(4):
                sp.dma_start(ov[:, k * 32:(k + 1) * 32, :], c.x[:, k * 32:(k + 1) * 32, :]).then_inc(stored, 16)
            sp.wait_ge(stored, 64)


def stats_stage(nc, c, name, var_scale, var_add):
    with ExitStack() as ctx:
        st = ctx.enter_context(nc.sbuf_tensor(name + "_st", [Q, S, 6], F32))
        dd = ctx.enter_context(nc.sbuf_tensor(name + "_dd", [Q, S], F32))
        vv = ctx.enter_context(nc.sbuf_tensor(name + "_vv", [Q, S], F32))
        sem = lambda n: c.sem(name + n)
        rows_done, steps, var_ready, std_ready = sem("_rows"), sem("_steps"), sem("_var"), sem("_std")
        block = ctx.enter_context(nc.Block())
        UN = 16

        @block.vector
        def _(dve):
            with dve.Fori(0, S // UN) as i:
                r = i * UN
                for j in range(UN):
                    nc.vector.bn_stats(st[:, bass.ds(r + j, 1), :].rearrange("p a n -> p (a n)"),
                                       c.x[:, bass.ds(r + j, 1), :].rearrange("p a n -> p (a n)")).then_inc(rows_done, 1)
            dve.wait_ge(rows_done, S)
            me, m2e, mo, m2o = st[:, :, 1], st[:, :, 2], st[:, :, 4], st[:, :, 5]
            chain = Chain(dve, steps)
            nc.vector.tensor_tensor(vv[:, :], m2e, m2o, ALU.add).then_inc(rows_done, 1)
            nc.vector.tensor_tensor(c.mean[:, :], me, mo, ALU.add).then_inc(rows_done, 1)
            chain(nc.vector.tensor_tensor(dd[:, :], me, mo, ALU.subtract))
            chain(nc.vector.tensor_tensor(dd[:, :], dd[:, :], dd[:, :], ALU.mult))
            dve.wait_ge(rows_done, S + 2)
            chain(nc.vector.scalar_tensor_tensor(out=vv[:, :], in0=dd[:, :], scalar=D / 4.0, in1=vv[:, :],
                                                 op0=ALU.mult, op1=ALU.add))
            nc.vector.tensor_scalar(vv[:, :], vv[:, :], var_scale / D, var_add, ALU.mult, ALU.add).then_inc(var_ready, 1)
            chain(nc.vector.tensor_scalar(c.mean[:, :], c.mean[:, :], 0.5, None, ALU.mult))
            dve.wait_ge(std_ready, 1)
            chain(nc.vector.reciprocal(c.rstd[:, :], dd[:, :]))

        @block.scalar
        def _(act):
            act.wait_ge(var_ready, 1)
            nc.scalar.activation(dd[:, :], vv[:, :], ACT.Sqrt).then_inc(std_ready, 1)
            act.wait_ge(std_ready, 1)


def transpose_stage(nc, c, name, paired, evacuate, dve_extra=None):
    groups = NG // 2 if paired else NG
    with ExitStack() as ctx:
        ring = ctx.enter_context(nc.sbuf_tensor(name + "_ring", [Q, 2, GR, 2, D], F32))
        ps = ctx.enter_context(nc.psum_tensor(name + "_ps", [128, 2, GT], F32))
        sem = lambda n: c.sem(name + n)
        normed, turned, taken = sem("_normed"), sem("_turned"), sem("_taken")
        block = ctx.enter_context(nc.Block())
        per = 2 * GR if paired else GR

        @block.vector
        def _(dve):
            def group(g, k):
                need(dve, turned, g - 1)
                for j in range(GR):
                    for half in ((0, 1) if paired else (0,)):
                        row = GR * g + j + half * (S // 2)
                        src = c.x[:, bass.ds(row, 1), :]
                        if paired:
                            dst = ring[:, k, j, half:half + 1, :]
                        else:
                            dst, src = ring[:, k, j, :, :], src.to_broadcast([Q, 2, D])
                        nc.vector.tensor_scalar(dst, src, c.mean[:, bass.ds(row, 1)], c.rstd[:, bass.ds(row, 1)],
                                                ALU.subtract, ALU.mult).then_inc(normed, 1)
            group(0, 0)
            group(1, 1)
            with dve.Fori(1, groups // 2) as i:
                g = 2 * i
                group(g, 0)
                group(g + 1, 1)

        @block.tensor
        def _(pe):
            def group(g, k):
                need(pe, taken, g - 1)
                pe.wait_ge(normed, per * (g + 1))
                for j in range(GR):
                    ins = nc.tensor.transpose(ps[:, k, j * Q:(j + 1) * Q],
                                              ring[:, k, j, :, :].rearrange("p a d -> p (a d)"), c.ident[:, :])
                ins.then_inc(turned, 1)
            group(0, 0)
            group(1, 1)
            with pe.Fori(1, groups // 2) as i:
                g = 2 * i
                group(g, 0)
                group(g + 1, 1)

        @block.scalar
        def _(act):
            with act.Fori(0, groups // 2) as i:
                g = 2 * i
                for k in range(2):
                    act.wait_ge(turned, g + k + 1)
                    evacuate(g + k, ps[:, k, :]).then_inc(taken, 1)


def attention_stage(nc, c, A, pair_scratch):
    with ExitStack() as ctx:
        def sb(name, shape, dt=F32):
            return ctx.enter_context(nc.sbuf_tensor(name, shape, dt))
        xT = sb("at_xT", [D + 1, T])
        wq, wk = sb("at_wq", [D, 128]), sb("at_wk", [D, 128])
        wvu = sb("at_wvu", [D + 1, 256])
        wb = sb("at_wb", [D, 128])
        wo = sb("at_wo", [128, D])
        bo = sb("at_bo", [1, D])
        ones = sb("at_ones", [1, 128])
        gamma, beta = sb("at_gamma", [D, 1]), sb("at_beta", [D, 1])
        mask, maskT = sb("at_mask", [128, 128]), sb("at_maskT", [128, 128])
        bias = sb("at_bias", [128, HEADS, 128])

        stats_stage(nc, c, "at_s", 1.0 + 1e-5, 1e-5 * 1e-6)
        with ExitStack() as wctx:
            wsem = c.sem("at_w")
            set_ = c.sem("at_set")
            block = wctx.enter_context(nc.Block())

            @block.sync
            def _(sp):
                n = 0
                for dst, src in ((wq[:, :], A["Wq"]), (wk[:, :], A["Wk"]), (wvu[0:D, 0:128], A["Wv"]),
                                 (wvu[0:D, 128:256], A["Wu"]), (wvu[D:D + 1, 128:256], row_of(A["bu"])),
                                 (wb[:, 0:HEADS], A["Wb"]), (wo[:, :], A["Wo"]), (bo[:, :], row_of(A["bo"])),
                                 (gamma[:, :], col_of(A["gamma"])), (beta[:, :], col_of(A["beta"])),
                                 (mask[:, :], A["mask"].rearrange("n s q -> (n s) q"))):
                    sp.dma_start(dst, src).then_inc(wsem, 16)
                    n += 16
                sp.wait_ge(wsem, n)

            @block.gpsimd
            def _(pool):
                nc.gpsimd.memset(xT[D:D + 1, :], 1.0).then_inc(set_, 1)
                nc.gpsimd.memset(wvu[D:D + 1, 0:128], 0.0).then_inc(set_, 1)
                nc.gpsimd.memset(ones[:, :], 1.0).then_inc(set_, 1)
                nc.gpsimd.memset(wb[:, HEADS:128], 0.0).then_inc(set_, 1)
                pool.wait_ge(set_, 4)

        def evacuate(g, ps):
            return nc.scalar.activation(xT[0:D, bass.ds(g * GT, GT)], ps[0:D, :], ACT.Identity,
                                        bias=beta[:, :], scale=gamma[:, :])
        transpose_stage(nc, c, "at_t", False, evacuate)

        with ExitStack() as bctx:
            pb = bctx.enter_context(nc.sbuf_tensor("at_pb", [HEADS, 2, GT], F32))
            psb = bctx.enter_context(nc.psum_tensor("at_psb", [128, 2, GT], F32))
            pst = bctx.enter_context(nc.psum_tensor("at_pst", [128, 128], F32))
            sem = lambda n: c.sem("ab_" + n)
            projected, copied, loaded, masked, turned, done = (
                sem(n) for n in ("proj", "copied", "loaded", "masked", "turned", "done"))
            stored = [sem("stored0"), sem("stored1")]
            block = bctx.enter_context(nc.Block())

            @block.tensor
            def _(pe):
                nc.tensor.transpose(pst[:, :], mask[:, :], c.ident[:, :]).then_inc(turned, 1)

                def group(g, k):
                    need(pe, copied, g - 1)
                    nc.tensor.matmul(psb[:, k, :], lhsT=wb[:, :], rhs=xT[0:D, bass.ds(g * GT, GT)],
                                     start=True, stop=True).then_inc(projected, 1)
                group(0, 0)
                group(1, 1)
                with pe.Fori(1, NG // 2) as i:
                    g = 2 * i
                    group(g, 0)
                    group(g + 1, 1)

            @block.scalar
            def _(act):
                def group(g, k, stores=0):
                    act.wait_ge(projected, g + 1)
                    need(act, stored[k], 16 * stores)
                    nc.scalar.copy(pb[:, k, :], psb[0:HEADS, k, :]).then_inc(copied, 1)
                group(0, 0)
                group(1, 1)
                with act.Fori(1, NG // 2) as i:
                    group(2 * i, 0, i)
                    group(2 * i + 1, 1, i)

            @block.sync
            def _(sp):
                with sp.Fori(0, NG // 2) as i:
                    g = 2 * i
                    for k in range(2):
                        sp.wait_ge(copied, g + k + 1)
                        sp.dma_start(pair_scratch[:, bass.ds((g + k) * GT, GT)], pb[:, k, :]).then_inc(stored[k], 16)
                for k in range(2):
                    sp.wait_ge(stored[k], 16 * NG // 2)
                sp.dma_start(bias[:, :, :], pair_scratch.rearrange("h (q v) -> q h v", q=128)).then_inc(loaded, 16)
                sp.wait_ge(loaded, 16)

            @block.vector
            def _(dve):
                dve.wait_ge(turned, 1)
                nc.vector.tensor_copy(maskT[:, :], pst[:, :]).then_inc(done, 1)
                nc.vector.tensor_scalar(mask[:, :], mask[:, :], 1.0, NEG, ALU.subtract, ALU.mult).then_inc(masked, 1)
                nc.vector.tensor_scalar(wo[:, :], wo[:, :], 0.5, None, ALU.mult).then_inc(done, 1)
                dve.wait_ge(masked, 1)
                dve.wait_ge(loaded, 16)
                for h in range(HEADS):
                    nc.vector.tensor_tensor(bias[:, h, :], bias[:, h, :], mask[:, :], ALU.add).then_inc(done, 1)
                dve.wait_ge(done, 2 + HEADS)

        attention_rows(nc, c, xT, wq, wk, wvu, wo, bo, ones, maskT, bias)


def row_steps(eng, step):
    def group(g, k, pair, has=lambda j: lambda lag: True):
        for j in range(GR):
            step(g * GR + j, j, g, k, has(j), pair)
    group(0, 0, 0, lambda j: lambda lag: lag <= j)
    group(1, 1, 1, lambda j: lambda lag: lag <= GR + j)
    with eng.Fori(1, NG // 2 - 1) as i:
        group(2 * i, 0, i)
        group(2 * i + 1, 1, i + 1)
    group(NG - 2, 0, NG // 2 - 1)
    group(NG - 1, 1, None)
    for d in range(LAG):
        step(S + d, d % GR, None, None, lambda lag: lag > d, None)


def attention_rows(nc, c, xT, wq, wk, wvu, wo, bo, ones, maskT, bias):
    with ExitStack() as ctx:
        def sb(name, shape, dt=F32):
            return ctx.enter_context(nc.sbuf_tensor(name, shape, dt))
        xg = sb("ar_xg", [D + 1, 2, GT])
        kT = sb("ar_kT", [128, 2, GT])
        qd = sb("ar_qd", [128, 2, GR, HEADS, 128])
        va = sb("ar_va", [128, GR, HEADS, HC + 1])
        gate = sb("ar_gate", [128, GR, 128])
        sc = sb("ar_sc", [128, GR, HEADS, 128])
        mx = sb("ar_mx", [128, GR, HEADS])
        ex = sb("ar_ex", [128, 2, HEADS, 128])
        exT = sb("ar_exT", [128, 2, HEADS * 128])
        rs = sb("ar_rs", [128, 2, HEADS])
        og = sb("ar_og", [128, 2, 128])
        og2 = sb("ar_og2", [128, 2, 128])
        ogT = sb("ar_ogT", [128, 2, 128])
        ps_s = ctx.enter_context(nc.psum_tensor("ar_pss", [128, 2, HEADS, 128], F32))
        ps_p = ctx.enter_context(nc.psum_tensor("ar_psp", [128, GT], F32))
        ps_v = ctx.enter_context(nc.psum_tensor("ar_psv", [128, 512], F32))
        ps_t = ctx.enter_context(nc.psum_tensor("ar_pst", [128, 512], F32))
        ps_o = ctx.enter_context(nc.psum_tensor("ar_pso", [128, 512], F32))
        ps_ot = ctx.enter_context(nc.psum_tensor("ar_psot", [128, 512], F32))
        ps_y = ctx.enter_context(nc.psum_tensor("ar_psy", [128, 512], F32))
        o_v = ps_o[:, 0:HEADS * (HC + 1)].rearrange("p (h c) -> p h c", h=HEADS)
        o_t = ps_ot[:, 0:128]
        o_y = ps_y[:, 0:D]
        sem = lambda n: c.sem("ar_" + n)
        g_proj, g_taken = sem("g_proj"), sem("g_taken")
        g_loaded = [sem("g_loaded0"), sem("g_loaded1")]
        (scored, vu_made, v_taken, g_made, added, maxed, shifted, exped, e_turned, e_taken, o_made,
         summed, gated, scaled, o_turned, o_taken, y_made, x_done, ones_set) = (
            sem(n) for n in ("scored", "vu", "v", "g", "added", "maxed", "shifted", "exped", "e_turned", "e_taken",
                             "o", "summed", "gated", "scaled", "o_turned", "o_taken", "y", "x", "ones"))
        block = ctx.enter_context(nc.Block())
        SCALE = float(HC) ** -0.5

        @block.sync
        def _(sp):
            def load(g, k):
                need(sp, vu_made, GR * (g - 1))
                sp.dma_start(xg[:, k, :], xT[:, bass.ds(g * GT, GT)]).then_inc(g_loaded[k], 16)
            load(0, 0)
            load(1, 1)
            with sp.Fori(1, NG // 2) as i:
                g = 2 * i
                load(g, 0)
                load(g + 1, 1)

        @block.tensor
        def _(pe):
            def project(g, k, which, pair):
                pe.wait_ge(g_loaded[k], 16 * (pair + 1))
                need(pe, g_taken, 2 * g + which)
                nc.tensor.matmul(ps_p[:, :], lhsT=(wq, wk)[which][:, :], rhs=xg[0:D, k, :],
                                 start=True, stop=True).then_inc(g_proj, 1)

            def score(r, j, g, k):
                pe.wait_ge(g_taken, 2 * (g + 1))
                need(pe, added, r - 1)
                nc.tensor.matmul(ps_s[:, j % 2, :, :], lhsT=kT[:, k, j * 128:(j + 1) * 128],
                                 rhs=qd[:, k, j, :, :], start=True, stop=True).then_inc(scored, 1)

            def values_gate(r, j, k):
                need(pe, v_taken, r)
                need(pe, g_made, r)
                nc.tensor.matmul(ps_v[:, 0:256], lhsT=xg[:, k, j * 128:(j + 1) * 128], rhs=wvu[:, :],
                                 start=True, stop=True).then_inc(vu_made, 1)

            def turn(r, j):
                pe.wait_ge(exped, r + 1)
                need(pe, e_taken, r)
                for h in range(HEADS):
                    ins = nc.tensor.transpose(ps_t[:, h * 128:(h + 1) * 128], ex[:, j % 2, h, :], c.ident[:, :])
                ins.then_inc(e_turned, 1)

            def attend(r, j):
                pe.wait_ge(e_taken, r + 1)
                pe.wait_ge(v_taken, r + 1)
                need(pe, gated, r)
                need(pe, summed, r)
                for h in range(HEADS):
                    ins = nc.tensor.matmul(o_v[:, h, :], lhsT=exT[:, j % 2, h * 128:(h + 1) * 128],
                                           rhs=va[:, j, h, :], start=True, stop=True)
                ins.then_inc(o_made, 1)

            def turn_output(r, j):
                pe.wait_ge(scaled, r + 1)
                need(pe, o_taken, r)
                nc.tensor.transpose(o_t, og2[:, j % 2, :], c.ident[:, :]).then_inc(o_turned, 1)

            def project_output(r, j):
                pe.wait_ge(o_taken, r + 1)
                need(pe, x_done, r)
                nc.tensor.matmul(o_y, lhsT=ogT[:, j % 2, :], rhs=wo[:, :], start=True, stop=False)
                nc.tensor.matmul(o_y, lhsT=ones[:, :], rhs=bo[:, :], start=False, stop=True).then_inc(y_made, 1)

            def step(r, j, g, k, has, pair):
                if has(0):
                    score(r, j, g, k)
                if has(2):
                    turn(r - 2, (j - 2) % GR)
                if has(3):
                    attend(r - 3, (j - 3) % GR)
                if has(0):
                    values_gate(r, j, k)
                if has(4):
                    turn_output(r - 4, j)
                if has(5):
                    project_output(r - 5, (j - 5) % GR)
                if pair is not None and j in (1, 2):
                    project(g + 1, 1 - k, j - 1, pair)
            pe.wait_ge(ones_set, 2)
            project(0, 0, 0, 0)
            project(0, 0, 1, 0)
            row_steps(pe, step)

        @block.vector
        def _(dve):
            nc.vector.memset(va[:, :, :, HC:HC + 1], 1.0).then_inc(ones_set, 1)
            nc.vector.memset(qd[:, :, :, :, :], 0.0).then_inc(ones_set, 1)

            def add_bias(r, j):
                dve.wait_ge(scored, r + 1)
                need(dve, exped, r - 3)
                nc.vector.tensor_tensor(sc[:, j, :, :], ps_s[:, j % 2, :, :], bias[:, :, :], ALU.add).then_inc(added, 1)

            def maximum(r, j):
                dve.wait_ge(added, r + 1)
                need(dve, shifted, r - 3)
                nc.vector.reduce_max(mx[:, j, :], sc[:, j, :, :], AX.X).then_inc(maxed, 1)

            def invert_sums(r, j):
                dve.wait_ge(o_made, r + 1)
                need(dve, scaled, r - 1)
                nc.vector.reciprocal(rs[:, j % 2, :], o_v[:, :, HC]).then_inc(summed, 1)

            def apply_gate(r, j):
                dve.wait_ge(g_made, r + 1)
                need(dve, scaled, r - 1)
                nc.vector.scalar_tensor_tensor(
                    out=og[:, j % 2, :].rearrange("p (h c) -> p h c", h=HEADS),
                    in0=gate[:, j, :].rearrange("p (h c) -> p h c", h=HEADS), scalar=1.0, in1=o_v[:, :, 0:HC],
                    op0=ALU.add, op1=ALU.mult).then_inc(gated, 1)

            def normalise(r, j):
                b = j % 2
                dve.wait_ge(gated, r + 1)
                dve.wait_ge(summed, r + 1)
                need(dve, o_turned, r - 1)
                nc.vector.tensor_tensor(og2[:, b, :].rearrange("p (h c) -> p h c", h=HEADS),
                                        og[:, b, :].rearrange("p (h c) -> p h c", h=HEADS),
                                        rs[:, b, :].rearrange("p (h a) -> p h a", a=1).to_broadcast([128, HEADS, HC]),
                                        ALU.mult).then_inc(scaled, 1)

            def add_to_x(r):
                dve.wait_ge(y_made, r + 1)
                xr = c.x[:, bass.ds(r, 1), :].rearrange("p a d -> p (a d)")
                nc.vector.scalar_tensor_tensor(out=xr, in0=o_y, scalar=maskT[:, bass.ds(r, 1)], in1=xr,
                                               op0=ALU.mult, op1=ALU.add).then_inc(x_done, 1)

            def step(r, j, g, k, has, pair):
                if has(6):
                    add_to_x(r - 6)
                if has(0):
                    add_bias(r, j)
                if has(3):
                    invert_sums(r - 3, (j - 3) % GR)
                    apply_gate(r - 3, (j - 3) % GR)
                if has(0):
                    maximum(r, j)
                if has(3):
                    normalise(r - 3, (j - 3) % GR)
            row_steps(dve, step)
            dve.wait_ge(x_done, S)

        @block.gpsimd
        def _(pool):
            with pool.Fori(0, NG) as g:
                for j in range(GR):
                    pool.wait_ge(maxed, g * GR + j + 1)
                    nc.gpsimd.tensor_tensor(sc[:, j, :, :], sc[:, j, :, :],
                                            mx[:, j, :].rearrange("p (h a) -> p h a", a=1).to_broadcast([128, HEADS, 128]),
                                            ALU.subtract).then_inc(shifted, 1)

        @block.scalar
        def _(act):
            def take(g, k, which):
                act.wait_ge(g_proj, 2 * g + which + 1)
                need(act, scored, GR * (g - 1))
                if which == 0:
                    for h in range(HEADS):
                        p = slice(HC * h, HC * (h + 1))
                        ins = nc.scalar.activation(qd[p, k, :, h, :], ps_p[p, :].rearrange("p (j v) -> p j v", j=GR),
                                                   ACT.Copy, scale=SCALE)
                else:
                    ins = nc.scalar.copy(kT[:, k, :], ps_p[:, :])
                ins.then_inc(g_taken, 1)

            def values(r, j):
                act.wait_ge(vu_made, r + 1)
                need(act, o_made, r - 3)
                nc.scalar.copy(va[:, j, :, 0:HC], ps_v[:, 0:128].rearrange("p (h c) -> p h c", h=HEADS)).then_inc(v_taken, 1)
                need(act, gated, r - 3)
                nc.scalar.activation(gate[:, j, :], ps_v[:, 128:256], ACT.Tanh, scale=0.5).then_inc(g_made, 1)

            def take_turned(r, j):
                act.wait_ge(e_turned, r + 1)
                need(act, o_made, r - 1)
                nc.scalar.copy(exT[:, j % 2, :], ps_t[:, :]).then_inc(e_taken, 1)

            def take_output(r, j):
                act.wait_ge(o_turned, r + 1)
                need(act, y_made, r - 1)
                nc.scalar.copy(ogT[:, j % 2, :], o_t).then_inc(o_taken, 1)

            def exponentiate(r, j):
                act.wait_ge(shifted, r + 1)
                need(act, e_turned, r - 1)
                nc.scalar.activation(ex[:, j % 2, :, :], sc[:, j, :, :], ACT.Exp).then_inc(exped, 1)

            def step(r, j, g, k, has, pair):
                if has(1):
                    exponentiate(r - 1, (j - 1) % GR)
                if pair is not None and j in (2, 3):
                    take(g + 1, 1 - k, j - 2)
                if has(2):
                    take_turned(r - 2, (j - 2) % GR)
                if has(0):
                    values(r, j)
                if has(4):
                    take_output(r - 4, j)
            act.wait_ge(ones_set, 2)
            take(0, 0, 0)
            take(0, 0, 1)
            row_steps(act, step)


def recurrence_stage(nc, c, W, V, gamma, beta):
    CH, L, HEAD = 256, 64, 16
    HALF = CH // 2
    TOL = 2.0 ** -21
    assert CH * L == T
    with ExitStack() as ctx:
        def sb(name, shape, dt=F32):
            return ctx.enter_context(nc.sbuf_tensor(name, shape, dt))
        n = sb("rn_n", [128, L, HALF])
        y = sb("rn_y", [128, L, HALF])
        stats_stage(nc, c, "rn_s", 1.0, 1e-5)

        def evacuate(g, ps):
            cs = Q // L * GR
            return nc.scalar.copy(n[:, :, bass.ds(g * cs, cs)].rearrange("p j c -> p c j"),
                                  ps.rearrange("p (c j) -> p c j", j=L))
        transpose_stage(nc, c, "rn_t", True, evacuate)

        wd = sb("rn_wd", [128, 128])
        wT = sb("rn_wT", [128, 128])
        vd, vT = sb("rn_vd", [128, 128]), sb("rn_vT", [128, 128])
        join = sb("rn_join", [128, 128])
        shift = sb("rn_shift", [128, 128])
        gm, bt = sb("rn_gamma", [128, 1]), sb("rn_beta", [128, 1])
        a, cc = sb("rn_a", [128, 1]), sb("rn_c", [128, 1])
        y0 = sb("rn_y0", [128, HALF])
        yh = sb("rn_yh", [128, HEAD, HALF])
        flag = sb("rn_flag", [1, 1], I32)

        with ExitStack() as bctx:
            st = bctx.enter_context(nc.sbuf_tensor("rn_st", [128, 16, 6], F32))
            mv = bctx.enter_context(nc.sbuf_tensor("rn_mv", [128, 2], F32))
            mc = bctx.enter_context(nc.sbuf_tensor("rn_mc", [128, 4], F32))
            ps = bctx.enter_context(nc.psum_tensor("rn_psw", [128, 2, 512], F32))
            pj = bctx.enter_context(nc.psum_tensor("rn_psj", [128, 512], F32))
            pt = bctx.enter_context(nc.psum_tensor("rn_pst", [128, 512], F32))
            sem = lambda s: c.sem("rb_" + s)
            cleared, loaded, turned, copied, made, read, joined, steps, var_ready, std_ready = (
                sem(s) for s in ("cleared", "loaded", "turned", "copied", "made", "read", "joined", "steps",
                                 "var", "std"))
            block = bctx.enter_context(nc.Block())

            @block.gpsimd
            def _(pool):
                for m in (wd, vd, join, shift):
                    nc.gpsimd.memset(m[:, :], 0.0).then_inc(cleared, 1)
                pool.wait_ge(cleared, 4)
                for k, base in enumerate((0, -D, D)):
                    nc.gpsimd.affine_select(out=join[:, :], in_=join[:, :], compare_op=ALU.not_equal, fill=0.5,
                                            base=base, pattern=[[-1, 128]], channel_multiplier=1).then_inc(cleared, 1)
                    pool.wait_ge(cleared, 5 + k)
                nc.gpsimd.affine_select(out=shift[:, :], in_=shift[:, :], compare_op=ALU.not_equal, fill=1.0,
                                        base=D, pattern=[[-1, 128]], channel_multiplier=1).then_inc(cleared, 1)
                pool.wait_ge(cleared, 8)

            @block.sync
            def _(sp):
                sp.wait_ge(cleared, 4)
                k = 0
                for half in (slice(0, D), slice(D, 2 * D)):
                    for dst, src in ((wd[half, half], W), (vd[half, half], V), (gm[half, :], col_of(gamma)),
                                     (bt[half, :], col_of(beta))):
                        sp.dma_start(dst, src).then_inc(loaded, 16)
                        k += 16
                sp.wait_ge(loaded, k)

            @block.tensor
            def _(pe):
                pe.wait_ge(loaded, 128)
                nc.tensor.transpose(pt[:, 0:128], wd[:, :], c.ident[:, :])
                nc.tensor.transpose(pt[:, 128:256], vd[:, :], c.ident[:, :]).then_inc(turned, 1)
                pe.wait_ge(copied, 2)
                nf = n[:, :, :].rearrange("p j c -> p (j c)")
                for k in range(16):
                    need(pe, read, k - 1)
                    nc.tensor.matmul(ps[:, k % 2, :], lhsT=wT[:, :], rhs=nf[:, k * 512:(k + 1) * 512],
                                     start=True, stop=True).then_inc(made, 1)
                pe.wait_ge(steps, 1)
                pe.wait_ge(cleared, 8)
                nc.tensor.matmul(pj[:, 0:1], lhsT=join[:, :], rhs=mv[:, 0:1], start=True, stop=True).then_inc(joined, 1)
                pe.wait_ge(steps, 5)
                nc.tensor.matmul(pj[:, 1:2], lhsT=join[:, :], rhs=mc[:, 2:3], start=True, stop=True).then_inc(joined, 1)
                pe.wait_ge(steps, 7)
                nc.tensor.transpose(pt[:, 0:128], wd[:, :], c.ident[:, :]).then_inc(turned, 1)

            @block.vector
            def _(dve):
                chain = Chain(dve, steps)
                dve.wait_ge(turned, 1)
                nc.vector.tensor_copy(wT[:, :], pt[:, 0:128]).then_inc(copied, 1)
                nc.vector.tensor_copy(vT[:, :], pt[:, 128:256]).then_inc(copied, 1)
                for k in range(16):
                    dve.wait_ge(made, k + 1)
                    nc.vector.bn_stats(st[:, k, :], ps[:, k % 2, :]).then_inc(read, 1)
                dve.wait_ge(read, 16)
                chain(nc.vector.bn_aggr(mv[:, :], st[:, :, :].rearrange("p k s -> p (k s)")))
                dve.wait_ge(joined, 1)
                chain(nc.vector.tensor_copy(mc[:, 0:1], pj[:, 0:1]))
                chain(nc.vector.tensor_tensor(mc[:, 1:2], mv[:, 0:1], mc[:, 0:1], ALU.subtract))
                chain(nc.vector.tensor_tensor(mc[:, 1:2], mc[:, 1:2], mc[:, 1:2], ALU.mult))
                chain(nc.vector.tensor_tensor(mc[:, 2:3], mc[:, 1:2], mv[:, 1:2], ALU.add))
                dve.wait_ge(joined, 2)
                nc.vector.tensor_scalar(mc[:, 3:4], pj[:, 1:2], 1e-5, None, ALU.add).then_inc(var_ready, 1)
                dve.wait_ge(std_ready, 1)
                chain(nc.vector.reciprocal(a[:, :], mc[:, 2:3]))
                dve.wait_ge(loaded, 128)
                chain(nc.vector.tensor_scalar(wd[:, :], wd[:, :], a[:, :], gm[:, :], ALU.mult, ALU.mult))
                chain(nc.vector.tensor_scalar(cc[:, :], mc[:, 0:1], a[:, :], gm[:, :], ALU.mult, ALU.mult))
                chain(nc.vector.tensor_tensor(cc[:, :], bt[:, :], cc[:, :], ALU.subtract))
                dve.wait_ge(turned, 2)
                chain(nc.vector.tensor_copy(wT[:, :], pt[:, 0:128]))

            @block.scalar
            def _(act):
                act.wait_ge(var_ready, 1)
                nc.scalar.activation(mc[:, 2:3], mc[:, 3:4], ACT.Sqrt).then_inc(std_ready, 1)
                act.wait_ge(std_ready, 1)

        with ExitStack() as sctx:
            pu = sctx.enter_context(nc.psum_tensor("rn_psu", [128, 4, 512], F32))
            pe_end = sctx.enter_context(nc.psum_tensor("rn_pse", [128, 512], F32))
            pf = sctx.enter_context(nc.psum_tensor("rn_psf", [128, 512], F32))
            diff = sctx.enter_context(nc.sbuf_tensor("rn_diff", [128, HALF], F32))
            worst = sctx.enter_context(nc.sbuf_tensor("rn_worst", [128, 1], F32))
            worst1 = sctx.enter_context(nc.sbuf_tensor("rn_worst1", [1, 1], F32))
            sem = lambda s: c.sem("rs_" + s)
            summed, stepped, shifted, started, compared, worst_turned, flagged = (
                sem(s) for s in ("summed", "stepped", "shifted", "started", "compared", "turned", "flagged"))
            more_summed, more_stepped, more_shifted, more_started = (
                sem(s) for s in ("more_summed", "more_stepped", "more_shifted", "more_started"))
            block = sctx.enter_context(nc.Block())
            UN = 4

            def drive(pe, slot, j, first=False):
                return nc.tensor.matmul(pu[:, slot, 0:HALF], lhsT=wT[:, :], rhs=at(n, j), start=True, stop=first)

            def at(tile, j):
                return tile[:, j, :] if isinstance(j, int) else tile[:, bass.ds(j, 1), :].rearrange("p a c -> p (a c)")

            @block.tensor
            def _(pe):
                def step(t, slot, before, summed, stepped):
                    if t is not None:
                        pe.wait_ge(stepped, t)
                    nc.tensor.matmul(pu[:, slot, 0:HALF], lhsT=vT[:, :], rhs=before, start=False,
                                     stop=True).then_inc(summed, 1)

                drive(pe, 0, 0, first=True).then_inc(summed, 1)
                drive(pe, 1, 1)
                step(1, 1, at(y, 0), summed, stepped)
                for j in (2, 3):
                    drive(pe, j, j)
                    step(j, j, at(y, j - 1), summed, stepped)
                with pe.Fori(1, L // UN) as i:
                    for k in range(UN):
                        j = i * UN + k
                        drive(pe, k, j)
                        step(j, k, at(y, j - 1), summed, stepped)
                pe.wait_ge(stepped, L)
                nc.tensor.matmul(pe_end[:, 0:1], lhsT=shift[:, :], rhs=y[:, L - 1, HALF - 1:HALF],
                                 start=True, stop=True).then_inc(shifted, 1)
                for j in range(HEAD):
                    drive(pe, j % UN, j)
                    if j == 0:
                        pe.wait_ge(started, 2)
                    step(L + j, j % UN, at(yh, j - 1) if j else y0[:, :], summed, stepped)
                pe.wait_ge(compared, 2)
                nc.tensor.transpose(pf[0:1, 0:128], worst[:, :], c.ident[:, :]).then_inc(worst_turned, 1)
                pe.wait_ge(flagged, 1)
                unmet = nc.tensor.value_load(flag[0:1, 0:1], min_val=0, max_val=1)
                with pe.If(unmet > 0):
                    with pe.Fori(0, CH) as sweep:
                        nc.tensor.matmul(pe_end[:, 0:1], lhsT=shift[:, :], rhs=y[:, L - 1, HALF - 1:HALF],
                                         start=True, stop=True).then_inc(more_shifted, 1)
                        drive(pe, 0, 0)
                        pe.wait_ge(more_started, 2 * sweep + 2)
                        step(None, 0, y0[:, :], more_summed, more_stepped)
                        for j in range(1, UN):
                            drive(pe, j, j)
                            step(sweep * L + j, j, at(y, j - 1), more_summed, more_stepped)
                        with pe.Fori(1, L // UN) as i:
                            for k in range(UN):
                                j = i * UN + k
                                drive(pe, k, j)
                                step(sweep * L + j, k, at(y, j - 1), more_summed, more_stepped)
                        pe.wait_ge(more_stepped, sweep * L + L)

            @block.scalar
            def _(act):
                def step(t, slot, out, summed, stepped):
                    act.wait_ge(summed, t + 1)
                    nc.scalar.activation(out, pu[:, slot, 0:HALF], ACT.Sigmoid, bias=cc[:, :]).then_inc(stepped, 1)
                with act.Fori(0, L // UN) as i:
                    for k in range(UN):
                        step(i * UN + k, k, at(y, i * UN + k), summed, stepped)
                for j in range(HEAD):
                    step(L + j, j % UN, at(yh, j), summed, stepped)
                act.wait_ge(flagged, 1)
                unmet = nc.scalar.value_load(flag[0:1, 0:1], min_val=0, max_val=1)
                with act.If(unmet > 0):
                    with act.Fori(0, CH) as sweep:
                        act.wait_ge(more_started, 2 * sweep + 2)
                        with act.Fori(0, L // UN) as i:
                            for k in range(UN):
                                step(sweep * L + i * UN + k, k, at(y, i * UN + k), more_summed, more_stepped)

            @block.vector
            def _(dve):
                def starts(shifted, count, started):
                    dve.wait_ge(shifted, count)
                    nc.vector.tensor_copy(y0[:, 1:HALF], y[:, L - 1, 0:HALF - 1]).then_inc(started, 1)
                    nc.vector.tensor_copy(y0[:, 0:1], pe_end[:, 0:1]).then_inc(started, 1)
                starts(shifted, 1, started)
                dve.wait_ge(stepped, L + HEAD)
                nc.vector.tensor_tensor(diff[:, :], yh[:, HEAD - 1, :], y[:, HEAD - 1, :],
                                        ALU.subtract).then_inc(compared, 1)
                dve.wait_ge(compared, 1)
                nc.vector.tensor_reduce(out=worst[:, :], in_=diff[:, :], axis=AX.X, op=ALU.max,
                                        apply_absolute_value=True).then_inc(compared, 1)
                nc.vector.tensor_copy(y[:, 0:HEAD, :], yh[:, :, :]).then_inc(compared, 1)
                dve.wait_ge(worst_turned, 1)
                nc.vector.reduce_max(worst1[:, :], pf[0:1, 0:128], AX.X).then_inc(compared, 1)
                dve.wait_ge(compared, 4)
                nc.vector.tensor_scalar(flag[:, :], worst1[:, :], TOL, None, ALU.is_gt).then_inc(flagged, 1)
                dve.wait_ge(flagged, 1)
                unmet = nc.vector.value_load(flag[0:1, 0:1], min_val=0, max_val=1)
                with dve.If(unmet > 0):
                    with dve.Fori(0, CH) as sweep:
                        starts(more_shifted, sweep + 1, more_started)

        with ExitStack() as octx:
            ring = octx.enter_context(nc.sbuf_tensor("rn_ring", [128, 2, GR, Q], F32))
            ps = octx.enter_context(nc.psum_tensor("rn_pso", [128, 2, GR, 2, D], F32))
            sem = lambda s: c.sem("ro_" + s)
            copied, turned, added = sem("copied"), sem("turned"), sem("added")
            block = octx.enter_context(nc.Block())
            groups = NG // 2
            cs = Q // L * GR

            @block.scalar
            def _(act):
                def group(g, k):
                    need(act, turned, g - 1)
                    nc.scalar.copy(ring[:, k, :, :].rearrange("p b (c j) -> p (b c) j", j=L),
                                   y[:, :, bass.ds(g * cs, cs)].rearrange("p j c -> p c j")).then_inc(copied, 1)
                group(0, 0)
                group(1, 1)
                with act.Fori(1, groups // 2) as i:
                    group(2 * i, 0)
                    group(2 * i + 1, 1)

            @block.tensor
            def _(pe):
                def group(g, k):
                    pe.wait_ge(copied, g + 1)
                    need(pe, added, 2 * (g - 1))
                    for j in range(GR):
                        ins = nc.tensor.transpose(ps[:, k, j, :, :].rearrange("p a d -> p (a d)"),
                                                  ring[:, k, j, :], c.ident[:, :])
                    ins.then_inc(turned, 1)
                group(0, 0)
                group(1, 1)
                with pe.Fori(1, groups // 2) as i:
                    group(2 * i, 0)
                    group(2 * i + 1, 1)

            @block.vector
            def _(dve):
                with dve.Fori(0, groups // 2) as i:
                    for k in range(2):
                        g = 2 * i + k
                        dve.wait_ge(turned, g + 1)
                        for half in range(2):
                            rows = c.x[:, bass.ds(g * GR + half * (S // 2), GR), :]
                            nc.vector.tensor_tensor(rows, rows, ps[:, k, :, half, :], ALU.add).then_inc(added, 1)
                dve.wait_ge(added, 2 * groups)


INNER, STATES, RANK, TAPS = 128, 16, 4, 4
TC = 1024
HALF = TC // 2
RING = 4
COPY_RING, DECAY_RING = 8, 4
B_AHEAD, COPY_AHEAD, DECAY_AHEAD = 7, 5, 3
TAKE_FIRST = 23
NC = T // TC
PAD = 4
BCW = 2 * STATES


def state_space_stage(nc, c, W, y_scratch):
    with ExitStack() as ctx:
        def sb(name, shape, dt=F32):
            return ctx.enter_context(nc.sbuf_tensor(name, shape, dt))
        ns = sb("ss_n", [128, T + 2 * PAD])
        k = dict(
            taps=sb("ss_taps", [128, 2, 2, INNER]),
            z=sb("ss_wz", [D, INNER]), bc=sb("ss_wbc", [INNER, 4 * BCW]), dt=sb("ss_wdt", [INNER, INNER]),
            out=sb("ss_wout", [INNER, D]), cb=sb("ss_cb", [INNER, 1]), db=sb("ss_db", [INNER, 1]),
            dd=sb("ss_D", [INNER, 1]), A=sb("ss_A", [INNER, STATES]),
            sel=sb("ss_sel", [128, BCW], BF16))
        stats_stage(nc, c, "ss_s", 1.0, 1e-6)

        with ExitStack() as wctx:
            def wsb(name, shape, dt=F32):
                return wctx.enter_context(nc.sbuf_tensor(name, shape, dt))
            inx, inz = wsb("sw_inx", [INNER, D]), wsb("sw_inz", [INNER, D])
            cw, xw, dtw = wsb("sw_cw", [INNER, TAPS]), wsb("sw_xw", [RANK + BCW, INNER]), wsb("sw_dtw", [RANK, INNER])
            al, ow = wsb("sw_al", [INNER, STATES]), wsb("sw_ow", [D, INNER])
            tp = wsb("sw_tp", [INNER, 2, 2, 2, D])
            ps = wctx.enter_context(nc.psum_tensor("sw_ps", [128, 4, 512], F32))
            sem = lambda s: c.sem("sw_" + s)
            loaded, cleared, scaled, turned, copied, exped = (sem(s) for s in ("loaded", "cleared", "scaled",
                                                                              "turned", "copied", "exped"))
            block = wctx.enter_context(nc.Block())

            @block.sync
            def _(sp):
                n = 0
                with nc.allow_non_contiguous_dma(reason="512 weights"):
                    for dst, src in ((inx[:, :], W["in_w"][0:INNER, :]), (inz[:, :], W["in_w"][INNER:2 * INNER, :]),
                                     (cw[:, :], W["conv_w"]), (k["cb"][:, :], col_of(W["conv_b"])),
                                     (xw[:, :], W["x_w"]), (dtw[:, :], W["dt_w"].rearrange("d r -> r d")),
                                     (k["db"][:, :], col_of(W["dt_b"])), (al[:, :], W["A_log"]),
                                     (k["dd"][:, :], col_of(W["D"])), (ow[:, :], W["out_w"])):
                        sp.dma_start(dst, src).then_inc(loaded, 16)
                        n += 16
                assert n == 160
                sp.wait_ge(loaded, n)

            @block.gpsimd
            def _(pool):
                nc.gpsimd.memset(k["sel"][:, :], 0.0).then_inc(cleared, 1)
                nc.gpsimd.memset(ns[:, 0:PAD + 1], 0.0).then_inc(cleared, 1)
                nc.gpsimd.memset(ns[:, T + PAD:T + 2 * PAD], 0.0).then_inc(cleared, 1)
                pool.wait_ge(cleared, 3)
                for part, at in enumerate((0, 64, 96)):
                    nc.gpsimd.affine_select(out=k["sel"][:, :], in_=k["sel"][:, :], compare_op=ALU.not_equal,
                                            fill=1.0, base=-at, pattern=[[-1, BCW]],
                                            channel_multiplier=1).then_inc(cleared, 1)
                    pool.wait_ge(cleared, 4 + part)

            @block.scalar
            def _(act):
                act.wait_ge(loaded, 160)
                nc.scalar.activation(al[:, :], al[:, :], ACT.Exp).then_inc(exped, 1)

            @block.vector
            def _(dve):
                dve.wait_ge(loaded, 160)
                order = (((3, 2), (1, 0)), ((2, 3), (0, 1)))
                for way in range(2):
                    for pair in range(2):
                        for half in range(2):
                            tap = order[way][pair][half]
                            nc.vector.tensor_scalar(tp[:, way, pair, half, :], inx[:, :], cw[:, tap:tap + 1], None,
                                                    ALU.mult).then_inc(scaled, 1)
                dve.wait_ge(exped, 1)
                nc.vector.tensor_scalar(k["A"][:, :], al[:, :], -1.0, None, ALU.mult).then_inc(copied, 1)
                dve.wait_ge(turned, 1)
                for way in range(2):
                    for pair in range(2):
                        nc.vector.tensor_copy(k["taps"][:, way, pair, :],
                                              ps[:, 0, (2 * way + pair) * 128:(2 * way + pair + 1) * 128]).then_inc(copied, 1)
                nc.vector.tensor_copy(k["z"][:, :], ps[0:D, 1, 0:128]).then_inc(copied, 1)
                nc.vector.tensor_copy(k["out"][:, :], ps[:, 1, 128:128 + D]).then_inc(copied, 1)
                for part in range(4):
                    nc.vector.tensor_copy(k["bc"][:, part * BCW:(part + 1) * BCW],
                                          ps[:, 1, 256 + RANK:256 + RANK + BCW]).then_inc(copied, 1)
                nc.vector.tensor_copy(k["dt"][:, :], ps[:, 2, 0:128]).then_inc(copied, 1)
                dve.wait_ge(copied, 12)

            @block.tensor
            def _(pe):
                pe.wait_ge(scaled, 8)
                for way in range(2):
                    for pair in range(2):
                        nc.tensor.transpose(ps[:, 0, (2 * way + pair) * 128:(2 * way + pair + 1) * 128],
                                            tp[:, way, pair, :, :].rearrange("p a d -> p (a d)"), c.ident[:, :])
                nc.tensor.transpose(ps[0:D, 1, 0:128], inz[:, :], c.ident[:, :])
                nc.tensor.transpose(ps[:, 1, 128:128 + D], ow[:, :], c.ident[0:D, 0:D])
                nc.tensor.transpose(ps[:, 1, 256:256 + RANK + BCW], xw[:, :], c.ident[0:RANK + BCW, 0:RANK + BCW])
                nc.tensor.matmul(ps[:, 2, 0:128], lhsT=xw[0:RANK, :], rhs=dtw[:, :], start=True,
                                 stop=True).then_inc(turned, 1)

        def evacuate(g, ps):
            nc.scalar.copy(ns[0:D, bass.ds(g * GT + PAD, GT)], ps[0:D, :])
            return nc.scalar.copy(ns[D:2 * D, bass.ds(g * GT + PAD + 1, GT)], ps[D:2 * D, :])
        transpose_stage(nc, c, "ss_t", False, evacuate)

        for way in range(2):
            scan_direction(nc, c, ns, k, way, y_scratch)


def scan_direction(nc, c, ns, k, way, y_scratch):
    back = way == 1
    N = "sb_" if back else "sf_"
    U = 2 * STATES
    with ExitStack() as ctx:
        def sb(name, shape, dt=F32):
            return ctx.enter_context(nc.sbuf_tensor(N + name, shape, dt))

        def sem(name):
            return c.sem(N + name)
        xc, dt, dtx = sb("xc", [128, 2, TC]), sb("dt", [128, 2, TC]), sb("dtx", [128, 2, TC])
        bcs = sb("bcs", [128, 2, TC], BF16)
        dbx, h, hc = (sb(s, [128, RING, HALF]) for s in ("dbx", "h", "hc"))
        dA, bb = sb("dA", [128, DECAY_RING, HALF]), sb("bb", [128, COPY_RING, HALF])
        ta, tb, tc = (sb(s, [128, TC]) for s in ("ta", "tb", "tc"))
        rest = ta
        state = sb("state", [128, STATES])
        yo = sb("yo", [128, TC])
        if back:
            zs = sb("zs", [128, TC])
            yf = tb
        bank = lambda name: ctx.enter_context(nc.psum_tensor(N + name, [128, TC], F32))
        p_b, p_c, p_y, p_p = bank("pb"), bank("pc"), bank("py"), bank("pp")
        b_made, b_taken, c_made, exped, injected, scanned, kept, read, summed = (
            sem(s) for s in ("b_made", "b_taken", "c_made", "exped", "injected", "scanned", "kept", "read", "summed"))
        (conv, conv_taken, z_made, z_copied, z_taken, dt_made, relu_made, dt_taken, e_made, log_made, w_made, corr,
         corr2, dt_done, dtx_done, bc_made, bc_hi, bc_rest, bc_mid, bc_low, y_taken, y_joined, y_gated, projected,
         x_done, y_stored, y_loaded, zeroed) = (
            sem(s) for s in ("conv", "conv_t", "z", "z_c", "z_t", "dt", "relu", "dt_t", "e", "log", "w", "corr", "corr2",
                             "dt_d", "dtx", "bc", "bc_hi", "bc_rest", "bc_mid", "bc_low", "y_t", "y_j", "y_g",
                             "proj", "x_d", "y_st", "y_ld", "zero"))
        block = ctx.enter_context(nc.Block())
        halves = [slice(0, HALF), slice(HALF, TC)]

        def cols(s):
            return halves[(s // STATES) ^ way]

        def ahead(n, par, s, steps):
            return (n, par, s + steps) if s + steps < U else (n + 1, 1 - par, s + steps - U)

        def base(n):
            return n * -TC + (NC - 1) * TC if back else n * TC

        def run(eng, unit, prepare=(), tail=(), own=()):
            def chunk(n, par, first=False, last=False):
                for s in range(U):
                    unit(n, par, s, first, last)
                    for at, step in prepare:
                        if at == s and not last:
                            step(n + 1, 1 - par)
                    for at, step in tail:
                        if at == s and not first:
                            step(n - 1, 1 - par, last)
                    for at, step in own:
                        if at == s:
                            step(n, last)
            for _, step in prepare:
                step(0, 0)
            chunk(0, 0, first=True)
            chunk(1, 1)
            with eng.Fori(1, NC // 2 - 1) as i:
                chunk(2 * i, 0)
                chunk(2 * i + 1, 1)
            chunk(NC - 2, 0)
            chunk(NC - 1, 1, last=True)

        @block.tensor
        def _(pe):
            def gate_in(hf):
                def step(m, last):
                    need(pe, x_done, m)
                    pe.wait_ge(bc_rest, NC if last else m + 2)
                    ins = nc.tensor.matmul(p_p[:, hf], lhsT=k["z"][:, :],
                                           rhs=ns[0:D, bass.ds(base(m) + PAD + hf.start, HALF)], start=True, stop=True)
                    if hf.start:
                        ins.then_inc(z_made, 1)
                return step

            def convolve(hf):
                def step(m, par):
                    need(pe, bc_rest, m)
                    if back:
                        need(pe, z_copied, m - 1)
                    for pair, off in enumerate((1, 3) if back else (0, -2)):
                        ins = nc.tensor.matmul(p_p[:, hf], lhsT=k["taps"][:, way, pair, :],
                                               rhs=ns[:, bass.ds(base(m) + PAD + off + hf.start, HALF)],
                                               start=(pair == 0), stop=(pair == 1))
                    if hf.start:
                        ins.then_inc(conv, 1)
                return step

            def step_size(hf):
                def step(m, par):
                    pe.wait_ge(conv_taken, m + 1)
                    ins = nc.tensor.matmul(p_p[:, hf], lhsT=k["dt"][:, :], rhs=xc[:, par, hf], start=True, stop=True)
                    if hf.start:
                        ins.then_inc(dt_made, 1)
                return step

            def in_out(hf):
                def step(m, par):
                    pe.wait_ge(dt_taken, m + 1)
                    ins = nc.tensor.matmul(p_p[:, hf], lhsT=k["bc"][:, :], rhs=xc[:, par, hf], start=True, stop=True)
                    if hf.start:
                        ins.then_inc(bc_made, 1)
                return step

            def spread(bank, row, s, par, b):
                return nc.tensor.matmul(bank[:, halves[b]], lhsT=k["sel"][:, row:row + 1].to_broadcast([128, 128]), rhs=bcs[:, par, cols(s)],
                                        start=True, stop=True)

            def spread_b(u, n, par, s):
                if s == 0:
                    pe.wait_ge(bc_low, n + 1)
                need(pe, b_taken, u - 1)
                spread(p_b, s % STATES, s, par, s % 2).then_inc(b_made, 1)

            def spread_c(u, n, par, s):
                need(pe, read, u - 1)
                spread(p_c, STATES + s % STATES, s, par, s % 2).then_inc(c_made, 1)

            def total(u, s, n):
                pe.wait_ge(read, u + 1)
                if s % STATES == 0:
                    need(pe, y_taken, 2 * n - 1 + s // STATES)
                nc.tensor.matmul(p_y[:, cols(s)], lhsT=c.ident[:, :], rhs=hc[:, s % RING, :],
                                 start=(s % STATES == 0), stop=(s % STATES == STATES - 1)).then_inc(summed, 1)

            def project(m, par, last):
                pe.wait_ge(y_gated, m + 1)
                pe.wait_ge(bc_rest, NC if last else m + 3)
                need(pe, x_done, m)
                for j in range(TC // Q):
                    ins = nc.tensor.matmul(p_p[:, j * D:(j + 1) * D], lhsT=yo[:, j * Q:(j + 1) * Q],
                                           rhs=k["out"][:, :], start=True, stop=True)
                ins.then_inc(projected, 1)

            def unit(n, par, s, first, last):
                u = n * U + s
                if first and s == 0:
                    for j in range(B_AHEAD):
                        spread_b(j, 0, par, j)
                    spread_c(0, 0, par, 0)
                if not (last and s >= U - B_AHEAD):
                    spread_b(u + B_AHEAD, *ahead(n, par, s, B_AHEAD))
                if not (first and s < 2):
                    total(u - 2, (s - 2) % U, n if s >= 2 else n - 1)
                if not (last and s == U - 1):
                    spread_c(u + 1, *ahead(n, par, s, 1))

            a, b = halves
            prepare = [(0, convolve(a)), (2, convolve(b)), (7, step_size(a)), (8, step_size(b)),
                       (14, in_out(a)), (15, in_out(b))]
            if back:
                run(pe, unit, prepare, [(20, project)], [(24, gate_in(a)), (25, gate_in(b))])
            else:
                run(pe, unit, prepare)
            total(NC * U - 2, U - 2, NC - 1)
            total(NC * U - 1, U - 1, NC - 1)
            if back:
                project(NC - 1, 1, True)

        @block.scalar
        def _(act):
            def take_z(m, last):
                act.wait_ge(z_made, m + 1)
                need(act, y_gated, m)
                nc.scalar.copy(zs[:, :], p_p[:, :]).then_inc(z_copied, 1)

            def silu_x(m, par):
                act.wait_ge(conv, m + 1)
                need(act, y_taken, 2 * m - 2)
                need(act, dtx_done, 2 * m - 2)
                nc.scalar.activation(xc[:, par, :], p_p[:, :], ACT.Silu, bias=k["cb"][:, :]).then_inc(conv_taken, 1)

            def silu_z(m, par, last):
                act.wait_ge(z_copied, m + 1)
                nc.scalar.activation(zs[:, :], zs[:, :], ACT.Silu).then_inc(z_taken, 1)

            def exp_log_tables(*_):
                nc.scalar.preload_act_table_set("natural_log_exp_and_others")

            def softplus_relu(m, par):
                act.wait_ge(dt_made, m + 1)
                need(act, exped, U * (m - 1))
                nc.scalar.activation(dt[:, par, :], p_p[:, :], ACT.Relu, bias=k["db"][:, :]).then_inc(relu_made, 1)

            def softplus_abs(m, par):
                need(act, bc_low, m)
                need(act, bc_mid, m)
                nc.scalar.activation(ta[:, :], p_p[:, :], ACT.Abs, bias=k["db"][:, :]).then_inc(dt_taken, 1)

            def softplus_exp(m, par):
                act.wait_ge(dt_taken, m + 1)
                nc.scalar.activation(ta[:, :], ta[:, :], ACT.Exp, scale=-1.0).then_inc(e_made, 1)

            def softplus_log(m, par):
                act.wait_ge(e_made, m + 1)
                need(act, corr2, 2 * m)
                if back:
                    need(act, y_joined, m - 1)
                nc.scalar.activation(tb[:, :], ta[:, :], ACT.Ln, bias=c.one[:, :]).then_inc(log_made, 1)

            def bc_high(m, par):
                act.wait_ge(bc_made, m + 1)
                need(act, c_made, U * (m - 1))
                nc.scalar.copy(bcs[:, par, :], p_p[:, :]).then_inc(bc_hi, 1)

            def bc_middle(m, par):
                act.wait_ge(bc_rest, m + 1)
                nc.scalar.copy(bcs[64:128, par, :], rest[64:128, :]).then_inc(bc_mid, 1)

            def copy_b(u, s):
                act.wait_ge(b_made, u + 1)
                need(act, injected, u + 1 - COPY_RING)
                nc.scalar.copy(bb[:, s % COPY_RING, :], p_b[:, halves[s % 2]]).then_inc(b_taken, 1)

            def decay(u, n, par, s):
                if s == 0:
                    act.wait_ge(dt_done, n + 1)
                need(act, scanned, u + 1 - DECAY_RING)
                q = s % STATES
                nc.scalar.activation(dA[:, s % DECAY_RING, :], dt[:, par, cols(s)], ACT.Exp,
                                     scale=k["A"][:, q:q + 1]).then_inc(exped, 1)

            def keep(u, s):
                act.wait_ge(scanned, u + 1)
                q, e = s % STATES, 0 if back else HALF - 1
                nc.scalar.copy(state[:, q:q + 1], h[:, s % RING, e:e + 1]).then_inc(kept, 1)

            def unit(n, par, s, first, last):
                u = n * U + s
                if first and s == 0:
                    for j in range(COPY_AHEAD):
                        copy_b(j, j)
                    for j in range(DECAY_AHEAD):
                        decay(j, 0, par, j)
                if not (last and s >= U - COPY_AHEAD):
                    copy_b(u + COPY_AHEAD, s + COPY_AHEAD)
                if not (last and s >= U - DECAY_AHEAD):
                    decay(u + DECAY_AHEAD, *ahead(n, par, s, DECAY_AHEAD))
                if not (first and s < 2):
                    keep(u - 2, s - 2)

            act.wait_ge(zeroed, 1)
            prepare = [(4, silu_x), (11, softplus_relu), (12, softplus_abs), (13, softplus_exp),
                       (14, softplus_log), (17, bc_high), (19, bc_middle)]
            exp_log_tables()
            if back:
                run(act, unit, prepare, [(4, silu_z)], [(4, exp_log_tables), (27, take_z)])
                silu_z(NC - 1, 1, True)
            else:
                run(act, unit, prepare[:1] + [(4, exp_log_tables)] + prepare[1:])

        @block.gpsimd
        def _(pool):
            def correct(hf):
                def step(m, par):
                    pool.wait_ge(w_made, m + 1)
                    nc.gpsimd.tensor_tensor(tc[:, hf], ta[:, hf], tc[:, hf], ALU.subtract).then_inc(corr, 1)
                return step

            def correct2(hf):
                def step(m, par):
                    pool.wait_ge(corr, 2 * m + 2)
                    pool.wait_ge(log_made, m + 1)
                    nc.gpsimd.tensor_tensor(tc[:, hf], tc[:, hf], tb[:, hf], ALU.add).then_inc(corr2, 1)
                return step

            def dt_x(hf):
                def step(m, par):
                    pool.wait_ge(dt_done, m + 1)
                    need(pool, injected, U * (m - 1))
                    nc.gpsimd.tensor_tensor(dtx[:, par, hf], dt[:, par, hf], xc[:, par, hf], ALU.mult).then_inc(dtx_done, 1)
                return step

            def join(m, par, last):
                pool.wait_ge(y_taken, 2 * m + 2)
                pool.wait_ge(y_loaded, 16 * (m + 1))
                nc.gpsimd.tensor_tensor(yo[:, :], yo[:, :], yf[:, :], ALU.add).then_inc(y_joined, 1)

            def unit(n, par, s, first, last):
                u, b = n * U + s, s % RING
                if s == 0:
                    pool.wait_ge(dtx_done, 2 * n + 2)
                pool.wait_ge(b_taken, u + 1)
                need(pool, scanned, u + 1 - RING)
                nc.gpsimd.tensor_tensor(dbx[:, b, :], dtx[:, par, cols(s)], bb[:, s % COPY_RING, :], ALU.mult).then_inc(injected, 1)

            nc.gpsimd.memset(state[:, :], 0.0).then_inc(zeroed, 1)
            run(pool, unit, [(16, correct(halves[0])), (17, correct(halves[1])), (19, correct2(halves[0])),
                             (20, correct2(halves[1])), (26, dt_x(halves[0])), (27, dt_x(halves[1]))],
                [(5, join)] if back else [])
            if back:
                join(NC - 1, 1, True)

        @block.vector
        def _(dve):
            def one_plus(m, par):
                dve.wait_ge(e_made, m + 1)
                need(dve, dt_done, m)
                nc.vector.tensor_scalar(tc[:, :], ta[:, :], 1.0, 1.0, ALU.add, ALU.subtract).then_inc(w_made, 1)

            def step_sum(m, par):
                dve.wait_ge(corr2, 2 * m + 2)
                dve.wait_ge(relu_made, m + 1)
                nc.vector.tensor_tensor(dt[:, par, :], dt[:, par, :], tc[:, :], ALU.add).then_inc(dt_done, 1)

            def bc_remainder(m, par):
                dve.wait_ge(bc_hi, m + 1)
                dve.wait_ge(corr, 2 * m + 2)
                dve.wait_ge(log_made, m + 1)
                nc.vector.tensor_tensor(rest[:, :], p_p[:, :], bcs[:, par, :], ALU.subtract).then_inc(bc_rest, 1)

            def bc_lowest(m, par):
                dve.wait_ge(bc_mid, m + 1)
                dve.wait_ge(bc_rest, m + 1)
                nc.vector.tensor_tensor(bcs[96:128, par, :], rest[96:128, :], bcs[96:128, par, :],
                                        ALU.subtract).then_inc(bc_low, 1)

            def take_y(m, par, half):
                dve.wait_ge(summed, U * m + (half + 1) * STATES)
                if half == 0 and back:
                    need(dve, projected, m)
                elif half == 0:
                    need(dve, y_stored, 16 * m)
                at = halves[half ^ way]
                nc.vector.scalar_tensor_tensor(out=yo[:, at], in0=xc[:, par, at], scalar=k["dd"][:, :], in1=p_y[:, at],
                                               op0=ALU.mult, op1=ALU.add).then_inc(y_taken, 1)

            def take_second(m, par, last):
                take_y(m, par, 1)

            def gate(m, par, last):
                dve.wait_ge(y_joined, m + 1)
                dve.wait_ge(z_taken, m + 1)
                nc.vector.tensor_tensor(yo[:, :], yo[:, :], zs[:, :], ALU.mult).then_inc(y_gated, 1)

            def add_x(m, par, last):
                dve.wait_ge(projected, m + 1)
                rows = TC // Q
                xr = c.x[:, bass.ds(m * -rows + (NC - 1) * rows, rows), :]
                nc.vector.tensor_tensor(xr, xr, p_p[:, 0:rows * D].rearrange("p (r d) -> p r d", d=D),
                                        ALU.add).then_inc(x_done, 1)

            def read_c(u, s):
                b = s % RING
                dve.wait_ge(scanned, u + 1)
                dve.wait_ge(c_made, u + 1)
                need(dve, summed, u + 1 - RING)
                nc.vector.tensor_tensor(hc[:, b, :], h[:, b, :], p_c[:, halves[s % 2]], ALU.mult).then_inc(read, 1)

            def unit(n, par, s, first, last):
                u, b, q = n * U + s, s % RING, s % STATES
                dve.wait_ge(exped, u + 1)
                dve.wait_ge(injected, u + 1)
                need(dve, kept, u + 1 - RING)
                need(dve, read, u + 1 - RING)
                flow = lambda t, slot=b: t[:, slot, ::-1] if back else t[:, slot, :]
                nc.vector.tensor_tensor_scan(out=flow(h), data0=flow(dA, s % DECAY_RING),
                                             data1=flow(dbx), initial=state[:, q:q + 1],
                                             op0=ALU.mult, op1=ALU.add).then_inc(scanned, 1)
                if not (first and s == 0):
                    read_c(u - 1, s - 1 if s else U - 1)
                if s == TAKE_FIRST:
                    take_y(n, par, 0)

            dve.wait_ge(zeroed, 1)
            run(dve, unit, [(15, one_plus), (18, bc_remainder), (20, bc_lowest), (21, step_sum)],
                [(3, take_second), (8, gate), (22, add_x)] if back else [(3, take_second)])
            read_c(NC * U - 1, U - 1)
            take_y(NC - 1, 1, 1)
            if back:
                gate(NC - 1, 1, True)
                add_x(NC - 1, 1, True)

        @block.sync
        def _(sp):
            if back:
                def load(n, last=False):
                    sp.wait_ge(corr2, 2 * NC if last else 2 * n + 4)
                    need(sp, y_joined, n)
                    sp.dma_start(yf[:, :], y_scratch[:, bass.ds(base(n), TC)]).then_inc(y_loaded, 16)
                load(0)
                with sp.Fori(1, NC - 1) as n:
                    load(n)
                load(NC - 1, True)
            else:
                with sp.Fori(0, NC) as n:
                    sp.wait_ge(y_taken, 2 * n + 2)
                    sp.dma_start(y_scratch[:, bass.ds(base(n), TC)], yo[:, :]).then_inc(y_stored, 16)
                sp.wait_ge(y_stored, 16 * NC)


EXPERTS = 8


def experts_stage(nc, c, W, out):
    with ExitStack() as ctx:
        def sb(name, shape, dt=F32):
            return ctx.enter_context(nc.sbuf_tensor(name, shape, dt))
        xT = sb("ex_xT", [D + 1, T])
        wr = sb("ex_wr", [D + 1, EXPERTS])
        we = sb("ex_we", [D + 1, EXPERTS, D])
        wt = sb("ex_wt", [Q, S, EXPERTS])
        xg = sb("ex_xg", [D + 1, 2, GT])
        stats_stage(nc, c, "ex_s", 1.0, 1e-5)

        with ExitStack() as wctx:
            loaded = c.sem("ew_loaded")
            set_ = c.sem("ew_set")
            block = wctx.enter_context(nc.Block())

            @block.sync
            def _(sp):
                sp.dma_start(wr[0:D, :], W["router_w"]).then_inc(loaded, 16)
                sp.dma_start(wr[D:D + 1, :], row_of(W["router_b"])).then_inc(loaded, 16)
                sp.dma_start(we[0:D, :, :], W["expert_w"].rearrange("e d c -> d e c")).then_inc(loaded, 16)
                sp.dma_start(we[D:D + 1, :, :], W["expert_b"].rearrange("(a e) c -> a e c", a=1)).then_inc(loaded, 16)
                sp.wait_ge(loaded, 64)

            @block.gpsimd
            def _(pool):
                nc.gpsimd.memset(xT[D:D + 1, :], 1.0).then_inc(set_, 1)
                pool.wait_ge(set_, 1)

        def evacuate(g, ps):
            return nc.scalar.copy(xT[0:D, bass.ds(g * GT, GT)], ps[0:D, :])
        transpose_stage(nc, c, "ex_t", False, evacuate)

        def loads(sp, used, sems):
            def load(g, k):
                need(sp, used, GR * (g - 1))
                sp.dma_start(xg[:, k, :], xT[:, bass.ds(g * GT, GT)]).then_inc(sems[k], 16)
            load(0, 0)
            load(1, 1)
            with sp.Fori(1, NG // 2) as i:
                load(2 * i, 0)
                load(2 * i + 1, 1)

        with ExitStack() as rctx:
            def rsb(name, shape):
                return rctx.enter_context(nc.sbuf_tensor(name, shape, F32))
            p, e, eq = rsb("er_p", [Q, S, EXPERTS]), rsb("er_e", [Q, S, EXPERTS]), rsb("er_eq", [Q, S, EXPERTS])
            top = rsb("er_top", [Q, 2, S])
            key, tot = rsb("er_key", [Q, S]), rsb("er_tot", [Q, S])
            rank = rsb("er_rank", [Q, EXPERTS])
            ps = rctx.enter_context(nc.psum_tensor("er_ps", [Q, S, EXPERTS], F32))
            sem = lambda n: c.sem("er_" + n)
            routed, ranked, steps, shifted, exped = (sem(n) for n in ("routed", "ranked", "steps", "shifted", "exped"))
            loaded = [sem("loaded0"), sem("loaded1")]
            block = rctx.enter_context(nc.Block())
            wide = lambda t: t.rearrange("p (s a) -> p s a", a=1).to_broadcast([Q, S, EXPERTS])

            @block.sync
            def _(sp):
                loads(sp, routed, loaded)

            @block.tensor
            def _(pe):
                with pe.Fori(0, NG // 2) as i:
                    for k in range(2):
                        pe.wait_ge(loaded[k], 16 * (i + 1))
                        for j in range(GR):
                            nc.tensor.matmul(ps[:, bass.ds((2 * i + k) * GR + j, 1), :].rearrange("p a e -> p (a e)"),
                                             lhsT=xg[:, k, j * Q:(j + 1) * Q], rhs=wr[:, :],
                                             start=True, stop=True).then_inc(routed, 1)

            @block.gpsimd
            def _(pool):
                for j in range(EXPERTS):
                    nc.gpsimd.memset(rank[:, j:j + 1], float(EXPERTS - j)).then_inc(ranked, 1)

            @block.scalar
            def _(act):
                act.wait_ge(shifted, 1)
                nc.scalar.activation(e[:, :, :], p[:, :, :], ACT.Exp).then_inc(exped, 1)

            @block.vector
            def _(dve):
                chain = Chain(dve, steps)
                dve.wait_ge(routed, S)
                chain(nc.vector.reduce_max(key[:, :], ps[:, :, :], AX.X))
                nc.vector.tensor_tensor(p[:, :, :], ps[:, :, :], wide(key[:, :]), ALU.subtract).then_inc(shifted, 1)
                dve.wait_ge(exped, 1)
                chain(nc.vector.reduce_sum(tot[:, :], e[:, :, :], AX.X))
                chain(nc.vector.reciprocal(tot[:, :], tot[:, :]))
                chain(nc.vector.tensor_tensor(p[:, :, :], e[:, :, :], wide(tot[:, :]), ALU.mult))
                dve.wait_ge(ranked, EXPERTS)
                ranks = rank[:, :].rearrange("p (a e) -> p a e", a=1).to_broadcast([Q, S, EXPERTS])
                for choice, pick in ((0, e), (1, wt)):
                    chain(nc.vector.reduce_max(top[:, choice, :], p[:, :, :], AX.X))
                    chain(nc.vector.tensor_tensor(eq[:, :, :], p[:, :, :], wide(top[:, choice, :]), ALU.is_equal))
                    chain(nc.vector.tensor_tensor(eq[:, :, :], eq[:, :, :], ranks, ALU.mult))
                    chain(nc.vector.reduce_max(key[:, :], eq[:, :, :], AX.X))
                    chain(nc.vector.tensor_tensor(pick[:, :, :], eq[:, :, :], wide(key[:, :]), ALU.is_equal))
                    if choice == 0:
                        chain(nc.vector.scalar_tensor_tensor(out=p[:, :, :], in0=e[:, :, :], scalar=-2.0,
                                                             in1=p[:, :, :], op0=ALU.mult, op1=ALU.add))
                chain(nc.vector.tensor_tensor(tot[:, :], top[:, 0, :], top[:, 1, :], ALU.add))
                chain(nc.vector.reciprocal(tot[:, :], tot[:, :]))
                for choice, pick in ((0, e), (1, wt)):
                    chain(nc.vector.tensor_tensor(top[:, choice, :], top[:, choice, :], tot[:, :], ALU.mult))
                    chain(nc.vector.tensor_tensor(pick[:, :, :], pick[:, :, :], wide(top[:, choice, :]), ALU.mult))
                chain(nc.vector.tensor_tensor(wt[:, :, :], wt[:, :, :], e[:, :, :], ALU.add))

        with ExitStack() as ectx:
            hw = ectx.enter_context(nc.sbuf_tensor("ee_hw", [Q, 2, EXPERTS + 1, D], F32))
            ps = ectx.enter_context(nc.psum_tensor("ee_ps", [Q, GR, EXPERTS, D], F32))
            sem = lambda n: c.sem("ee_" + n)
            made, weighed, carried, summed, stored = (sem(n) for n in ("made", "weighed", "carried", "summed", "stored"))
            loaded = [sem("loaded0"), sem("loaded1")]
            block = ectx.enter_context(nc.Block())
            ov = out.rearrange("b s q d -> q (b s) d")

            @block.sync
            def _(sp):
                loads(sp, made, loaded)

            @block.tensor
            def _(pe):
                def group(g, k, i):
                    pe.wait_ge(loaded[k], 16 * (i + 1))
                    for j in range(GR):
                        need(pe, weighed, g * GR + j - GR + 1)
                        nc.tensor.matmul(ps[:, j, :, :], lhsT=xg[:, k, j * Q:(j + 1) * Q], rhs=we[:, :, :],
                                         start=True, stop=True).then_inc(made, 1)
                group(0, 0, 0)
                group(1, 1, 0)
                with pe.Fori(1, NG // 2) as i:
                    group(2 * i, 0, i)
                    group(2 * i + 1, 1, i)

            @block.scalar
            def _(act):
                def row(r, b):
                    need(act, summed, r - 1)
                    nc.scalar.copy(hw[:, b, EXPERTS:EXPERTS + 1, :], c.x[:, bass.ds(r, 1), :]).then_inc(carried, 1)
                row(0, 0)
                row(1, 1)
                with act.Fori(1, S // 2) as i:
                    row(2 * i, 0)
                    row(2 * i + 1, 1)

            @block.vector
            def _(dve):
                def weigh(r, j):
                    dve.wait_ge(made, r + 1)
                    need(dve, summed, r - 1)
                    nc.vector.tensor_tensor(
                        hw[:, j % 2, 0:EXPERTS, :], ps[:, j, :, :],
                        wt[:, bass.ds(r, 1), :].rearrange("p a (e b) -> p (a e) b", b=1).to_broadcast([Q, EXPERTS, D]),
                        ALU.mult).then_inc(weighed, 1)

                def add(r, j):
                    dve.wait_ge(weighed, r + 1)
                    dve.wait_ge(carried, r + 1)
                    nc.vector.tensor_reduce(out=c.x[:, bass.ds(r, 1), :].rearrange("p a d -> p (a d)"),
                                            in_=hw[:, j % 2, :, :].rearrange("p e d -> p d e"), axis=AX.X,
                                            op=ALU.add).then_inc(summed, 1)
                weigh(0, 0)
                for j in range(1, GR):
                    weigh(j, j)
                    add(j - 1, j - 1)
                with dve.Fori(1, NG) as g:
                    for j in range(GR):
                        weigh(g * GR + j, j)
                        add(g * GR + j - 1, (j - 1) % GR)
                add(S - 1, GR - 1)

            @block.gpsimd
            def _(pool):
                with pool.Fori(0, NG) as g:
                    pool.wait_ge(summed, GR * (g + 1))
                    nc.gpsimd.dma_start(ov[:, bass.ds(g * GR, GR), :], c.x[:, bass.ds(g * GR, GR), :]).then_inc(stored, 16)
                pool.wait_ge(stored, 16 * NG)


def build(nc, I, out, stages=(0, 1, 2, 3)):
    pair = nc.dram_tensor("pair_scratch", (HEADS, T), F32, kind="Internal").ap()
    with ExitStack() as ctx:
        c = Core(nc, ctx)
        load_stage(nc, c, I["x"])
        if 0 in stages:
            A = {n: I["L0_conv_" + n] for n in ("mask", "gamma", "beta", "Wq", "Wk", "Wv", "Wb", "Wu", "bu", "Wo", "bo")}
            attention_stage(nc, c, A, pair)
            c.clear_semaphores()
        if 1 in stages:
            recurrence_stage(nc, c, *(I["L0_ffn_" + n] for n in ("W", "V", "gamma", "beta")))
            c.clear_semaphores()
        if 2 in stages:
            y = nc.dram_tensor("y_scratch", (INNER, T), F32, kind="Internal").ap()
            W = {n: I["L1_conv_" + n] for n in ("in_w", "conv_w", "conv_b", "x_w", "dt_w", "dt_b", "A_log", "D", "out_w")}
            state_space_stage(nc, c, W, y)
            c.clear_semaphores()
        if 3 in stages:
            experts_stage(nc, c, {n: I["L1_ffn_" + n] for n in ("router_w", "router_b", "expert_w", "expert_b")}, out)
        else:
            store_stage(nc, c, out)


_INS = ['x', 'L0_conv_mask', 'L0_conv_gamma', 'L0_conv_beta', 'L0_conv_Wq', 'L0_conv_Wk', 'L0_conv_Wv', 'L0_conv_Wb',
        'L0_conv_Wu', 'L0_conv_bu', 'L0_conv_Wo', 'L0_conv_bo', 'L0_ffn_W', 'L0_ffn_V', 'L0_ffn_gamma',
        'L0_ffn_beta', 'L1_conv_in_w', 'L1_conv_conv_w', 'L1_conv_conv_b', 'L1_conv_x_w', 'L1_conv_dt_w',
        'L1_conv_dt_b', 'L1_conv_A_log', 'L1_conv_D', 'L1_conv_out_w', 'L1_ffn_router_w', 'L1_ffn_router_b',
        'L1_ffn_expert_w', 'L1_ffn_expert_b']
_OUT = ((1, 128, 128, 64), 'float32')


def kernel(**inputs):
    import numpy as _np
    import concourse.bacc as _bacc
    from concourse import mybir as _mybir
    from concourse.bass_utils import run_bass_kernel_spmd as _run

    nc = _bacc.Bacc("TRN2", target_bir_lowering=False, num_devices=1)
    arrays, aps = {}, {}
    for name in _INS:
        a = _np.ascontiguousarray(inputs[name])
        arrays[f"in_{name}_dram"] = a
        aps[name] = nc.dram_tensor(f"in_{name}_dram", a.shape, _mybir.dt.from_np(a.dtype), kind="ExternalInput").ap()
    shape, dtype = _OUT
    out = nc.dram_tensor("out_0_dram", shape, _mybir.dt.from_np(_np.dtype(dtype)), kind="ExternalOutput").ap()
    build(nc, aps, out)
    r = _run(nc, [arrays], core_ids=[0])
    return r.results[0]["out_0_dram"]
```

```python
import numpy as np
from contextlib import ExitStack
import concourse.bass as bass
from concourse import mybir

F32 = mybir.dt.float32
BF16 = mybir.dt.bfloat16
I32 = mybir.dt.int32
ACT = mybir.ActivationFunctionType
ALU = mybir.AluOpType
AX = mybir.AxisListType

S = 128
Q = 128
D = 64
T = S * Q
GR = 4
GT = GR * Q
NG = S // GR
HEADS, HC = 4, 32
LAG = 6
NEG = 1.0e9


def need(eng, sem, count):
    if not (isinstance(count, int) and count <= 0):
        eng.wait_ge(sem, count)


class Chain:

    def __init__(self, eng, sem):
        self.eng, self.sem, self.n = eng, sem, 0

    def __call__(self, ins):
        self.n += 1
        ins.then_inc(self.sem, 1)
        self.eng.wait_ge(self.sem, self.n)


def row_of(ap):
    return ap.rearrange("(a n) -> a n", a=1)


def col_of(ap):
    return ap.rearrange("(p a) -> p a", a=1)


class Core:

    def __init__(self, nc, ctx):
        self.nc, self.used = nc, []

        def sb(name, shape, dt=F32):
            return ctx.enter_context(nc.sbuf_tensor(name, shape, dt))
        self.x = sb("x_tok", [Q, S, D])
        self.ident = sb("ident", [128, 128])
        self.one = sb("one_col", [128, 1])

    def sem(self, name):
        self.used.append(self.nc.alloc_semaphore(name=name))
        return self.used[-1]

    def clear_semaphores(self):
        self.nc.clear_and_free_semaphores(self.used)
        self.nc.all_engine_barrier()
        self.used = []


def identity_stage(nc, c):
    with ExitStack() as ctx:
        blank = c.sem("id_blank")
        made = c.sem("id_made")
        block = ctx.enter_context(nc.Block())

        @block.gpsimd
        def _(pool):
            nc.gpsimd.memset(c.ident[:, :], 0.0).then_inc(blank, 1)
            nc.gpsimd.memset(c.one[:, :], 1.0).then_inc(made, 1)
            pool.wait_ge(blank, 1)
            nc.gpsimd.affine_select(out=c.ident[:, :], in_=c.ident[:, :], compare_op=ALU.not_equal, fill=1.0,
                                    base=0, pattern=[[-1, 128]], channel_multiplier=1).then_inc(made, 1)
            pool.wait_ge(made, 2)


def norm_stage(nc, c, name, var_scale, var_add, evacuate, halves=1, twice=False, load=None, more_loads=None,
               more_sets=None, before=None, use=None):
    CR, RING = 8, 4
    LAGS = 4 if use is not None else 3
    R = CR // halves
    NCH = S // CR
    GPC = R // GR
    wide = 2 if twice else halves
    with ExitStack() as ctx:
        def sb(n, shape):
            return ctx.enter_context(nc.sbuf_tensor(name + n, shape, F32))
        cen = sb("_cen", [Q, RING, halves, R, D])
        out = sb("_out", [Q, RING, R, 2, D])
        sq = sb("_sq", [Q, 2, CR, D])
        total, squares, std = sb("_sum", [Q, RING, CR]), sb("_squares", [Q, RING, CR]), sb("_std", [Q, RING, CR])
        add = sb("_add", [Q, 1])
        ps = ctx.enter_context(nc.psum_tensor(name + "_ps", [128, RING, GT], F32))
        sem = lambda n: c.sem(name + n)
        summed, centred, squared, spread, rooted, inverted, scaled, turned, taken, set_, more = (
            sem("_" + n) for n in ("summed", "centred", "squared", "spread", "rooted", "inverted", "scaled", "turned",
                                   "taken", "set", "more"))
        loaded = [sem("_loaded%d" % j) for j in range(RING)] if load is not None else None
        block = ctx.enter_context(nc.Block())
        rows = c.x[:, :, :].rearrange("q (a s) d -> q a s d", a=halves)
        part = lambda k: rows[:, :, bass.ds(k * R, R), :]
        each = lambda t: t.rearrange("q (a r b) -> q a r b", a=halves, b=1).to_broadcast([Q, halves, R, D])
        by_half = lambda t: t.rearrange("q (a r) -> q a r", a=halves)
        shaped = lambda t: t.rearrange("q (a r) d -> q a r d", a=halves)

        def run(eng, step):
            def body(i, has):
                for j in range(RING):
                    step(i, i * RING + j, j, has(j))
            body(0, lambda j: lambda lag: lag <= j)
            body(1, lambda j: lambda lag: lag <= RING + j)
            with eng.Fori(2, NCH // RING) as i:
                body(i, lambda j: lambda lag: True)
            for d in range(LAGS):
                step(None, NCH + d, d, lambda lag: LAGS >= lag > d)

        @block.sync
        def _(sp):
            if load is not None:
                source = load.rearrange("q (a s) d -> q a s d", a=halves)

                def piece(i, j):
                    need(sp, loaded[j], 16 * halves * i)
                    k = i * RING + j
                    for a in range(halves):
                        sp.dma_start(part(k)[:, a, :, :], source[:, a, bass.ds(k * R, R), :]).then_inc(loaded[j], 16)
                for j in range(RING):
                    piece(0, j)
                with sp.Fori(1, NCH // RING) as i:
                    for j in range(RING):
                        piece(i, j)
            if more_loads is not None:
                sp.wait_ge(more, more_loads(sp, more))

        @block.vector
        def _(dve):
            def step(i, k, j, has):
                if has(0):
                    if load is not None:
                        dve.wait_ge(loaded[j], 16 * halves * (i + 1))
                    need(dve, centred, k - RING + 1)
                    nc.vector.reduce_sum(by_half(total[:, j, :]), part(k), AX.X).then_inc(summed, 1)
                if has(2):
                    dve.wait_ge(rooted, k - 1)
                    need(dve, scaled, k - 2 - RING + 1)
                    nc.vector.reciprocal(std[:, (j - 2) % RING, :], std[:, (j - 2) % RING, :]).then_inc(inverted, 1)
                if has(0):
                    dve.wait_ge(summed, k + 1)
                    need(dve, scaled, k - RING + 1)
                    nc.vector.scalar_tensor_tensor(out=cen[:, j, :, :, :], in0=each(total[:, j, :]), scalar=-1.0 / D,
                                                   in1=part(k), op0=ALU.mult, op1=ALU.add).then_inc(centred, 1)
                if has(1):
                    b = (j - 1) % RING
                    dve.wait_ge(squared, k)
                    nc.vector.reduce_sum(squares[:, b, :], sq[:, b % 2, :, :], AX.X).then_inc(spread, 1)
            run(dve, step)

        @block.scalar
        def _(act):
            def step(i, k, j, has):
                if has(0):
                    act.wait_ge(centred, k + 1)
                    need(act, spread, k - 1)
                    nc.scalar.activation(shaped(sq[:, j % 2, :, :]), cen[:, j, :, :, :], ACT.Square).then_inc(squared, 1)
                if has(1):
                    b = (j - 1) % RING
                    act.wait_ge(spread, k)
                    need(act, scaled, k - RING)
                    nc.scalar.activation(std[:, b, :], squares[:, b, :], ACT.Sqrt, bias=add[:, :],
                                         scale=var_scale / D).then_inc(rooted, 1)
                if has(3):
                    for b in range(GPC):
                        g = (k - 3) * GPC + b
                        act.wait_ge(turned, g + 1)
                        slot = ((j - 3) * GPC + b) % RING
                        evacuate(*((g, ps[:, slot, :]) if use is None else (g, ps[:, slot, :], slot))).then_inc(taken, 1)
            act.wait_ge(set_, 1)
            run(act, step)

        @block.gpsimd
        def _(pool):
            def step(i, k, j, has):
                if has(2):
                    b = (j - 2) % RING
                    pool.wait_ge(inverted, k - 1)
                    pool.wait_ge(squared, k - 1)
                    need(pool, turned, GPC * (k - 2 - RING + 1))
                    shape = [Q, R, wide, D]
                    rstd = std[:, b, :].rearrange("q (a r z) -> q r a z", a=halves, z=1).to_broadcast(shape)
                    src = cen[:, b, :, :, :].rearrange("q a r d -> q r a d")
                    nc.gpsimd.tensor_tensor(out[:, b, :, 0:wide, :], src.to_broadcast(shape) if twice else src, rstd,
                                            ALU.mult).then_inc(scaled, 1)
            nc.gpsimd.memset(add[:, :], var_add).then_inc(set_, 1)
            if wide == 1:
                nc.gpsimd.memset(out[:, :, :, 1, :], 0.0).then_inc(set_, 1)
            run(pool, step)
            if more_sets is not None:
                pool.wait_ge(scaled, NCH)
                pool.wait_ge(set_, (2 if wide == 1 else 1) + more_sets(set_))

        @block.tensor
        def _(pe):
            def step(i, k, j, has):
                if has(2):
                    slot = (j - 2) % RING
                    pe.wait_ge(scaled, k - 1)
                    for b in range(GPC):
                        need(pe, taken, (k - 2) * GPC + b - RING + 1)
                        bank = ps[:, ((j - 2) * GPC + b) % RING, :]
                        for r in range(GR):
                            ins = nc.tensor.transpose(bank[:, r * Q:(r + 1) * Q],
                                                      out[:, slot, b * GR + r, :, :].rearrange("q a d -> q (a d)"),
                                                      c.ident[:, :])
                        ins.then_inc(turned, 1)
                if use is not None and has(4):
                    for b in range(GPC):
                        g = (k - 4) * GPC + b
                        pe.wait_ge(taken, g + 1)
                        use(g, (j * GPC + b) % RING)
            if wide == 1:
                pe.wait_ge(set_, 2)
            if before is not None:
                before()
            run(pe, step)


def attention_stage(nc, c, A, x_in):
    with ExitStack() as ctx:
        def sb(name, shape, dt=F32):
            return ctx.enter_context(nc.sbuf_tensor(name, shape, dt))
        xT = sb("at_xT", [D, T])
        xg = sb("at_xg", [128, 4, GT])
        wq, wk = sb("at_wq", [D, 128]), sb("at_wk", [D, 128])
        wvu = sb("at_wvu", [D + 1, 256])
        wb = sb("at_wb", [128, HEADS])
        wo = sb("at_wo", [128, D])
        bo = sb("at_bo", [1, D])
        bo_all = sb("at_bo_all", [128, D])
        ones = sb("at_ones", [1, 128])
        gamma, beta = sb("at_gamma", [D, 1]), sb("at_beta", [D, 1])
        mask, maskT = sb("at_mask", [128, 128]), sb("at_maskT", [128, 128])
        bias = sb("at_bias", [128, HEADS, 128])

        def load_weights(sp, loaded):
            n = 0
            for dst, src in ((wq[:, :], A["Wq"]), (wk[:, :], A["Wk"]), (wvu[0:D, 0:128], A["Wv"]),
                             (wvu[0:D, 128:256], A["Wu"]), (wvu[D:D + 1, 128:256], row_of(A["bu"])),
                             (wo[:, :], A["Wo"]), (bo[:, :], row_of(A["bo"])),
                             (mask[:, :], A["mask"].rearrange("n s q -> (n s) q"))):
                sp.dma_start(dst, src).then_inc(loaded, 16)
                n += 16
            return n

        def set_constants(done):
            nc.gpsimd.memset(wvu[D:D + 1, 0:128], 0.0).then_inc(done, 1)
            nc.gpsimd.memset(ones[:, :], 1.0).then_inc(done, 1)
            return 2

        with ExitStack() as wctx:
            affine_loaded, padded = c.sem("at_affine"), c.sem("at_padded")
            block = wctx.enter_context(nc.Block())

            @block.sync
            def _(sp):
                sp.dma_start(gamma[:, :], col_of(A["gamma"])).then_inc(affine_loaded, 16)
                sp.dma_start(beta[:, :], col_of(A["beta"])).then_inc(affine_loaded, 16)
                sp.dma_start(wb[0:D, :], A["Wb"]).then_inc(affine_loaded, 16)
                sp.wait_ge(affine_loaded, 48)

            @block.gpsimd
            def _(pool):
                nc.gpsimd.memset(wb[D:128, :], 0.0).then_inc(padded, 1)
                nc.gpsimd.memset(xg[D:128, :, :], 0.0).then_inc(padded, 1)
                pool.wait_ge(padded, 2)
                nc.gpsimd.memset(xg[D:D + 1, :, :], 1.0).then_inc(padded, 1)
                pool.wait_ge(padded, 3)

        with ExitStack() as bctx:
            pairs = bctx.enter_context(nc.psum_tensor("at_pairs", [Q, S, HEADS], F32))
            paired = c.sem("at_paired")

            def evacuate(g, ps, slot):
                need(nc.scalar, paired, GR * (g - 3))
                nc.scalar.activation(xg[0:D, slot, :], ps[0:D, :], ACT.Identity, bias=beta[:, :], scale=gamma[:, :])
                return nc.scalar.activation(xT[:, bass.ds(g * GT, GT)], ps[0:D, :], ACT.Identity,
                                            bias=beta[:, :], scale=gamma[:, :])

            def pair(g, slot):
                for j in range(GR):
                    nc.tensor.matmul(pairs[:, bass.ds(g * GR + j, 1), :].rearrange("p a e -> p (a e)"),
                                     lhsT=xg[:, slot, j * Q:(j + 1) * Q], rhs=wb[:, :],
                                     start=True, stop=True).then_inc(paired, 1)
            norm_stage(nc, c, "at_n", 1.0 + 1e-5, 1e-5 * 1e-6, evacuate, load=x_in, more_loads=load_weights,
                       more_sets=set_constants, use=pair)

            pb = bctx.enter_context(nc.sbuf_tensor("at_pb", [Q, HEADS, S], F32))
            psb = bctx.enter_context(nc.psum_tensor("at_psb", [128, HEADS, 128], F32))
            pst = bctx.enter_context(nc.psum_tensor("at_pst", [128, 512], F32))
            sem = lambda n: c.sem("ab_" + n)
            copied, masked, turned, mask_turned, done = (sem(n) for n in ("copied", "masked", "turned", "mask_turned", "done"))
            block = bctx.enter_context(nc.Block())

            @block.tensor
            def _(pe):
                nc.tensor.transpose(pst[:, 0:128], mask[:, :], c.ident[:, :])
                nc.tensor.matmul(pst[:, 128:128 + D], lhsT=ones[:, :], rhs=bo[:, :], start=True,
                                 stop=True).then_inc(mask_turned, 1)
                pe.wait_ge(copied, 1)
                for h in range(HEADS):
                    ins = nc.tensor.transpose(psb[:, h, :], pb[:, h, :], c.ident[:, :])
                ins.then_inc(turned, 1)

            @block.scalar
            def _(act):
                act.wait_ge(paired, S)
                nc.scalar.copy(pb[:, :, :], pairs[:, :, :].rearrange("v q h -> v h q")).then_inc(copied, 1)

            @block.vector
            def _(dve):
                dve.wait_ge(mask_turned, 1)
                nc.vector.tensor_copy(maskT[:, :], pst[:, 0:128]).then_inc(done, 1)
                nc.vector.tensor_copy(bo_all[:, :], pst[:, 128:128 + D]).then_inc(done, 1)
                nc.vector.tensor_scalar(mask[:, :], mask[:, :], 1.0, NEG, ALU.subtract, ALU.mult).then_inc(masked, 1)
                nc.vector.tensor_scalar(wo[:, :], wo[:, :], 0.5, None, ALU.mult).then_inc(done, 1)
                dve.wait_ge(masked, 1)
                dve.wait_ge(turned, 1)
                for h in range(HEADS):
                    nc.vector.tensor_tensor(bias[:, h, :], psb[:, h, :], mask[:, :], ALU.add).then_inc(done, 1)
                dve.wait_ge(done, 3 + HEADS)

        attention_rows(nc, c, xT, xg, wq, wk, wvu, wo, bo_all, maskT, bias)


def row_steps(eng, step):
    def group(g, k, pair, has=lambda j: lambda lag: True):
        for j in range(GR):
            step(g * GR + j, j, g, k, has(j), pair)
    group(0, 0, 0, lambda j: lambda lag: lag <= j)
    group(1, 1, 1, lambda j: lambda lag: lag <= GR + j)
    with eng.Fori(1, NG // 2 - 1) as i:
        group(2 * i, 0, i)
        group(2 * i + 1, 1, i + 1)
    group(NG - 2, 0, NG // 2 - 1)
    group(NG - 1, 1, None)
    for d in range(LAG):
        step(S + d, d % GR, None, None, lambda lag: lag > d, None)


def attention_rows(nc, c, xT, xg, wq, wk, wvu, wo, bo_all, maskT, bias):
    with ExitStack() as ctx:
        def sb(name, shape, dt=F32):
            return ctx.enter_context(nc.sbuf_tensor(name, shape, dt))
        kT = sb("ar_kT", [128, 2, GT])
        qd = sb("ar_qd", [128, 2, GR, HEADS, 128])
        va = sb("ar_va", [128, GR, HEADS, HC + 1])
        gate = sb("ar_gate", [128, GR, 128])
        sc = sb("ar_sc", [128, GR, HEADS, 128])
        mx = sb("ar_mx", [128, GR, HEADS])
        ex = sb("ar_ex", [128, 2, HEADS, 128])
        exT = sb("ar_exT", [128, 2, HEADS * 128])
        rs = sb("ar_rs", [128, 2, HEADS])
        og = sb("ar_og", [128, 2, 128])
        og2 = sb("ar_og2", [128, 2, 128])
        ogT = sb("ar_ogT", [128, 2, 128])
        ps_s = ctx.enter_context(nc.psum_tensor("ar_pss", [128, 2, HEADS, 128], F32))
        ps_p = ctx.enter_context(nc.psum_tensor("ar_psp", [128, GT], F32))
        ps_v = ctx.enter_context(nc.psum_tensor("ar_psv", [128, 512], F32))
        ps_t = ctx.enter_context(nc.psum_tensor("ar_pst", [128, 512], F32))
        ps_o = ctx.enter_context(nc.psum_tensor("ar_pso", [128, 512], F32))
        ps_ot = ctx.enter_context(nc.psum_tensor("ar_psot", [128, 512], F32))
        ps_y = ctx.enter_context(nc.psum_tensor("ar_psy", [128, 512], F32))
        o_v = ps_o[:, 0:HEADS * (HC + 1)].rearrange("p (h c) -> p h c", h=HEADS)
        o_t = ps_ot[:, 0:128]
        o_y = ps_y[:, 0:D]
        sem = lambda n: c.sem("ar_" + n)
        g_proj, g_taken = sem("g_proj"), sem("g_taken")
        g_loaded = [sem("g_loaded0"), sem("g_loaded1")]
        (scored, vu_made, v_taken, g_made, added, maxed, shifted, exped, e_turned, e_taken, o_made,
         summed, gated, scaled, o_turned, o_taken, y_made, x_done, biased, ones_set) = (
            sem(n) for n in ("scored", "vu", "v", "g", "added", "maxed", "shifted", "exped", "e_turned", "e_taken",
                             "o", "summed", "gated", "scaled", "o_turned", "o_taken", "y", "x", "biased", "ones"))
        block = ctx.enter_context(nc.Block())
        SCALE = float(HC) ** -0.5

        @block.sync
        def _(sp):
            def load(g, k):
                need(sp, vu_made, GR * (g - 1))
                sp.dma_start(xg[0:D, k, :], xT[:, bass.ds(g * GT, GT)]).then_inc(g_loaded[k], 16)
            load(0, 0)
            load(1, 1)
            with sp.Fori(1, NG // 2) as i:
                g = 2 * i
                load(g, 0)
                load(g + 1, 1)

        @block.tensor
        def _(pe):
            def project(g, k, which, pair):
                pe.wait_ge(g_loaded[k], 16 * (pair + 1))
                need(pe, g_taken, 2 * g + which)
                nc.tensor.matmul(ps_p[:, :], lhsT=(wq, wk)[which][:, :], rhs=xg[0:D, k, :],
                                 start=True, stop=True).then_inc(g_proj, 1)

            def score(r, j, g, k):
                pe.wait_ge(g_taken, 2 * (g + 1))
                need(pe, added, r - 1)
                nc.tensor.matmul(ps_s[:, j % 2, :, :], lhsT=kT[:, k, j * 128:(j + 1) * 128],
                                 rhs=qd[:, k, j, :, :], start=True, stop=True).then_inc(scored, 1)

            def values_gate(r, j, k):
                need(pe, v_taken, r)
                need(pe, g_made, r)
                nc.tensor.matmul(ps_v[:, 0:256], lhsT=xg[0:D + 1, k, j * 128:(j + 1) * 128], rhs=wvu[:, :],
                                 start=True, stop=True).then_inc(vu_made, 1)

            def turn(r, j):
                pe.wait_ge(exped, r + 1)
                need(pe, e_taken, r)
                for h in range(HEADS):
                    ins = nc.tensor.transpose(ps_t[:, h * 128:(h + 1) * 128], ex[:, j % 2, h, :], c.ident[:, :])
                ins.then_inc(e_turned, 1)

            def attend(r, j):
                pe.wait_ge(e_taken, r + 1)
                pe.wait_ge(v_taken, r + 1)
                need(pe, gated, r)
                need(pe, summed, r)
                for h in range(HEADS):
                    ins = nc.tensor.matmul(o_v[:, h, :], lhsT=exT[:, j % 2, h * 128:(h + 1) * 128],
                                           rhs=va[:, j, h, :], start=True, stop=True)
                ins.then_inc(o_made, 1)

            def turn_output(r, j):
                pe.wait_ge(scaled, r + 1)
                need(pe, o_taken, r)
                nc.tensor.transpose(o_t, og2[:, j % 2, :], c.ident[:, :]).then_inc(o_turned, 1)

            def project_output(r, j):
                pe.wait_ge(o_taken, r + 1)
                need(pe, x_done, r)
                nc.tensor.matmul(o_y, lhsT=ogT[:, j % 2, :], rhs=wo[:, :], start=True, stop=True).then_inc(y_made, 1)

            def step(r, j, g, k, has, pair):
                if has(0):
                    score(r, j, g, k)
                if has(2):
                    turn(r - 2, (j - 2) % GR)
                if has(3):
                    attend(r - 3, (j - 3) % GR)
                if has(0):
                    values_gate(r, j, k)
                if has(4):
                    turn_output(r - 4, j)
                if has(5):
                    project_output(r - 5, (j - 5) % GR)
                if pair is not None and j in (1, 2):
                    project(g + 1, 1 - k, j - 1, pair)
            pe.wait_ge(ones_set, 2)
            project(0, 0, 0, 0)
            project(0, 0, 1, 0)
            row_steps(pe, step)

        @block.vector
        def _(dve):
            nc.vector.memset(va[:, :, :, HC:HC + 1], 1.0).then_inc(ones_set, 1)
            nc.vector.memset(qd[:, :, :, :, :], 0.0).then_inc(ones_set, 1)

            def add_bias(r, j):
                dve.wait_ge(scored, r + 1)
                need(dve, exped, r - 3)
                nc.vector.tensor_tensor(sc[:, j, :, :], ps_s[:, j % 2, :, :], bias[:, :, :], ALU.add).then_inc(added, 1)

            def maximum(r, j):
                dve.wait_ge(added, r + 1)
                need(dve, shifted, r - 3)
                nc.vector.reduce_max(mx[:, j, :], sc[:, j, :, :], AX.X).then_inc(maxed, 1)

            def invert_sums(r, j):
                dve.wait_ge(o_made, r + 1)
                need(dve, scaled, r - 1)
                nc.vector.reciprocal(rs[:, j % 2, :], o_v[:, :, HC]).then_inc(summed, 1)

            def apply_gate(r, j):
                dve.wait_ge(g_made, r + 1)
                need(dve, scaled, r - 1)
                nc.vector.scalar_tensor_tensor(
                    out=og[:, j % 2, :].rearrange("p (h c) -> p h c", h=HEADS),
                    in0=gate[:, j, :].rearrange("p (h c) -> p h c", h=HEADS), scalar=1.0, in1=o_v[:, :, 0:HC],
                    op0=ALU.add, op1=ALU.mult).then_inc(gated, 1)

            def normalise(r, j):
                b = j % 2
                dve.wait_ge(gated, r + 1)
                dve.wait_ge(summed, r + 1)
                need(dve, o_turned, r - 1)
                nc.vector.tensor_tensor(og2[:, b, :].rearrange("p (h c) -> p h c", h=HEADS),
                                        og[:, b, :].rearrange("p (h c) -> p h c", h=HEADS),
                                        rs[:, b, :].rearrange("p (h a) -> p h a", a=1).to_broadcast([128, HEADS, HC]),
                                        ALU.mult).then_inc(scaled, 1)

            def add_output_bias(r):
                xr = c.x[:, bass.ds(r, 1), :].rearrange("p a d -> p (a d)")
                nc.vector.scalar_tensor_tensor(out=xr, in0=bo_all[:, :], scalar=maskT[:, bass.ds(r, 1)], in1=xr,
                                               op0=ALU.mult, op1=ALU.add).then_inc(biased, 1)

            def add_to_x(r):
                dve.wait_ge(biased, r + 1)
                dve.wait_ge(y_made, r + 1)
                xr = c.x[:, bass.ds(r, 1), :].rearrange("p a d -> p (a d)")
                nc.vector.scalar_tensor_tensor(out=xr, in0=o_y, scalar=maskT[:, bass.ds(r, 1)], in1=xr,
                                               op0=ALU.mult, op1=ALU.add).then_inc(x_done, 1)

            def step(r, j, g, k, has, pair):
                if has(6):
                    add_to_x(r - 6)
                if has(0):
                    add_bias(r, j)
                if has(3):
                    invert_sums(r - 3, (j - 3) % GR)
                    apply_gate(r - 3, (j - 3) % GR)
                if has(0):
                    maximum(r, j)
                    add_output_bias(r)
                if has(3):
                    normalise(r - 3, (j - 3) % GR)
            row_steps(dve, step)
            dve.wait_ge(x_done, S)

        @block.gpsimd
        def _(pool):
            with pool.Fori(0, NG) as g:
                for j in range(GR):
                    pool.wait_ge(maxed, g * GR + j + 1)
                    nc.gpsimd.tensor_tensor(sc[:, j, :, :], sc[:, j, :, :],
                                            mx[:, j, :].rearrange("p (h a) -> p h a", a=1).to_broadcast([128, HEADS, 128]),
                                            ALU.subtract).then_inc(shifted, 1)

        @block.scalar
        def _(act):
            def take(g, k, which):
                act.wait_ge(g_proj, 2 * g + which + 1)
                need(act, scored, GR * (g - 1))
                if which == 0:
                    for h in range(HEADS):
                        p = slice(HC * h, HC * (h + 1))
                        ins = nc.scalar.activation(qd[p, k, :, h, :], ps_p[p, :].rearrange("p (j v) -> p j v", j=GR),
                                                   ACT.Copy, scale=SCALE)
                else:
                    ins = nc.scalar.copy(kT[:, k, :], ps_p[:, :])
                ins.then_inc(g_taken, 1)

            def values(r, j):
                act.wait_ge(vu_made, r + 1)
                need(act, o_made, r - 3)
                nc.scalar.copy(va[:, j, :, 0:HC], ps_v[:, 0:128].rearrange("p (h c) -> p h c", h=HEADS)).then_inc(v_taken, 1)
                need(act, gated, r - 3)
                nc.scalar.activation(gate[:, j, :], ps_v[:, 128:256], ACT.Tanh, scale=0.5).then_inc(g_made, 1)

            def take_turned(r, j):
                act.wait_ge(e_turned, r + 1)
                need(act, o_made, r - 1)
                nc.scalar.copy(exT[:, j % 2, :], ps_t[:, :]).then_inc(e_taken, 1)

            def take_output(r, j):
                act.wait_ge(o_turned, r + 1)
                need(act, y_made, r - 1)
                nc.scalar.copy(ogT[:, j % 2, :], o_t).then_inc(o_taken, 1)

            def exponentiate(r, j):
                act.wait_ge(shifted, r + 1)
                need(act, e_turned, r - 1)
                nc.scalar.activation(ex[:, j % 2, :, :], sc[:, j, :, :], ACT.Exp).then_inc(exped, 1)

            def step(r, j, g, k, has, pair):
                if has(1):
                    exponentiate(r - 1, (j - 1) % GR)
                if pair is not None and j in (2, 3):
                    take(g + 1, 1 - k, j - 2)
                if has(2):
                    take_turned(r - 2, (j - 2) % GR)
                if has(0):
                    values(r, j)
                if has(4):
                    take_output(r - 4, j)
            act.wait_ge(ones_set, 2)
            take(0, 0, 0)
            take(0, 0, 1)
            row_steps(act, step)


def recurrence_stage(nc, c, W, V, gamma, beta):
    CH, L, HEAD = 512, 32, 16
    HALF = CH // 2
    TOL = 2.0 ** -21
    assert CH * L == T
    with ExitStack() as ctx:
        def sb(name, shape, dt=F32):
            return ctx.enter_context(nc.sbuf_tensor(name, shape, dt))
        n = sb("rn_n", [128, L, HALF])
        y = sb("rn_y", [128, L, HALF])

        def evacuate(g, ps):
            cs = Q // L * GR
            return nc.scalar.copy(n[:, :, bass.ds(g * cs, cs)].rearrange("p j c -> p c j"),
                                  ps.rearrange("p (c j) -> p c j", j=L))
        norm_stage(nc, c, "rn_n", 1.0, 1e-5, evacuate, halves=2)

        wd = sb("rn_wd", [128, 128])
        wT = sb("rn_wT", [128, 128])
        vd, vT = sb("rn_vd", [128, 128]), sb("rn_vT", [128, 128])
        join = sb("rn_join", [128, 128])
        shift = sb("rn_shift", [128, 128])
        gm, bt = sb("rn_gamma", [128, 1]), sb("rn_beta", [128, 1])
        a, cc = sb("rn_a", [128, 1]), sb("rn_c", [128, 1])
        y0 = sb("rn_y0", [128, HALF])
        yh = sb("rn_yh", [128, HEAD, HALF])
        flag = sb("rn_flag", [1, 1], I32)

        with ExitStack() as bctx:
            st = bctx.enter_context(nc.sbuf_tensor("rn_st", [128, 16, 6], F32))
            mv = bctx.enter_context(nc.sbuf_tensor("rn_mv", [128, 2], F32))
            mc = bctx.enter_context(nc.sbuf_tensor("rn_mc", [128, 4], F32))
            ps = bctx.enter_context(nc.psum_tensor("rn_psw", [128, 2, 512], F32))
            pj = bctx.enter_context(nc.psum_tensor("rn_psj", [128, 512], F32))
            pt = bctx.enter_context(nc.psum_tensor("rn_pst", [128, 512], F32))
            sem = lambda s: c.sem("rb_" + s)
            cleared, loaded, turned, copied, made, read, joined, steps, var_ready, std_ready = (
                sem(s) for s in ("cleared", "loaded", "turned", "copied", "made", "read", "joined", "steps",
                                 "var", "std"))
            block = bctx.enter_context(nc.Block())

            @block.gpsimd
            def _(pool):
                for m in (wd, vd, join, shift):
                    nc.gpsimd.memset(m[:, :], 0.0).then_inc(cleared, 1)
                pool.wait_ge(cleared, 4)
                for k, base in enumerate((0, -D, D)):
                    nc.gpsimd.affine_select(out=join[:, :], in_=join[:, :], compare_op=ALU.not_equal, fill=0.5,
                                            base=base, pattern=[[-1, 128]], channel_multiplier=1).then_inc(cleared, 1)
                    pool.wait_ge(cleared, 5 + k)
                nc.gpsimd.affine_select(out=shift[:, :], in_=shift[:, :], compare_op=ALU.not_equal, fill=1.0,
                                        base=D, pattern=[[-1, 128]], channel_multiplier=1).then_inc(cleared, 1)
                pool.wait_ge(cleared, 8)

            @block.sync
            def _(sp):
                sp.wait_ge(cleared, 4)
                k = 0
                for half in (slice(0, D), slice(D, 2 * D)):
                    for dst, src in ((wd[half, half], W), (vd[half, half], V), (gm[half, :], col_of(gamma)),
                                     (bt[half, :], col_of(beta))):
                        sp.dma_start(dst, src).then_inc(loaded, 16)
                        k += 16
                sp.wait_ge(loaded, k)

            @block.tensor
            def _(pe):
                pe.wait_ge(loaded, 128)
                nc.tensor.transpose(pt[:, 0:128], wd[:, :], c.ident[:, :])
                nc.tensor.transpose(pt[:, 128:256], vd[:, :], c.ident[:, :]).then_inc(turned, 1)
                pe.wait_ge(copied, 2)
                nf = n[:, :, :].rearrange("p j c -> p (j c)")
                for k in range(16):
                    need(pe, read, k - 1)
                    nc.tensor.matmul(ps[:, k % 2, :], lhsT=wT[:, :], rhs=nf[:, k * 512:(k + 1) * 512],
                                     start=True, stop=True).then_inc(made, 1)
                pe.wait_ge(steps, 1)
                pe.wait_ge(cleared, 8)
                nc.tensor.matmul(pj[:, 0:1], lhsT=join[:, :], rhs=mv[:, 0:1], start=True, stop=True).then_inc(joined, 1)
                pe.wait_ge(steps, 5)
                nc.tensor.matmul(pj[:, 1:2], lhsT=join[:, :], rhs=mc[:, 2:3], start=True, stop=True).then_inc(joined, 1)
                pe.wait_ge(steps, 7)
                nc.tensor.transpose(pt[:, 0:128], wd[:, :], c.ident[:, :]).then_inc(turned, 1)

            @block.vector
            def _(dve):
                chain = Chain(dve, steps)
                dve.wait_ge(turned, 1)
                nc.vector.tensor_copy(wT[:, :], pt[:, 0:128]).then_inc(copied, 1)
                nc.vector.tensor_copy(vT[:, :], pt[:, 128:256]).then_inc(copied, 1)
                for k in range(16):
                    dve.wait_ge(made, k + 1)
                    nc.vector.bn_stats(st[:, k, :], ps[:, k % 2, :]).then_inc(read, 1)
                dve.wait_ge(read, 16)
                chain(nc.vector.bn_aggr(mv[:, :], st[:, :, :].rearrange("p k s -> p (k s)")))
                dve.wait_ge(joined, 1)
                chain(nc.vector.tensor_copy(mc[:, 0:1], pj[:, 0:1]))
                chain(nc.vector.tensor_tensor(mc[:, 1:2], mv[:, 0:1], mc[:, 0:1], ALU.subtract))
                chain(nc.vector.tensor_tensor(mc[:, 1:2], mc[:, 1:2], mc[:, 1:2], ALU.mult))
                chain(nc.vector.tensor_tensor(mc[:, 2:3], mc[:, 1:2], mv[:, 1:2], ALU.add))
                dve.wait_ge(joined, 2)
                nc.vector.tensor_scalar(mc[:, 3:4], pj[:, 1:2], 1e-5, None, ALU.add).then_inc(var_ready, 1)
                dve.wait_ge(std_ready, 1)
                chain(nc.vector.reciprocal(a[:, :], mc[:, 2:3]))
                dve.wait_ge(loaded, 128)
                chain(nc.vector.tensor_scalar(wd[:, :], wd[:, :], a[:, :], gm[:, :], ALU.mult, ALU.mult))
                chain(nc.vector.tensor_scalar(cc[:, :], mc[:, 0:1], a[:, :], gm[:, :], ALU.mult, ALU.mult))
                chain(nc.vector.tensor_tensor(cc[:, :], bt[:, :], cc[:, :], ALU.subtract))
                dve.wait_ge(turned, 2)
                chain(nc.vector.tensor_copy(wT[:, :], pt[:, 0:128]))

            @block.scalar
            def _(act):
                act.wait_ge(var_ready, 1)
                nc.scalar.activation(mc[:, 2:3], mc[:, 3:4], ACT.Sqrt).then_inc(std_ready, 1)
                act.wait_ge(std_ready, 1)

        with ExitStack() as sctx:
            pu = sctx.enter_context(nc.psum_tensor("rn_psu", [128, 4, 512], F32))
            pe_end = sctx.enter_context(nc.psum_tensor("rn_pse", [128, 512], F32))
            pf = sctx.enter_context(nc.psum_tensor("rn_psf", [128, 512], F32))
            diff = sctx.enter_context(nc.sbuf_tensor("rn_diff", [128, HALF], F32))
            worst = sctx.enter_context(nc.sbuf_tensor("rn_worst", [128, 1], F32))
            worst1 = sctx.enter_context(nc.sbuf_tensor("rn_worst1", [1, 1], F32))
            sem = lambda s: c.sem("rs_" + s)
            summed, stepped, shifted, started, compared, worst_turned, flagged = (
                sem(s) for s in ("summed", "stepped", "shifted", "started", "compared", "turned", "flagged"))
            more_summed, more_stepped, more_shifted, more_started = (
                sem(s) for s in ("more_summed", "more_stepped", "more_shifted", "more_started"))
            block = sctx.enter_context(nc.Block())
            UN = 4

            def drive(pe, slot, j, first=False):
                return nc.tensor.matmul(pu[:, slot, 0:HALF], lhsT=wT[:, :], rhs=at(n, j), start=True, stop=first)

            def at(tile, j):
                return tile[:, j, :] if isinstance(j, int) else tile[:, bass.ds(j, 1), :].rearrange("p a c -> p (a c)")

            @block.tensor
            def _(pe):
                def step(t, slot, before, summed, stepped):
                    if t is not None:
                        pe.wait_ge(stepped, t)
                    nc.tensor.matmul(pu[:, slot, 0:HALF], lhsT=vT[:, :], rhs=before, start=False,
                                     stop=True).then_inc(summed, 1)

                drive(pe, 0, 0, first=True).then_inc(summed, 1)
                drive(pe, 1, 1)
                step(1, 1, at(y, 0), summed, stepped)
                for j in (2, 3):
                    drive(pe, j, j)
                    step(j, j, at(y, j - 1), summed, stepped)
                with pe.Fori(1, L // UN) as i:
                    for k in range(UN):
                        j = i * UN + k
                        drive(pe, k, j)
                        step(j, k, at(y, j - 1), summed, stepped)
                pe.wait_ge(stepped, L)
                nc.tensor.matmul(pe_end[:, 0:1], lhsT=shift[:, :], rhs=y[:, L - 1, HALF - 1:HALF],
                                 start=True, stop=True).then_inc(shifted, 1)
                for j in range(HEAD):
                    drive(pe, j % UN, j)
                    if j == 0:
                        pe.wait_ge(started, 2)
                    step(L + j, j % UN, at(yh, j - 1) if j else y0[:, :], summed, stepped)
                pe.wait_ge(compared, 2)
                nc.tensor.transpose(pf[0:1, 0:128], worst[:, :], c.ident[:, :]).then_inc(worst_turned, 1)
                pe.wait_ge(flagged, 1)
                unmet = nc.tensor.value_load(flag[0:1, 0:1], min_val=0, max_val=1)
                with pe.If(unmet > 0):
                    with pe.Fori(0, CH) as sweep:
                        nc.tensor.matmul(pe_end[:, 0:1], lhsT=shift[:, :], rhs=y[:, L - 1, HALF - 1:HALF],
                                         start=True, stop=True).then_inc(more_shifted, 1)
                        drive(pe, 0, 0)
                        pe.wait_ge(more_started, 2 * sweep + 2)
                        step(None, 0, y0[:, :], more_summed, more_stepped)
                        for j in range(1, UN):
                            drive(pe, j, j)
                            step(sweep * L + j, j, at(y, j - 1), more_summed, more_stepped)
                        with pe.Fori(1, L // UN) as i:
                            for k in range(UN):
                                j = i * UN + k
                                drive(pe, k, j)
                                step(sweep * L + j, k, at(y, j - 1), more_summed, more_stepped)
                        pe.wait_ge(more_stepped, sweep * L + L)

            @block.scalar
            def _(act):
                nc.scalar.preload_act_table_set("sigmoid_and_others")

                def step(t, slot, out, summed, stepped):
                    act.wait_ge(summed, t + 1)
                    nc.scalar.activation(out, pu[:, slot, 0:HALF], ACT.Sigmoid, bias=cc[:, :]).then_inc(stepped, 1)
                with act.Fori(0, L // UN) as i:
                    for k in range(UN):
                        step(i * UN + k, k, at(y, i * UN + k), summed, stepped)
                for j in range(HEAD):
                    step(L + j, j % UN, at(yh, j), summed, stepped)
                act.wait_ge(flagged, 1)
                unmet = nc.scalar.value_load(flag[0:1, 0:1], min_val=0, max_val=1)
                with act.If(unmet > 0):
                    with act.Fori(0, CH) as sweep:
                        act.wait_ge(more_started, 2 * sweep + 2)
                        with act.Fori(0, L // UN) as i:
                            for k in range(UN):
                                step(sweep * L + i * UN + k, k, at(y, i * UN + k), more_summed, more_stepped)

            @block.vector
            def _(dve):
                def starts(shifted, count, started):
                    dve.wait_ge(shifted, count)
                    nc.vector.tensor_copy(y0[:, 1:HALF], y[:, L - 1, 0:HALF - 1]).then_inc(started, 1)
                    nc.vector.tensor_copy(y0[:, 0:1], pe_end[:, 0:1]).then_inc(started, 1)
                starts(shifted, 1, started)
                dve.wait_ge(stepped, L + HEAD)
                nc.vector.tensor_tensor(diff[:, :], yh[:, HEAD - 1, :], y[:, HEAD - 1, :],
                                        ALU.subtract).then_inc(compared, 1)
                dve.wait_ge(compared, 1)
                nc.vector.tensor_reduce(out=worst[:, :], in_=diff[:, :], axis=AX.X, op=ALU.max,
                                        apply_absolute_value=True).then_inc(compared, 1)
                nc.vector.tensor_copy(y[:, 0:HEAD, :], yh[:, :, :]).then_inc(compared, 1)
                dve.wait_ge(worst_turned, 1)
                nc.vector.reduce_max(worst1[:, :], pf[0:1, 0:128], AX.X).then_inc(compared, 1)
                dve.wait_ge(compared, 4)
                nc.vector.tensor_scalar(flag[:, :], worst1[:, :], TOL, None, ALU.is_gt).then_inc(flagged, 1)
                dve.wait_ge(flagged, 1)
                unmet = nc.vector.value_load(flag[0:1, 0:1], min_val=0, max_val=1)
                with dve.If(unmet > 0):
                    with dve.Fori(0, CH) as sweep:
                        starts(more_shifted, sweep + 1, more_started)

        with ExitStack() as octx:
            ring = octx.enter_context(nc.sbuf_tensor("rn_ring", [128, 2, GR, Q], F32))
            ps = octx.enter_context(nc.psum_tensor("rn_pso", [128, 2, GR, 2, D], F32))
            sem = lambda s: c.sem("ro_" + s)
            copied, turned, added = sem("copied"), sem("turned"), sem("added")
            block = octx.enter_context(nc.Block())
            groups = NG // 2
            cs = Q // L * GR

            @block.scalar
            def _(act):
                def group(g, k):
                    need(act, turned, g - 1)
                    nc.scalar.copy(ring[:, k, :, :].rearrange("p b (c j) -> p (b c) j", j=L),
                                   y[:, :, bass.ds(g * cs, cs)].rearrange("p j c -> p c j")).then_inc(copied, 1)
                group(0, 0)
                group(1, 1)
                with act.Fori(1, groups // 2) as i:
                    group(2 * i, 0)
                    group(2 * i + 1, 1)

            @block.tensor
            def _(pe):
                def group(g, k):
                    pe.wait_ge(copied, g + 1)
                    need(pe, added, 2 * (g - 1))
                    for j in range(GR):
                        ins = nc.tensor.transpose(ps[:, k, j, :, :].rearrange("p a d -> p (a d)"),
                                                  ring[:, k, j, :], c.ident[:, :])
                    ins.then_inc(turned, 1)
                group(0, 0)
                group(1, 1)
                with pe.Fori(1, groups // 2) as i:
                    group(2 * i, 0)
                    group(2 * i + 1, 1)

            @block.vector
            def _(dve):
                with dve.Fori(0, groups // 2) as i:
                    for k in range(2):
                        g = 2 * i + k
                        dve.wait_ge(turned, g + 1)
                        for half in range(2):
                            rows = c.x[:, bass.ds(g * GR + half * (S // 2), GR), :]
                            nc.vector.tensor_tensor(rows, rows, ps[:, k, :, half, :], ALU.add).then_inc(added, 1)
                dve.wait_ge(added, 2 * groups)


INNER, STATES, RANK, TAPS = 128, 16, 4, 4
TC = 1024
HALF = TC // 2
RING = 4
COPY_RING, DECAY_RING = 8, 4
B_AHEAD, COPY_AHEAD, DECAY_AHEAD = 7, 5, 3
TAKE_FIRST = 23
NC = T // TC
PAD = 4
BCW = 2 * STATES


def state_space_stage(nc, c, W, y_scratch):
    with ExitStack() as ctx:
        def sb(name, shape, dt=F32):
            return ctx.enter_context(nc.sbuf_tensor(name, shape, dt))
        ns = sb("ss_n", [128, T + 2 * PAD])
        k = dict(
            taps=sb("ss_taps", [128, 2, 2, INNER]),
            z=sb("ss_wz", [D, INNER]), bc=sb("ss_wbc", [INNER, 4 * BCW]), dt=sb("ss_wdt", [INNER, INNER]),
            out=sb("ss_wout", [INNER, D]), cb=sb("ss_cb", [INNER, 1]), db=sb("ss_db", [INNER, 1]),
            dd=sb("ss_D", [INNER, 1]), A=sb("ss_A", [INNER, STATES]),
            sel=sb("ss_sel", [128, BCW], BF16))

        with ExitStack() as wctx:
            def wsb(name, shape, dt=F32):
                return wctx.enter_context(nc.sbuf_tensor(name, shape, dt))
            inx, inz = wsb("sw_inx", [INNER, D]), wsb("sw_inz", [INNER, D])
            cw, xw, dtw = wsb("sw_cw", [INNER, TAPS]), wsb("sw_xw", [RANK + BCW, INNER]), wsb("sw_dtw", [RANK, INNER])
            al, ow = wsb("sw_al", [INNER, STATES]), wsb("sw_ow", [D, INNER])
            tp = wsb("sw_tp", [INNER, 2, 2, 2, D])
            ps = wctx.enter_context(nc.psum_tensor("sw_ps", [128, 4, 512], F32))
            sem = lambda s: c.sem("sw_" + s)
            loaded, cleared, scaled, turned, copied, exped = (sem(s) for s in ("loaded", "cleared", "scaled",
                                                                              "turned", "copied", "exped"))
            block = wctx.enter_context(nc.Block())

            @block.sync
            def _(sp):
                n = 0
                with nc.allow_non_contiguous_dma(reason="512 weights"):
                    for dst, src in ((inx[:, :], W["in_w"][0:INNER, :]), (inz[:, :], W["in_w"][INNER:2 * INNER, :]),
                                     (cw[:, :], W["conv_w"]), (k["cb"][:, :], col_of(W["conv_b"])),
                                     (xw[:, :], W["x_w"]), (dtw[:, :], W["dt_w"].rearrange("d r -> r d")),
                                     (k["db"][:, :], col_of(W["dt_b"])), (al[:, :], W["A_log"]),
                                     (k["dd"][:, :], col_of(W["D"])), (ow[:, :], W["out_w"])):
                        sp.dma_start(dst, src).then_inc(loaded, 16)
                        n += 16
                assert n == 160
                sp.wait_ge(loaded, n)

            @block.gpsimd
            def _(pool):
                nc.gpsimd.memset(k["sel"][:, :], 0.0).then_inc(cleared, 1)
                nc.gpsimd.memset(ns[:, 0:PAD + 1], 0.0).then_inc(cleared, 1)
                nc.gpsimd.memset(ns[:, T + PAD:T + 2 * PAD], 0.0).then_inc(cleared, 1)
                pool.wait_ge(cleared, 3)
                for part, at in enumerate((0, 64, 96)):
                    nc.gpsimd.affine_select(out=k["sel"][:, :], in_=k["sel"][:, :], compare_op=ALU.not_equal,
                                            fill=1.0, base=-at, pattern=[[-1, BCW]],
                                            channel_multiplier=1).then_inc(cleared, 1)
                    pool.wait_ge(cleared, 4 + part)

            @block.scalar
            def _(act):
                act.wait_ge(loaded, 160)
                nc.scalar.activation(al[:, :], al[:, :], ACT.Exp).then_inc(exped, 1)

            @block.vector
            def _(dve):
                dve.wait_ge(loaded, 160)
                order = (((3, 2), (1, 0)), ((2, 3), (0, 1)))
                for way in range(2):
                    for pair in range(2):
                        for half in range(2):
                            tap = order[way][pair][half]
                            nc.vector.tensor_scalar(tp[:, way, pair, half, :], inx[:, :], cw[:, tap:tap + 1], None,
                                                    ALU.mult).then_inc(scaled, 1)
                dve.wait_ge(exped, 1)
                nc.vector.tensor_scalar(k["A"][:, :], al[:, :], -1.0, None, ALU.mult).then_inc(copied, 1)
                dve.wait_ge(turned, 1)
                for way in range(2):
                    for pair in range(2):
                        nc.vector.tensor_copy(k["taps"][:, way, pair, :],
                                              ps[:, 0, (2 * way + pair) * 128:(2 * way + pair + 1) * 128]).then_inc(copied, 1)
                nc.vector.tensor_copy(k["z"][:, :], ps[0:D, 1, 0:128]).then_inc(copied, 1)
                nc.vector.tensor_copy(k["out"][:, :], ps[:, 1, 128:128 + D]).then_inc(copied, 1)
                for part in range(4):
                    nc.vector.tensor_copy(k["bc"][:, part * BCW:(part + 1) * BCW],
                                          ps[:, 1, 256 + RANK:256 + RANK + BCW]).then_inc(copied, 1)
                nc.vector.tensor_copy(k["dt"][:, :], ps[:, 2, 0:128]).then_inc(copied, 1)
                dve.wait_ge(copied, 12)

            @block.tensor
            def _(pe):
                pe.wait_ge(scaled, 8)
                for way in range(2):
                    for pair in range(2):
                        nc.tensor.transpose(ps[:, 0, (2 * way + pair) * 128:(2 * way + pair + 1) * 128],
                                            tp[:, way, pair, :, :].rearrange("p a d -> p (a d)"), c.ident[:, :])
                nc.tensor.transpose(ps[0:D, 1, 0:128], inz[:, :], c.ident[:, :])
                nc.tensor.transpose(ps[:, 1, 128:128 + D], ow[:, :], c.ident[0:D, 0:D])
                nc.tensor.transpose(ps[:, 1, 256:256 + RANK + BCW], xw[:, :], c.ident[0:RANK + BCW, 0:RANK + BCW])
                nc.tensor.matmul(ps[:, 2, 0:128], lhsT=xw[0:RANK, :], rhs=dtw[:, :], start=True,
                                 stop=True).then_inc(turned, 1)

        def evacuate(g, ps):
            nc.scalar.copy(ns[0:D, bass.ds(g * GT + PAD, GT)], ps[0:D, :])
            return nc.scalar.copy(ns[D:2 * D, bass.ds(g * GT + PAD + 1, GT)], ps[D:2 * D, :])
        norm_stage(nc, c, "ss_n", 1.0, 1e-6, evacuate, twice=True)

        for way in range(2):
            scan_direction(nc, c, ns, k, way, y_scratch)


def scan_direction(nc, c, ns, k, way, y_scratch):
    back = way == 1
    N = "sb_" if back else "sf_"
    U = 2 * STATES
    with ExitStack() as ctx:
        def sb(name, shape, dt=F32):
            return ctx.enter_context(nc.sbuf_tensor(N + name, shape, dt))

        def sem(name):
            return c.sem(N + name)
        xc, dt, dtx = sb("xc", [128, 2, TC]), sb("dt", [128, 2, TC]), sb("dtx", [128, 2, TC])
        bcs = sb("bcs", [128, 2, TC], BF16)
        dbx, h, hc = (sb(s, [128, RING, HALF]) for s in ("dbx", "h", "hc"))
        dA, bb = sb("dA", [128, DECAY_RING, HALF]), sb("bb", [128, COPY_RING, HALF])
        ta, tb, tc = (sb(s, [128, TC]) for s in ("ta", "tb", "tc"))
        rest = ta
        state = sb("state", [128, STATES])
        yo = sb("yo", [128, TC])
        if back:
            zs = sb("zs", [128, TC])
            yf = tb
        bank = lambda name: ctx.enter_context(nc.psum_tensor(N + name, [128, TC], F32))
        p_b, p_c, p_y, p_p = bank("pb"), bank("pc"), bank("py"), bank("pp")
        b_made, b_taken, c_made, exped, injected, scanned, kept, read, summed = (
            sem(s) for s in ("b_made", "b_taken", "c_made", "exped", "injected", "scanned", "kept", "read", "summed"))
        (conv, conv_taken, z_made, z_copied, z_taken, dt_made, relu_made, dt_taken, e_made, log_made, w_made, corr,
         corr2, dt_done, dtx_done, bc_made, bc_hi, bc_rest, bc_mid, bc_low, y_taken, y_joined, y_gated, projected,
         x_done, y_stored, y_loaded, zeroed) = (
            sem(s) for s in ("conv", "conv_t", "z", "z_c", "z_t", "dt", "relu", "dt_t", "e", "log", "w", "corr", "corr2",
                             "dt_d", "dtx", "bc", "bc_hi", "bc_rest", "bc_mid", "bc_low", "y_t", "y_j", "y_g",
                             "proj", "x_d", "y_st", "y_ld", "zero"))
        block = ctx.enter_context(nc.Block())
        halves = [slice(0, HALF), slice(HALF, TC)]

        def cols(s):
            return halves[(s // STATES) ^ way]

        def ahead(n, par, s, steps):
            return (n, par, s + steps) if s + steps < U else (n + 1, 1 - par, s + steps - U)

        def base(n):
            return n * -TC + (NC - 1) * TC if back else n * TC

        def run(eng, unit, prepare=(), tail=(), own=()):
            def chunk(n, par, first=False, last=False):
                for s in range(U):
                    unit(n, par, s, first, last)
                    for at, step in prepare:
                        if at == s and not last:
                            step(n + 1, 1 - par)
                    for at, step in tail:
                        if at == s and not first:
                            step(n - 1, 1 - par, last)
                    for at, step in own:
                        if at == s:
                            step(n, last)
            for _, step in prepare:
                step(0, 0)
            chunk(0, 0, first=True)
            chunk(1, 1)
            with eng.Fori(1, NC // 2 - 1) as i:
                chunk(2 * i, 0)
                chunk(2 * i + 1, 1)
            chunk(NC - 2, 0)
            chunk(NC - 1, 1, last=True)

        @block.tensor
        def _(pe):
            def gate_in(hf):
                def step(m, last):
                    need(pe, x_done, m)
                    pe.wait_ge(bc_rest, NC if last else m + 2)
                    ins = nc.tensor.matmul(p_p[:, hf], lhsT=k["z"][:, :],
                                           rhs=ns[0:D, bass.ds(base(m) + PAD + hf.start, HALF)], start=True, stop=True)
                    if hf.start:
                        ins.then_inc(z_made, 1)
                return step

            def convolve(hf):
                def step(m, par):
                    need(pe, bc_rest, m)
                    if back:
                        need(pe, z_copied, m - 1)
                    for pair, off in enumerate((1, 3) if back else (0, -2)):
                        ins = nc.tensor.matmul(p_p[:, hf], lhsT=k["taps"][:, way, pair, :],
                                               rhs=ns[:, bass.ds(base(m) + PAD + off + hf.start, HALF)],
                                               start=(pair == 0), stop=(pair == 1))
                    if hf.start:
                        ins.then_inc(conv, 1)
                return step

            def step_size(hf):
                def step(m, par):
                    pe.wait_ge(conv_taken, m + 1)
                    ins = nc.tensor.matmul(p_p[:, hf], lhsT=k["dt"][:, :], rhs=xc[:, par, hf], start=True, stop=True)
                    if hf.start:
                        ins.then_inc(dt_made, 1)
                return step

            def in_out(hf):
                def step(m, par):
                    pe.wait_ge(dt_taken, m + 1)
                    ins = nc.tensor.matmul(p_p[:, hf], lhsT=k["bc"][:, :], rhs=xc[:, par, hf], start=True, stop=True)
                    if hf.start:
                        ins.then_inc(bc_made, 1)
                return step

            def spread(bank, row, s, par, b):
                return nc.tensor.matmul(bank[:, halves[b]], lhsT=k["sel"][:, row:row + 1].to_broadcast([128, 128]), rhs=bcs[:, par, cols(s)],
                                        start=True, stop=True)

            def spread_b(u, n, par, s):
                if s == 0:
                    pe.wait_ge(bc_low, n + 1)
                need(pe, b_taken, u - 1)
                spread(p_b, s % STATES, s, par, s % 2).then_inc(b_made, 1)

            def spread_c(u, n, par, s):
                need(pe, read, u - 1)
                spread(p_c, STATES + s % STATES, s, par, s % 2).then_inc(c_made, 1)

            def total(u, s, n):
                pe.wait_ge(read, u + 1)
                if s % STATES == 0:
                    need(pe, y_taken, 2 * n - 1 + s // STATES)
                nc.tensor.matmul(p_y[:, cols(s)], lhsT=c.ident[:, :], rhs=hc[:, s % RING, :],
                                 start=(s % STATES == 0), stop=(s % STATES == STATES - 1)).then_inc(summed, 1)

            def project(m, par, last):
                pe.wait_ge(y_gated, m + 1)
                pe.wait_ge(bc_rest, NC if last else m + 3)
                need(pe, x_done, m)
                for j in range(TC // Q):
                    ins = nc.tensor.matmul(p_p[:, j * D:(j + 1) * D], lhsT=yo[:, j * Q:(j + 1) * Q],
                                           rhs=k["out"][:, :], start=True, stop=True)
                ins.then_inc(projected, 1)

            def unit(n, par, s, first, last):
                u = n * U + s
                if first and s == 0:
                    for j in range(B_AHEAD):
                        spread_b(j, 0, par, j)
                    spread_c(0, 0, par, 0)
                if not (last and s >= U - B_AHEAD):
                    spread_b(u + B_AHEAD, *ahead(n, par, s, B_AHEAD))
                if not (first and s < 2):
                    total(u - 2, (s - 2) % U, n if s >= 2 else n - 1)
                if not (last and s == U - 1):
                    spread_c(u + 1, *ahead(n, par, s, 1))

            a, b = halves
            prepare = [(0, convolve(a)), (2, convolve(b)), (7, step_size(a)), (8, step_size(b)),
                       (14, in_out(a)), (15, in_out(b))]
            if back:
                run(pe, unit, prepare, [(20, project)], [(24, gate_in(a)), (25, gate_in(b))])
            else:
                run(pe, unit, prepare)
            total(NC * U - 2, U - 2, NC - 1)
            total(NC * U - 1, U - 1, NC - 1)
            if back:
                project(NC - 1, 1, True)

        @block.scalar
        def _(act):
            def take_z(m, last):
                act.wait_ge(z_made, m + 1)
                need(act, y_gated, m)
                nc.scalar.copy(zs[:, :], p_p[:, :]).then_inc(z_copied, 1)

            def silu_x(m, par):
                act.wait_ge(conv, m + 1)
                need(act, y_taken, 2 * m - 2)
                need(act, dtx_done, 2 * m - 2)
                nc.scalar.activation(xc[:, par, :], p_p[:, :], ACT.Silu, bias=k["cb"][:, :]).then_inc(conv_taken, 1)

            def silu_z(m, par, last):
                act.wait_ge(z_copied, m + 1)
                nc.scalar.activation(zs[:, :], zs[:, :], ACT.Silu).then_inc(z_taken, 1)

            def exp_log_tables(*_):
                nc.scalar.preload_act_table_set("natural_log_exp_and_others")

            def softplus_relu(m, par):
                act.wait_ge(dt_made, m + 1)
                need(act, exped, U * (m - 1))
                nc.scalar.activation(dt[:, par, :], p_p[:, :], ACT.Relu, bias=k["db"][:, :]).then_inc(relu_made, 1)

            def softplus_abs(m, par):
                need(act, bc_low, m)
                need(act, bc_mid, m)
                nc.scalar.activation(ta[:, :], p_p[:, :], ACT.Abs, bias=k["db"][:, :]).then_inc(dt_taken, 1)

            def softplus_exp(m, par):
                act.wait_ge(dt_taken, m + 1)
                nc.scalar.activation(ta[:, :], ta[:, :], ACT.Exp, scale=-1.0).then_inc(e_made, 1)

            def softplus_log(m, par):
                act.wait_ge(e_made, m + 1)
                need(act, corr2, 2 * m)
                if back:
                    need(act, y_joined, m - 1)
                nc.scalar.activation(tb[:, :], ta[:, :], ACT.Ln, bias=c.one[:, :]).then_inc(log_made, 1)

            def bc_high(m, par):
                act.wait_ge(bc_made, m + 1)
                need(act, c_made, U * (m - 1))
                nc.scalar.copy(bcs[:, par, :], p_p[:, :]).then_inc(bc_hi, 1)

            def bc_middle(m, par):
                act.wait_ge(bc_rest, m + 1)
                nc.scalar.copy(bcs[64:128, par, :], rest[64:128, :]).then_inc(bc_mid, 1)

            def copy_b(u, s):
                act.wait_ge(b_made, u + 1)
                need(act, injected, u + 1 - COPY_RING)
                nc.scalar.copy(bb[:, s % COPY_RING, :], p_b[:, halves[s % 2]]).then_inc(b_taken, 1)

            def decay(u, n, par, s):
                if s == 0:
                    act.wait_ge(dt_done, n + 1)
                need(act, scanned, u + 1 - DECAY_RING)
                q = s % STATES
                nc.scalar.activation(dA[:, s % DECAY_RING, :], dt[:, par, cols(s)], ACT.Exp,
                                     scale=k["A"][:, q:q + 1]).then_inc(exped, 1)

            def keep(u, s):
                act.wait_ge(scanned, u + 1)
                q, e = s % STATES, 0 if back else HALF - 1
                nc.scalar.copy(state[:, q:q + 1], h[:, s % RING, e:e + 1]).then_inc(kept, 1)

            def unit(n, par, s, first, last):
                u = n * U + s
                if first and s == 0:
                    for j in range(COPY_AHEAD):
                        copy_b(j, j)
                    for j in range(DECAY_AHEAD):
                        decay(j, 0, par, j)
                if not (last and s >= U - COPY_AHEAD):
                    copy_b(u + COPY_AHEAD, s + COPY_AHEAD)
                if not (last and s >= U - DECAY_AHEAD):
                    decay(u + DECAY_AHEAD, *ahead(n, par, s, DECAY_AHEAD))
                if not (first and s < 2):
                    keep(u - 2, s - 2)

            act.wait_ge(zeroed, 1)
            prepare = [(4, silu_x), (11, softplus_relu), (12, softplus_abs), (13, softplus_exp),
                       (14, softplus_log), (17, bc_high), (19, bc_middle)]
            exp_log_tables()
            if back:
                run(act, unit, prepare, [(4, silu_z)], [(4, exp_log_tables), (27, take_z)])
                silu_z(NC - 1, 1, True)
            else:
                run(act, unit, prepare[:1] + [(4, exp_log_tables)] + prepare[1:])

        @block.gpsimd
        def _(pool):
            def correct(hf):
                def step(m, par):
                    pool.wait_ge(w_made, m + 1)
                    nc.gpsimd.tensor_tensor(tc[:, hf], ta[:, hf], tc[:, hf], ALU.subtract).then_inc(corr, 1)
                return step

            def correct2(hf):
                def step(m, par):
                    pool.wait_ge(corr, 2 * m + 2)
                    pool.wait_ge(log_made, m + 1)
                    nc.gpsimd.tensor_tensor(tc[:, hf], tc[:, hf], tb[:, hf], ALU.add).then_inc(corr2, 1)
                return step

            def dt_x(hf):
                def step(m, par):
                    pool.wait_ge(dt_done, m + 1)
                    need(pool, injected, U * (m - 1))
                    nc.gpsimd.tensor_tensor(dtx[:, par, hf], dt[:, par, hf], xc[:, par, hf], ALU.mult).then_inc(dtx_done, 1)
                return step

            def join(m, par, last):
                pool.wait_ge(y_taken, 2 * m + 2)
                pool.wait_ge(y_loaded, 16 * (m + 1))
                nc.gpsimd.tensor_tensor(yo[:, :], yo[:, :], yf[:, :], ALU.add).then_inc(y_joined, 1)

            def unit(n, par, s, first, last):
                u, b = n * U + s, s % RING
                if s == 0:
                    pool.wait_ge(dtx_done, 2 * n + 2)
                pool.wait_ge(b_taken, u + 1)
                need(pool, scanned, u + 1 - RING)
                nc.gpsimd.tensor_tensor(dbx[:, b, :], dtx[:, par, cols(s)], bb[:, s % COPY_RING, :], ALU.mult).then_inc(injected, 1)

            nc.gpsimd.memset(state[:, :], 0.0).then_inc(zeroed, 1)
            run(pool, unit, [(16, correct(halves[0])), (17, correct(halves[1])), (19, correct2(halves[0])),
                             (20, correct2(halves[1])), (26, dt_x(halves[0])), (27, dt_x(halves[1]))],
                [(5, join)] if back else [])
            if back:
                join(NC - 1, 1, True)

        @block.vector
        def _(dve):
            def one_plus(m, par):
                dve.wait_ge(e_made, m + 1)
                need(dve, dt_done, m)
                nc.vector.tensor_scalar(tc[:, :], ta[:, :], 1.0, 1.0, ALU.add, ALU.subtract).then_inc(w_made, 1)

            def step_sum(m, par):
                dve.wait_ge(corr2, 2 * m + 2)
                dve.wait_ge(relu_made, m + 1)
                nc.vector.tensor_tensor(dt[:, par, :], dt[:, par, :], tc[:, :], ALU.add).then_inc(dt_done, 1)

            def bc_remainder(m, par):
                dve.wait_ge(bc_hi, m + 1)
                dve.wait_ge(corr, 2 * m + 2)
                dve.wait_ge(log_made, m + 1)
                nc.vector.tensor_tensor(rest[:, :], p_p[:, :], bcs[:, par, :], ALU.subtract).then_inc(bc_rest, 1)

            def bc_lowest(m, par):
                dve.wait_ge(bc_mid, m + 1)
                dve.wait_ge(bc_rest, m + 1)
                nc.vector.tensor_tensor(bcs[96:128, par, :], rest[96:128, :], bcs[96:128, par, :],
                                        ALU.subtract).then_inc(bc_low, 1)

            def take_y(m, par, half):
                dve.wait_ge(summed, U * m + (half + 1) * STATES)
                if half == 0 and back:
                    need(dve, projected, m)
                elif half == 0:
                    need(dve, y_stored, 16 * m)
                at = halves[half ^ way]
                nc.vector.scalar_tensor_tensor(out=yo[:, at], in0=xc[:, par, at], scalar=k["dd"][:, :], in1=p_y[:, at],
                                               op0=ALU.mult, op1=ALU.add).then_inc(y_taken, 1)

            def take_second(m, par, last):
                take_y(m, par, 1)

            def gate(m, par, last):
                dve.wait_ge(y_joined, m + 1)
                dve.wait_ge(z_taken, m + 1)
                nc.vector.tensor_tensor(yo[:, :], yo[:, :], zs[:, :], ALU.mult).then_inc(y_gated, 1)

            def add_x(m, par, last):
                dve.wait_ge(projected, m + 1)
                rows = TC // Q
                xr = c.x[:, bass.ds(m * -rows + (NC - 1) * rows, rows), :]
                nc.vector.tensor_tensor(xr, xr, p_p[:, 0:rows * D].rearrange("p (r d) -> p r d", d=D),
                                        ALU.add).then_inc(x_done, 1)

            def read_c(u, s):
                b = s % RING
                dve.wait_ge(scanned, u + 1)
                dve.wait_ge(c_made, u + 1)
                need(dve, summed, u + 1 - RING)
                nc.vector.tensor_tensor(hc[:, b, :], h[:, b, :], p_c[:, halves[s % 2]], ALU.mult).then_inc(read, 1)

            def unit(n, par, s, first, last):
                u, b, q = n * U + s, s % RING, s % STATES
                dve.wait_ge(exped, u + 1)
                dve.wait_ge(injected, u + 1)
                need(dve, kept, u + 1 - RING)
                need(dve, read, u + 1 - RING)
                flow = lambda t, slot=b: t[:, slot, ::-1] if back else t[:, slot, :]
                nc.vector.tensor_tensor_scan(out=flow(h), data0=flow(dA, s % DECAY_RING),
                                             data1=flow(dbx), initial=state[:, q:q + 1],
                                             op0=ALU.mult, op1=ALU.add).then_inc(scanned, 1)
                if not (first and s == 0):
                    read_c(u - 1, s - 1 if s else U - 1)
                if s == TAKE_FIRST:
                    take_y(n, par, 0)

            dve.wait_ge(zeroed, 1)
            run(dve, unit, [(15, one_plus), (18, bc_remainder), (20, bc_lowest), (21, step_sum)],
                [(3, take_second), (8, gate), (22, add_x)] if back else [(3, take_second)])
            read_c(NC * U - 1, U - 1)
            take_y(NC - 1, 1, 1)
            if back:
                gate(NC - 1, 1, True)
                add_x(NC - 1, 1, True)

        @block.sync
        def _(sp):
            if back:
                def load(n, last=False):
                    sp.wait_ge(corr2, 2 * NC if last else 2 * n + 4)
                    need(sp, y_joined, n)
                    sp.dma_start(yf[:, :], y_scratch[:, bass.ds(base(n), TC)]).then_inc(y_loaded, 16)
                load(0)
                with sp.Fori(1, NC - 1) as n:
                    load(n)
                load(NC - 1, True)
            else:
                with sp.Fori(0, NC) as n:
                    sp.wait_ge(y_taken, 2 * n + 2)
                    sp.dma_start(y_scratch[:, bass.ds(base(n), TC)], yo[:, :]).then_inc(y_stored, 16)
                sp.wait_ge(y_stored, 16 * NC)


EXPERTS = 8


def experts_stage(nc, c, W, out):
    SLOTS = 4
    with ExitStack() as ctx:
        def sb(name, shape, dt=F32):
            return ctx.enter_context(nc.sbuf_tensor(name, shape, dt))
        xT = sb("ex_xT", [D, T])
        wr = sb("ex_wr", [D + 1, EXPERTS])
        we = sb("ex_we", [128, EXPERTS, D])
        wt = sb("ex_wt", [Q, S, EXPERTS])
        xg = sb("ex_xg", [128, SLOTS, GT])

        def load_weights(sp, loaded):
            sp.dma_start(we[0:D, :, :], W["expert_w"].rearrange("e d c -> d e c")).then_inc(loaded, 16)
            return 16

        def set_ones(done):
            nc.gpsimd.memset(we[D:128, :, :], 0.0).then_inc(done, 1)
            return 1

        rctx = ctx.enter_context(ExitStack())
        routes = rctx.enter_context(nc.psum_tensor("er_ps", [Q, S, EXPERTS], F32))
        routed = c.sem("er_routed")
        ones_set = c.sem("ex_ones")

        def evacuate(g, ps, slot):
            need(nc.scalar, routed, GR * (g - SLOTS + 1))
            nc.scalar.copy(xg[0:D, slot, :], ps[0:D, :])
            return nc.scalar.copy(xT[0:D, bass.ds(g * GT, GT)], ps[0:D, :])

        def route(g, slot):
            for j in range(GR):
                nc.tensor.matmul(routes[:, bass.ds(g * GR + j, 1), :].rearrange("p a e -> p (a e)"),
                                 lhsT=xg[0:D + 1, slot, j * Q:(j + 1) * Q], rhs=wr[:, :],
                                 start=True, stop=True).then_inc(routed, 1)

        def router_there():
            nc.tensor.wait_ge(ones_set, 1)
            nc.tensor.wait_ge(weights_loaded, 32)

        with ExitStack() as wctx:
            weights_loaded = c.sem("ex_router_loaded")
            block = wctx.enter_context(nc.Block())

            @block.sync
            def _(sp):
                sp.dma_start(wr[0:D, :], W["router_w"]).then_inc(weights_loaded, 16)
                sp.dma_start(wr[D:D + 1, :], row_of(W["router_b"])).then_inc(weights_loaded, 16)

            @block.gpsimd
            def _(pool):
                nc.gpsimd.memset(xg[D:D + 1, :, :], 1.0).then_inc(ones_set, 1)
        norm_stage(nc, c, "ex_n", 1.0, 1e-5, evacuate, more_loads=load_weights, more_sets=set_ones, before=router_there,
                   use=route)

        def loads(sp, used, sems):
            def load(g, k):
                need(sp, used, GR * (g - SLOTS + 1))
                sp.dma_start(xg[0:D, k, :], xT[:, bass.ds(g * GT, GT)]).then_inc(sems[k], 16)
            for k in range(SLOTS):
                load(k, k)
            with sp.Fori(1, NG // SLOTS) as i:
                for k in range(SLOTS):
                    load(SLOTS * i + k, k)

        def rsb(name, shape):
            return rctx.enter_context(nc.sbuf_tensor(name, shape, F32))
        p, e, eq = rsb("er_p", [Q, S, EXPERTS]), rsb("er_e", [Q, S, EXPERTS]), rsb("er_eq", [Q, S, EXPERTS])
        top = rsb("er_top", [Q, 2, S])
        key, tot = rsb("er_key", [Q, S]), rsb("er_tot", [Q, S])
        rank = rsb("er_rank", [Q, EXPERTS])
        ps = routes
        sem = lambda n: c.sem("er_" + n)
        ranked, steps, shifted, exped, biased = (sem(n) for n in ("ranked", "steps", "shifted", "exped", "biased"))
        block = rctx.enter_context(nc.Block())
        wide = lambda t: t.rearrange("p (s a) -> p s a", a=1).to_broadcast([Q, S, EXPERTS])

        @block.sync
        def _(sp):
            sp.dma_start(we[D:D + 1, :, :], W["expert_b"].rearrange("(a e) c -> a e c", a=1)).then_inc(biased, 16)
            sp.wait_ge(biased, 16)

        @block.gpsimd
        def _(pool):
            for j in range(EXPERTS):
                nc.gpsimd.memset(rank[:, j:j + 1], float(EXPERTS - j)).then_inc(ranked, 1)
            pool.wait_ge(ranked, EXPERTS)
            nc.gpsimd.memset(xg[D:128, :, :], 0.0).then_inc(ranked, 1)
            pool.wait_ge(ranked, EXPERTS + 1)
            nc.gpsimd.memset(xg[D:D + 1, :, :], 1.0).then_inc(ranked, 1)
            pool.wait_ge(ranked, EXPERTS + 2)

        @block.scalar
        def _(act):
            act.wait_ge(shifted, 1)
            nc.scalar.activation(e[:, :, :], p[:, :, :], ACT.Exp).then_inc(exped, 1)

        @block.vector
        def _(dve):
            chain = Chain(dve, steps)
            dve.wait_ge(routed, S)
            chain(nc.vector.reduce_max(key[:, :], ps[:, :, :], AX.X))
            nc.vector.tensor_tensor(p[:, :, :], ps[:, :, :], wide(key[:, :]), ALU.subtract).then_inc(shifted, 1)
            dve.wait_ge(exped, 1)
            chain(nc.vector.reduce_sum(tot[:, :], e[:, :, :], AX.X))
            chain(nc.vector.reciprocal(tot[:, :], tot[:, :]))
            chain(nc.vector.tensor_tensor(p[:, :, :], e[:, :, :], wide(tot[:, :]), ALU.mult))
            dve.wait_ge(ranked, EXPERTS)
            ranks = rank[:, :].rearrange("p (a e) -> p a e", a=1).to_broadcast([Q, S, EXPERTS])
            for choice, pick in ((0, e), (1, wt)):
                chain(nc.vector.reduce_max(top[:, choice, :], p[:, :, :], AX.X))
                chain(nc.vector.tensor_tensor(eq[:, :, :], p[:, :, :], wide(top[:, choice, :]), ALU.is_equal))
                chain(nc.vector.tensor_tensor(eq[:, :, :], eq[:, :, :], ranks, ALU.mult))
                chain(nc.vector.reduce_max(key[:, :], eq[:, :, :], AX.X))
                chain(nc.vector.tensor_tensor(pick[:, :, :], eq[:, :, :], wide(key[:, :]), ALU.is_equal))
                if choice == 0:
                    chain(nc.vector.scalar_tensor_tensor(out=p[:, :, :], in0=e[:, :, :], scalar=-2.0,
                                                         in1=p[:, :, :], op0=ALU.mult, op1=ALU.add))
            chain(nc.vector.tensor_tensor(tot[:, :], top[:, 0, :], top[:, 1, :], ALU.add))
            chain(nc.vector.reciprocal(tot[:, :], tot[:, :]))
            for choice, pick in ((0, e), (1, wt)):
                chain(nc.vector.tensor_tensor(top[:, choice, :], top[:, choice, :], tot[:, :], ALU.mult))
                chain(nc.vector.tensor_tensor(pick[:, :, :], pick[:, :, :], wide(top[:, choice, :]), ALU.mult))
            chain(nc.vector.tensor_tensor(wt[:, :, :], wt[:, :, :], e[:, :, :], ALU.add))

        rctx.close()

        with ExitStack() as ectx:
            hw = ectx.enter_context(nc.sbuf_tensor("ee_hw", [Q, GR, 1 + EXPERTS, D], F32))
            ps = ectx.enter_context(nc.psum_tensor("ee_ps", [Q, GR, EXPERTS, D], F32))
            sem = lambda n: c.sem("ee_" + n)
            made, weighed, carried, halved, summed, stored = (
                sem(n) for n in ("made", "weighed", "carried", "halved", "summed", "stored"))
            loaded = [sem("loaded%d" % k) for k in range(SLOTS)]
            block = ectx.enter_context(nc.Block())
            ov = out.rearrange("b s q d -> q (b s) d")

            @block.sync
            def _(sp):
                loads(sp, made, loaded)

            @block.tensor
            def _(pe):
                def group(g, k, i):
                    pe.wait_ge(loaded[k], 16 * (i + 1))
                    for j in range(GR):
                        need(pe, weighed, g * GR + j - GR + 1)
                        nc.tensor.matmul(ps[:, j, :, :], lhsT=xg[:, k, j * Q:(j + 1) * Q], rhs=we[:, :, :],
                                         start=True, stop=True).then_inc(made, 1)
                for k in range(SLOTS):
                    group(k, k, 0)
                with pe.Fori(1, NG // SLOTS) as i:
                    for k in range(SLOTS):
                        group(SLOTS * i + k, k, i)

            @block.scalar
            def _(act):
                def carry(g):
                    for j in range(GR):
                        r = g * GR + j
                        need(act, summed, r - GR + 1)
                        nc.scalar.copy(hw[:, j, 0:1, :], c.x[:, bass.ds(r, 1), :]).then_inc(carried, 1)

                def store(g):
                    act.wait_ge(summed, GR * (g + 1))
                    nc.scalar.dma_start(ov[:, bass.ds(g * GR, GR), :], c.x[:, bass.ds(g * GR, GR), :]).then_inc(stored, 16)
                carry(0)
                with act.Fori(1, NG) as g:
                    carry(g)
                    store(g - 1)
                store(NG - 1)
                act.wait_ge(stored, 16 * NG)

            @block.vector
            def _(dve):
                def weigh(r, j):
                    dve.wait_ge(made, r + 1)
                    need(dve, summed, r - GR + 1)
                    nc.vector.tensor_tensor(
                        hw[:, j, 1:1 + EXPERTS, :], ps[:, j, :, :],
                        wt[:, bass.ds(r, 1), :].rearrange("p a (e b) -> p (a e) b", b=1).to_broadcast([Q, EXPERTS, D]),
                        ALU.mult).then_inc(weighed, 1)

                def add(r, j):
                    dve.wait_ge(halved, r + 1)
                    dve.wait_ge(carried, r + 1)
                    nc.vector.tensor_reduce(out=c.x[:, bass.ds(r, 1), :].rearrange("p a d -> p (a d)"),
                                            in_=hw[:, j, 0:1 + EXPERTS // 2, :].rearrange("p e d -> p d e"), axis=AX.X,
                                            op=ALU.add).then_inc(summed, 1)
                BEHIND = 2
                for j in range(GR):
                    weigh(j, j)
                    if j >= BEHIND:
                        add(j - BEHIND, j - BEHIND)
                with dve.Fori(1, NG) as g:
                    for j in range(GR):
                        weigh(g * GR + j, j)
                        add(g * GR + j - BEHIND, (j - BEHIND) % GR)
                for r in range(S - BEHIND, S):
                    add(r, r % GR)

            @block.gpsimd
            def _(pool):
                with pool.Fori(0, NG) as g:
                    for j in range(GR):
                        pool.wait_ge(weighed, g * GR + j + 1)
                        nc.gpsimd.tensor_tensor(hw[:, j, 1:5, :], hw[:, j, 1:5, :], hw[:, j, 5:9, :],
                                                ALU.add).then_inc(halved, 1)


def build(nc, I, out):
    with ExitStack() as ctx:
        c = Core(nc, ctx)
        identity_stage(nc, c)
        A = {n: I["L0_conv_" + n] for n in ("mask", "gamma", "beta", "Wq", "Wk", "Wv", "Wb", "Wu", "bu", "Wo", "bo")}
        attention_stage(nc, c, A, I["x"].rearrange("b s q d -> q (b s) d"))
        c.clear_semaphores()
        recurrence_stage(nc, c, *(I["L0_ffn_" + n] for n in ("W", "V", "gamma", "beta")))
        c.clear_semaphores()
        y = nc.dram_tensor("y_scratch", (INNER, T), F32, kind="Internal").ap()
        W = {n: I["L1_conv_" + n] for n in ("in_w", "conv_w", "conv_b", "x_w", "dt_w", "dt_b", "A_log", "D", "out_w")}
        state_space_stage(nc, c, W, y)
        c.clear_semaphores()
        experts_stage(nc, c, {n: I["L1_ffn_" + n] for n in ("router_w", "router_b", "expert_w", "expert_b")}, out)


_INS = ['x', 'L0_conv_mask', 'L0_conv_gamma', 'L0_conv_beta', 'L0_conv_Wq', 'L0_conv_Wk', 'L0_conv_Wv', 'L0_conv_Wb',
        'L0_conv_Wu', 'L0_conv_bu', 'L0_conv_Wo', 'L0_conv_bo', 'L0_ffn_W', 'L0_ffn_V', 'L0_ffn_gamma',
        'L0_ffn_beta', 'L1_conv_in_w', 'L1_conv_conv_w', 'L1_conv_conv_b', 'L1_conv_x_w', 'L1_conv_dt_w',
        'L1_conv_dt_b', 'L1_conv_A_log', 'L1_conv_D', 'L1_conv_out_w', 'L1_ffn_router_w', 'L1_ffn_router_b',
        'L1_ffn_expert_w', 'L1_ffn_expert_b']
_OUT = ((1, 128, 128, 64), 'float32')


def kernel(**inputs):
    import numpy as _np
    import concourse.bacc as _bacc
    from concourse import mybir as _mybir
    from concourse.bass_utils import run_bass_kernel_spmd as _run

    nc = _bacc.Bacc("TRN2", target_bir_lowering=False, num_devices=1)
    arrays, aps = {}, {}
    for name in _INS:
        a = _np.ascontiguousarray(inputs[name])
        arrays[f"in_{name}_dram"] = a
        aps[name] = nc.dram_tensor(f"in_{name}_dram", a.shape, _mybir.dt.from_np(a.dtype), kind="ExternalInput").ap()
    shape, dtype = _OUT
    out = nc.dram_tensor("out_0_dram", shape, _mybir.dt.from_np(_np.dtype(dtype)), kind="ExternalOutput").ap()
    build(nc, aps, out)
    r = _run(nc, [arrays], core_ids=[0])
    return r.results[0]["out_0_dram"]
```
